# Optimizing a Trainium2 kernel written in Bass

```python
import numpy as np
import jax
import jax.numpy as jnp

def _softmax(x, axis=-1):
    return jax.nn.softmax(x, axis=axis)

def _gelu(x):
    return jax.nn.gelu(x, approximate=True)

def _silu(x):
    return jax.nn.silu(x)

def _sigmoid(x):
    return jax.nn.sigmoid(x)

def _layernorm(x, axis=-1, eps=1e-05):
    m = jnp.mean(x, axis=axis, keepdims=True)
    v = jnp.var(x, axis=axis, keepdims=True)
    return (x - m) / jnp.sqrt(v + eps)

def _scatter_add(tgt, idx, src, axis=0):
    return tgt.at[idx].add(src)

def _segment_sum(src, seg, n):
    return jax.ops.segment_sum(src, seg, n)
kernel_name = 'mk_decoder_preln_d2_seqx_r4_66af73'

def setup_inputs(seed: int=0):
    np.random.seed(seed)
    _w = jnp.asarray

    def _rec_inputs():
        import jax
        import jax.numpy as jnp
        _rk = jax.random.key(seed)
        x = -0.000125 + 0.9999 * jax.random.normal(jax.random.fold_in(_rk, 1), (4, 512, 256), jnp.float32)
        _lenS = 512 - jax.random.randint(jax.random.fold_in(_rk, 7), (4,), 0, max(1, 512 // 4) + 1, jnp.int32)
        _lenS2 = 512 - jax.random.randint(jax.random.fold_in(_rk, 8), (4,), 0, max(1, 512 // 4) + 1, jnp.int32)
        _ctx_1024P = jax.random.normal(jax.random.fold_in(_rk, 11), (4, 16, 256), jnp.float32)
        _ctx_1024c = jax.random.dirichlet(jax.random.fold_in(_rk, 511), 0.3 * jnp.ones((16,), jnp.float32), (4, 512))
        _ctx_1024t = jnp.einsum('bsk,bkd->bsd', _ctx_1024c, _ctx_1024P)
        _ctx_1024t = _ctx_1024t * jax.lax.rsqrt(jnp.mean(jnp.square(_ctx_1024t)) + 1e-12) * 0.953939
        ctx_1024 = -1.78809e-06 + 0.0312453 * (_ctx_1024t + 0.3 * jax.random.normal(jax.random.fold_in(_rk, 611), (4, 512, 256), jnp.float32))
        return (x, ctx_1024)
    x, ctx_1024 = _rec_inputs()

    def _L0_attn_setup():
        import jax, jax.numpy as jnp
        import numpy as np
        import math
        B, T, C = (2, 512, 256)
        NH = 16
        HD = C // NH

        def _rope_factor(T, d, dtype):
            theta = 1.0 / 10000.0 ** (2.0 * jnp.arange(0, d // 2, dtype=jnp.float32) / d)
            seq = jnp.arange(1, T + 1, dtype=jnp.float32)
            ang = jnp.einsum('n,d->nd', seq, theta)
            ang = jnp.concatenate([ang, ang], axis=-1)
            return (jnp.cos(ang) + jnp.sin(ang)).astype(dtype)
        key = jax.random.key(seed)
        ks = jax.random.split(key, 5)
        s = 0.02
        return {'x': jax.random.normal(ks[0], (B, T, C), dtype=jnp.float32), 'W_attn': jax.random.normal(ks[1], (3 * C, C), dtype=jnp.float32) * s, 'b_attn': jax.random.normal(ks[2], (3 * C,), dtype=jnp.float32) * s, 'W_proj': jax.random.normal(ks[3], (C, C), dtype=jnp.float32) * s, 'b_proj': jax.random.normal(ks[4], (C,), dtype=jnp.float32) * s}
    _L0_attn_all = _L0_attn_setup()
    _L0_attn_in = {k: v for k, v in _L0_attn_all.items() if k in ('W_attn', 'b_attn', 'W_proj', 'b_proj')}
    del _L0_attn_all

    def _L0_xattn_setup():
        import jax, jax.numpy as jnp
        import numpy as np
        E, T, H, F = (16, 512, 256, 1024)
        key = jax.random.key(seed)
        kx, k1, k2, k3 = jax.random.split(key, 4)
        s = 1.0 / np.sqrt(H)
        return {'x': jax.random.normal(kx, (E, T, H), dtype=jnp.float32), 'w1': jax.random.normal(k1, (E, F, H), dtype=jnp.float32) * s, 'v1': jax.random.normal(k2, (E, F, H), dtype=jnp.float32) * s, 'w2': jax.random.normal(k3, (E, F, H), dtype=jnp.float32) * s}
    _L0_xattn_all = _L0_xattn_setup()
    _L0_xattn_in = {k: v for k, v in _L0_xattn_all.items() if k in ()}
    del _L0_xattn_all

    def _L0_ffn_setup():
        import jax, jax.numpy as jnp
        import numpy as np
        D, H, E, K, S = (256, 512, 8, 2, 1)
        B, L = (4, 512)
        key = jax.random.key(seed)
        ks = jax.random.split(key, 9)
        std = 0.02
        return {'x': jax.random.normal(ks[0], (B, L, D), dtype=jnp.float32), 'router_w': jax.random.normal(ks[1], (E, D), dtype=jnp.float32) * std, 'experts_bias': jnp.zeros((E,), dtype=jnp.float32), 'w1': jax.random.normal(ks[2], (E, D, H), dtype=jnp.float32) * std, 'w3': jax.random.normal(ks[3], (E, D, H), dtype=jnp.float32) * std, 'w2': jax.random.normal(ks[4], (E, H, D), dtype=jnp.float32) * std, 'sw1': jax.random.normal(ks[5], (S, D, H), dtype=jnp.float32) * std, 'sw3': jax.random.normal(ks[6], (S, D, H), dtype=jnp.float32) * std, 'sw2': jax.random.normal(ks[7], (S, H, D), dtype=jnp.float32) * std}
    _L0_ffn_all = _L0_ffn_setup()
    _L0_ffn_in = {k: v for k, v in _L0_ffn_all.items() if k in ('router_w', 'experts_bias', 'w1', 'w3', 'w2', 'sw1', 'sw3', 'sw2')}
    del _L0_ffn_all

    def _L1_attn_setup():
        import jax, jax.numpy as jnp
        import numpy as np
        import math
        FEATURE_DIM = 256
        NUM_HEADS = 16
        HEAD_SIZE = FEATURE_DIM // NUM_HEADS
        key = jax.random.key(seed)
        ks = jax.random.split(key, 5)
        B, T, C = (4, 512, FEATURE_DIM)
        scale = 1.0 / math.sqrt(C)
        x = jax.random.normal(ks[0], (B, T, C), dtype=jnp.float32)
        W_qkv = jax.random.uniform(ks[1], (3 * C, C), jnp.float32, -scale, scale)
        b_qkv = jax.random.uniform(ks[2], (3 * C,), jnp.float32, -scale, scale)
        W_out = jax.random.uniform(ks[3], (C, C), jnp.float32, -scale, scale)
        b_out = jax.random.uniform(ks[4], (C,), jnp.float32, -scale, scale)
        return {'x': x, 'W_qkv': W_qkv, 'b_qkv': b_qkv, 'W_out': W_out, 'b_out': b_out}
    _L1_attn_all = _L1_attn_setup()
    _L1_attn_in = {k: v for k, v in _L1_attn_all.items() if k in ('W_qkv', 'b_qkv', 'W_out', 'b_out')}
    del _L1_attn_all

    def _L1_xattn_setup():
        import jax, jax.numpy as jnp
        import numpy as np
        import math
        B, T, E, H = (2, 512, 256, 16)
        D = E // H
        key = jax.random.key(seed)
        ks = jax.random.split(key, 8)
        s = 1.0 / math.sqrt(E)
        return {'input': jax.random.normal(ks[0], (B, T, E), jnp.float32), 'encoded_features': jax.random.normal(ks[1], (B, T, E), jnp.float32), 'Wq': jax.random.normal(ks[2], (E, E), jnp.float32) * s, 'bq': jnp.zeros((E,), jnp.float32), 'Wkv': jax.random.normal(ks[3], (E, 2 * E), jnp.float32) * s, 'bkv': jnp.zeros((2 * E,), jnp.float32), 'Wo': jax.random.normal(ks[4], (E, E), jnp.float32) * s, 'bo': jnp.zeros((E,), jnp.float32)}
    _L1_xattn_all = _L1_xattn_setup()
    _L1_xattn_in = {k: v for k, v in _L1_xattn_all.items() if k in ('Wq', 'bq', 'Wkv', 'bkv', 'Wo', 'bo')}
    del _L1_xattn_all

    def _L1_ffn_setup():
        import jax, jax.numpy as jnp
        import numpy as np
        JITTER_EPS = 0.01

        def phi_routing(logits, jitter_eps=JITTER_EPS):
            m, sel = jax.lax.top_k(logits, 2)
            T, E = logits.shape
            m1 = m[:, :1]
            factor1 = jnp.maximum(jnp.abs(logits), m1)
            mask1 = (m1 - logits) / factor1 > 2.0 * jitter_eps
            p1 = jax.nn.softmax(jnp.where(mask1, -jnp.inf, logits), axis=-1)
            mult1 = jnp.take_along_axis(p1, sel[:, :1], axis=-1)
            m2 = m[:, 1:2]
            factor2 = jnp.maximum(jnp.abs(logits), m2)
            mask2 = (m2 - logits) / factor2 > 2.0 * jitter_eps
            drop_top1 = jnp.arange(E)[None, :] == sel[:, :1]
            p2 = jax.nn.softmax(jnp.where(mask2 | drop_top1, -jnp.inf, logits), axis=-1)
            mult2 = jnp.take_along_axis(p2, sel[:, 1:2], axis=-1)
            return (jnp.concatenate([mult1, mult2], axis=-1), sel)
        key = jax.random.key(seed)
        k = jax.random.split(key, 5)
        B, S, H, F, E = (1, 128, 256, 1024, 8)
        return {'hidden_states': jax.random.normal(k[0], (B, S, H), jnp.float32), 'gate_w': jax.random.normal(k[1], (E, H), jnp.float32) * 0.02, 'w1': jax.random.normal(k[2], (E, F, H), jnp.float32) * 0.02, 'w2': jax.random.normal(k[3], (E, H, F), jnp.float32) * 0.02, 'w3': jax.random.normal(k[4], (E, F, H), jnp.float32) * 0.02}
    _L1_ffn_all = _L1_ffn_setup()
    _L1_ffn_in = {k: v for k, v in _L1_ffn_all.items() if k in ('gate_w', 'w1', 'w2', 'w3')}
    del _L1_ffn_all
    return {'x': x, 'ctx_1024': ctx_1024, 'L0_attn_W_attn': _L0_attn_in['W_attn'], 'L0_attn_b_attn': _L0_attn_in['b_attn'], 'L0_attn_W_proj': _L0_attn_in['W_proj'], 'L0_attn_b_proj': _L0_attn_in['b_proj'], 'L0_ffn_router_w': _L0_ffn_in['router_w'], 'L0_ffn_experts_bias': _L0_ffn_in['experts_bias'], 'L0_ffn_w1': _L0_ffn_in['w1'], 'L0_ffn_w3': _L0_ffn_in['w3'], 'L0_ffn_w2': _L0_ffn_in['w2'], 'L0_ffn_sw1': _L0_ffn_in['sw1'], 'L0_ffn_sw3': _L0_ffn_in['sw3'], 'L0_ffn_sw2': _L0_ffn_in['sw2'], 'L1_attn_W_qkv': _L1_attn_in['W_qkv'], 'L1_attn_b_qkv': _L1_attn_in['b_qkv'], 'L1_attn_W_out': _L1_attn_in['W_out'], 'L1_attn_b_out': _L1_attn_in['b_out'], 'L1_xattn_Wq': _L1_xattn_in['Wq'], 'L1_xattn_bq': _L1_xattn_in['bq'], 'L1_xattn_Wkv': _L1_xattn_in['Wkv'], 'L1_xattn_bkv': _L1_xattn_in['bkv'], 'L1_xattn_Wo': _L1_xattn_in['Wo'], 'L1_xattn_bo': _L1_xattn_in['bo'], 'L1_ffn_gate_w': _L1_ffn_in['gate_w'], 'L1_ffn_w1': _L1_ffn_in['w1'], 'L1_ffn_w2': _L1_ffn_in['w2'], 'L1_ffn_w3': _L1_ffn_in['w3']}

def reference(x, ctx_1024, L0_attn_W_attn, L0_attn_b_attn, L0_attn_W_proj, L0_attn_b_proj, L0_ffn_router_w, L0_ffn_experts_bias, L0_ffn_w1, L0_ffn_w3, L0_ffn_w2, L0_ffn_sw1, L0_ffn_sw3, L0_ffn_sw2, L1_attn_W_qkv, L1_attn_b_qkv, L1_attn_W_out, L1_attn_b_out, L1_xattn_Wq, L1_xattn_bq, L1_xattn_Wkv, L1_xattn_bkv, L1_xattn_Wo, L1_xattn_bo, L1_ffn_gate_w, L1_ffn_w1, L1_ffn_w2, L1_ffn_w3):
    import jax
    import jax.numpy as jnp

    def _L0_attn_ref(x, W_attn, b_attn, W_proj, b_proj):
        import jax, jax.numpy as jnp
        import numpy as np
        import math
        B, T, C = (2, 512, 256)
        NH = 16
        HD = C // NH

        def _rope_factor(T, d, dtype):
            theta = 1.0 / 10000.0 ** (2.0 * jnp.arange(0, d // 2, dtype=jnp.float32) / d)
            seq = jnp.arange(1, T + 1, dtype=jnp.float32)
            ang = jnp.einsum('n,d->nd', seq, theta)
            ang = jnp.concatenate([ang, ang], axis=-1)
            return (jnp.cos(ang) + jnp.sin(ang)).astype(dtype)
        Bs, Ts, Cs = x.shape
        qkv = x @ W_attn.T + b_attn
        q, k, v = jnp.split(qkv, 3, axis=-1)

        def to_heads(t):
            return t.reshape(Bs, Ts, NH, HD).transpose(0, 2, 1, 3)
        q, k, v = (to_heads(q), to_heads(k), to_heads(v))
        f = _rope_factor(Ts, HD, x.dtype)
        q = q * f
        k = k * f
        att = jnp.einsum('bhqd,bhkd->bhqk', q, k) * (1.0 / math.sqrt(HD))
        causal = jnp.tril(jnp.ones((Ts, Ts), dtype=bool))
        att = jnp.where(causal, att, jnp.finfo(att.dtype).min)
        att = jax.nn.softmax(att, axis=-1)
        y = jnp.einsum('bhqk,bhkd->bhqd', att, v)
        y = y.transpose(0, 2, 1, 3).reshape(Bs, Ts, Cs)
        y = y @ W_proj.T + b_proj
        return y

    def _L0_xattn_ref(x, w1, v1, w2):
        import jax, jax.numpy as jnp
        import numpy as np
        E, T, H, F = (16, 512, 256, 1024)
        x1 = jnp.einsum('eth,efh->etf', x, w1)
        x2 = jnp.einsum('eth,efh->etf', x, v1)
        h = jax.nn.gelu(x1, approximate=True) * x2
        return jnp.einsum('etf,efh->eth', h, w2)

    def _L0_ffn_ref(x, router_w, experts_bias, w1, w3, w2, sw1, sw3, sw2):
        import jax, jax.numpy as jnp
        import numpy as np
        D, H, E, K, S = (256, 512, 8, 2, 1)
        B, L = (4, 512)
        b, l, d = x.shape
        xf = x.reshape(-1, d)
        sg = jnp.einsum('td,sdh->tsh', xf, sw1)
        su = jnp.einsum('td,sdh->tsh', xf, sw3)
        shared_out = jnp.einsum('tsh,shd->td', jax.nn.silu(sg) * su, sw2)
        logits = xf @ router_w.T + experts_bias
        rw, sel = jax.lax.top_k(logits, K)
        rw = jax.nn.softmax(rw.astype(jnp.float32), axis=-1).astype(x.dtype)
        cw = (jax.nn.one_hot(sel, E, dtype=x.dtype) * rw[..., None]).sum(axis=1)
        g = jnp.einsum('td,edh->teh', xf, w1)
        u = jnp.einsum('td,edh->teh', xf, w3)
        eo = jax.nn.silu(g) * u
        moe_out = jnp.einsum('te,teh,ehd->td', cw, eo, w2)
        return (moe_out + shared_out).reshape(b, l, d)

    def _L1_attn_ref(x, W_qkv, b_qkv, W_out, b_out):
        import jax, jax.numpy as jnp
        import numpy as np
        import math
        FEATURE_DIM = 256
        NUM_HEADS = 16
        HEAD_SIZE = FEATURE_DIM // NUM_HEADS
        B, T, C = x.shape
        H, hs = (NUM_HEADS, HEAD_SIZE)
        qkv = x @ W_qkv.T + b_qkv
        qkv = qkv.reshape(B, T, H, 3 * hs)
        q = qkv[..., :hs]
        k = qkv[..., hs:2 * hs]
        v = qkv[..., 2 * hs:]
        att = jnp.einsum('bthd,bshd->bhts', q, k) / math.sqrt(hs)
        att_prob = jax.nn.softmax(att, axis=-1)
        att_v = jnp.einsum('bhts,bshd->bthd', att_prob, v)
        att_v = att_v.reshape(B, T, C)
        return att_v @ W_out.T + b_out

    def _L1_xattn_ref(input, encoded_features, Wq, bq, Wkv, bkv, Wo, bo):
        import jax, jax.numpy as jnp
        import numpy as np
        import math
        B, T, E, H = (2, 512, 256, 16)
        D = E // H
        b, tq, _ = input.shape
        tk = encoded_features.shape[1]
        q = (input @ Wq + bq).reshape(b, tq, H, D).transpose(0, 2, 1, 3)
        kv = (encoded_features @ Wkv + bkv).reshape(b, tk, 2, H, D).transpose(2, 0, 3, 1, 4)
        k, v = (kv[0], kv[1])
        scores = jnp.einsum('bhqd,bhkd->bhqk', q, k) / math.sqrt(D)
        attn = jax.nn.softmax(scores, axis=2)
        out = jnp.einsum('bhqk,bhkd->bhqd', attn, v)
        out = out.transpose(0, 2, 1, 3).reshape(b, tq, H * D)
        return out @ Wo + bo

    def _L1_ffn_ref(hidden_states, gate_w, w1, w2, w3):
        import jax, jax.numpy as jnp
        import numpy as np
        JITTER_EPS = 0.01

        def phi_routing(logits, jitter_eps=JITTER_EPS):
            m, sel = jax.lax.top_k(logits, 2)
            T, E = logits.shape
            m1 = m[:, :1]
            factor1 = jnp.maximum(jnp.abs(logits), m1)
            mask1 = (m1 - logits) / factor1 > 2.0 * jitter_eps
            p1 = jax.nn.softmax(jnp.where(mask1, -jnp.inf, logits), axis=-1)
            mult1 = jnp.take_along_axis(p1, sel[:, :1], axis=-1)
            m2 = m[:, 1:2]
            factor2 = jnp.maximum(jnp.abs(logits), m2)
            mask2 = (m2 - logits) / factor2 > 2.0 * jitter_eps
            drop_top1 = jnp.arange(E)[None, :] == sel[:, :1]
            p2 = jax.nn.softmax(jnp.where(mask2 | drop_top1, -jnp.inf, logits), axis=-1)
            mult2 = jnp.take_along_axis(p2, sel[:, 1:2], axis=-1)
            return (jnp.concatenate([mult1, mult2], axis=-1), sel)
        B, S, H = hidden_states.shape
        E = w1.shape[0]
        x = hidden_states.reshape(-1, H)
        logits = x @ gate_w.T
        routing_weights, selected = phi_routing(logits)
        T = x.shape[0]
        wte = jnp.zeros((T, E), x.dtype).at[jnp.arange(T)[:, None], selected].add(routing_weights)
        out = jnp.zeros_like(x)
        for e in range(E):
            h = jax.nn.silu(x @ w1[e].T) * (x @ w3[e].T)
            out = out + wte[:, e:e + 1] * (h @ w2[e].T)
        return out.reshape(B, S, H)
    x = x + _L0_attn_ref(_layernorm(x, axis=-1), L0_attn_W_attn, L0_attn_b_attn, L0_attn_W_proj, L0_attn_b_proj)
    x = x + _L0_xattn_ref(_layernorm(x, axis=-1), ctx_1024, ctx_1024, ctx_1024)
    x = x + _L0_ffn_ref(_layernorm(x, axis=-1), L0_ffn_router_w, L0_ffn_experts_bias, L0_ffn_w1, L0_ffn_w3, L0_ffn_w2, L0_ffn_sw1, L0_ffn_sw3, L0_ffn_sw2)
    x = x + _L1_attn_ref(_layernorm(x, axis=-1), L1_attn_W_qkv, L1_attn_b_qkv, L1_attn_W_out, L1_attn_b_out)
    x = x + _L1_xattn_ref(_layernorm(x, axis=-1), ctx_1024, L1_xattn_Wq, L1_xattn_bq, L1_xattn_Wkv, L1_xattn_bkv, L1_xattn_Wo, L1_xattn_bo)
    x = x + _L1_ffn_ref(_layernorm(x, axis=-1), L1_ffn_gate_w, L1_ffn_w1, L1_ffn_w2, L1_ffn_w3)
    return x

_drawn_inputs = setup_inputs


def setup_inputs(seed=0):
    import zlib

    import numpy as np

    out = dict(_drawn_inputs(seed))
    spreads = {'L0_ffn_experts_bias': (0.0, 0.8),
     'L1_xattn_bq': (0.0, 2.0),
     'L1_xattn_bkv': (0.0, 0.1),
     'L1_xattn_bo': (0.0, 0.428)}
    factors = {'L0_attn_W_attn': 5.073,
     'L0_attn_b_attn': 8.0,
     'L0_attn_W_proj': 4.265,
     'L0_attn_b_proj': 3.148,
     'L0_ffn_router_w': 6.596,
     'L0_ffn_w1': 5.667,
     'L0_ffn_w3': 5.606,
     'L0_ffn_w2': 5.589,
     'L0_ffn_sw1': 4.087,
     'L0_ffn_sw3': 4.045,
     'L0_ffn_sw2': 4.064,
     'L1_attn_b_qkv': 12.581,
     'L1_attn_b_out': 8.405,
     'L1_xattn_Wq': 8.0,
     'L1_xattn_Wkv': 6.117,
     'L1_attn_W_qkv': 3.73,
     'L1_ffn_gate_w': 7.299,
     'L1_ffn_w1': 6.376,
     'L1_ffn_w2': 6.307,
     'L1_ffn_w3': 6.334}
    for name, (base, spread) in spreads.items():
        noise = np.random.default_rng([zlib.crc32(name.encode()), seed]).standard_normal(out[name].shape)
        drawn = base * np.exp(spread * noise) if base else spread * noise
        out[name] = jnp.asarray(drawn.astype(out[name].dtype))
    for name, factor in factors.items():
        out[name] = (out[name] * factor).astype(out[name].dtype)
    return out
```

```python
from contextlib import ExitStack

import numpy as np

import concourse.bass as bass
from concourse import mybir

F32 = mybir.dt.float32
F32R = mybir.dt.float32r
BF16 = mybir.dt.bfloat16
ALU = mybir.AluOpType
ACT = mybir.ActivationFunctionType
AX = mybir.AxisListType

P = 128
B, T, D = 4, 512, 256
NT = T // P
CC = D // P
H, HD = 16, 16
GH = 4
NG = H // GH
NPAIR = H // 2
EPS = 1e-5
NEG = -1e30
SCALE = 1.0 / 4.0


class Steps:

    def __init__(self, sem, per):
        self.sem, self.per = sem, per

    def begin(self, eng):
        eng.sem_inc(self.sem, self.per)

    def count(self, b, step):
        return (b + 1) * self.per + step + 1

    def wait(self, eng, b, step):
        eng.wait_ge(self.sem, self.count(b, step))


def wait_all(eng, *waits):
    values = [s.count(b, step) for s, b, step in waits]
    for v in values:
        eng.compute_val(v)
    for (s, _, _), v in zip(waits, values):
        eng.wait_ge(s.sem, v)


def batch_body(eng, nb, body):
    with eng.Fori(0, nb - 1) as b:
        body(b, b + 1)
    body(nb - 1, None)


def attention_schedule(b, nxt, cross):
    for g in range(NG):
        target = (b, g + 2) if g < 2 else (nxt, g - 2)
        before = (b, g + 1) if 1 <= g < 3 else (nxt, g - 3)
        for j in range(2 * NT):
            yield "S", b, g, j
            if not cross and target[0] is not None:
                for u in (2 * j, 2 * j + 1):
                    yield "A", *target, u
            if not cross and j == 1 and g >= 1 and before[0] is not None:
                yield "M", *before, 0
            if nxt is not None and g == 0 and j == 0:
                yield "LN", nxt, 0, 0
            if nxt is not None and g < 2 and j % 2:
                yield "PREP", nxt, 4 * g + j // 2, 0
            if j >= 2 and j % 2 == 0:
                yield "PV", b, g, j // 2 - 1
            if j == 0 and g >= 1:
                yield "PV", b, g - 1, NT - 1
                yield "O", b, g - 1, 0
            if j == 1 and g >= 1:
                yield "N", b, g - 1, 0
            if nxt is not None and j == 4 and g >= 1:
                yield "STACK", nxt, g - 1, 0
    yield "PV", b, NG - 1, NT - 1
    yield "O", b, NG - 1, 0
    yield "N", b, NG - 1, 0
    if not cross and nxt is not None:
        yield "M", nxt, 1, 0
    yield "OUT", b, 0, 0
    yield "OUT", b, 1, 0
    if nxt is not None:
        yield "STACK", nxt, NG - 1, 0


def attention_prologue(cross):
    yield "LN", 0, 0, 0
    for use in range(8):
        yield "PREP", 0, use, 0
    for g in range(NG):
        yield "STACK", 0, g, 0
    if not cross:
        for g in range(2):
            for u in range(4 * NT):
                yield "A", 0, g, u
            yield "M", 0, g, 0


def run_attention(eng, cross, do):
    def steps(schedule):
        for kind, b, g, j in schedule:
            if kind in do:
                do[kind](b, g, j)

    steps(attention_prologue(cross))
    batch_body(eng, B, lambda b, nxt: steps(attention_schedule(b, nxt, cross)))


def attention(nc, tag, x, const, w, kind):
    cross, causal = kind == "cross", kind == "causal"
    with ExitStack() as ctx:
        def sb(name, shape, dt=F32):
            return ctx.enter_context(nc.sbuf_tensor(f"{tag}_sb_{name}", shape, dt))

        def ps(name, shape, dt=F32):
            return ctx.enter_context(nc.psum_tensor(f"{tag}_{name}", shape, dt))

        def sem(name):
            return ctx.enter_context(nc.semaphore(f"{tag}_{name}"))

        def steps(name, per):
            return Steps(sem(name), per)

        wqkv = sb("wqkv", [P, CC, 3 * D])
        wout = sb("wout", [P, NG, D])
        bqk = sb("bqk", [P, 2 * CC])
        bv = sb("bv", [1, D])
        bo = sb("bo", [1, D])
        stats = sb("stats", [P, NT, 6])
        mv = sb("mv", [P, NT, 2])
        rstd = sb("rstd", [P, 2, NT])
        xn = sb("xn", [P, NT, D])
        xnT = sb("xnT", [P, CC, T])
        ctxT = sb("ctxT", [P, CC, T]) if cross else None
        qk = sb("qk", [P, 4, T])
        hi = sb("hi", [P, 4, T], F32R)
        lo = sb("lo", [P, 4, T], F32R)
        kst = sb("kst", [P, NPAIR, T], F32R)
        qst = [sb(f"qst{e}", [P, NPAIR, T], F32R) for e in range(2)]
        v = sb("v", [P, B, NT, D])
        vaug = sb("vaug", [P, NT, H, 32])
        probs = sb("probs", [P, 4, 2, T])
        o = sb("o", [P, NG, T])
        rz = sb("rz", [P, T])
        mx = sb("mx", [P, NG, NT, GH])
        mT = sb("mT", [GH, NG, T], F32R)
        kmax = sb("kmax", [P, 2, 2])
        kbias = sb("kbias", [P, 4, 2])
        zsum = sb("zsum", [P, 4, 2])
        rzsum = sb("rzsum", [P, 2, 2])
        nothing = sb("nothing", [P, 1])

        s_ps = ps("s_ps", [P, 2, 2, T])
        a_ps = None if cross else ps("a_ps", [P, 2, T])
        m_ps = ps("m_ps", [P, T])
        o_ps = ps("o_ps", [P, T])

        w_in = sem("w_in")
        zeroed = sem("zeroed")
        ctx_in = sem("ctx_in")
        stacked = [sem(f"stacked{g}") for g in range(NG)]
        row_in = [sem(f"row_in{g}") for g in range(NG)]
        ln_stats = steps("ln_stats", 2 * NT)
        ln_rstd = steps("ln_rstd", 2)
        xn_done = steps("xn_done", NT)
        m_ready = steps("m_ready", 8)
        m_act = steps("m_act", 4)
        m_dve = steps("m_dve", 4)
        hi_done = steps("hi_done", 4)
        lo_done = steps("lo_done", 4)
        a_ready = steps("a_ready", 16 * NG)
        a_max = steps("a_max", 16 * NG)
        row_ready = steps("row_ready", NG)
        row_read = steps("row_read", NG)
        s_ready = steps("s_ready", 8 * NG)
        exp_done = steps("exp_done", 8 * NG)
        pv_done = steps("pv_done", NT * NG)
        vaug_done = steps("vaug_done", 8 * NG if cross else NG)
        o_copied = steps("o_copied", NG)
        z_ready = steps("z_ready", NG)
        z_read = steps("z_read", NG)
        o_normed = steps("o_normed", NG)
        out_ready = steps("out_ready", 2)
        x_added = steps("x_added", 2)
        kmax_done = steps("kmax_done", 8 * NG)
        kbias_done = steps("kbias_done", 8 * NG)
        rz_done = steps("rz_done", 8 * NG)

        def first_col(kt):
            return kt * P if causal else 0

        def reads_m(use):
            if 2 <= use < 6:
                return m_dve, use - 2
            return m_act, use if use < 2 else use - 4

        block = ctx.enter_context(nc.Block())

        @block.sync
        def _(sp):
            sp.dma_start(wqkv[:, :, :], w["wqkv"].rearrange("(c p) n -> p c n", p=P)).then_inc(w_in, 16)
            sp.dma_start(wout[:, :, :], w["wout"]).then_inc(w_in, 16)
            sp.dma_start(bqk[:, :], w["bqk"]).then_inc(w_in, 16)
            sp.dma_start(bv[:, :], w["bv"]).then_inc(w_in, 16)
            sp.dma_start(bo[:, :], w["bo"]).then_inc(w_in, 16)

            def context_in(b, *_):
                m_ready.wait(sp, b - 1, 7)
                sp.dma_start(ctxT[:, :, :], w["ctxT"][bass.ds(b, 1)].rearrange("o (c p) t -> p (o c) t", p=P)
                             ).then_inc(ctx_in, 16)

            def stack(b, g, _):
                hg = g // 2
                wait_all(sp, (hi_done, b, 2 + hg), (lo_done, b, 2 + hg), (s_ready, b - 1, 8 * g + 7))
                for p in (2 * g, 2 * g + 1):
                    r = 32 * (p % 4)
                    for blk, part in enumerate((hi, hi, lo)):
                        sp.dma_start(kst[32 * blk:32 * blk + 32, p, :].bitcast(F32),
                                     part[r:r + 32, 2 + hg, :].bitcast(F32)
                                     ).then_inc(stacked[g], 16)
                    for e in range(2):
                        for blk, part in enumerate((hi, lo, hi)):
                            at = 32 * blk + 16 * e
                            sp.dma_start(qst[e][at:at + 16, p, :].bitcast(F32),
                                         part[r + 16 * e:r + 16 * e + 16, hg, :].bitcast(F32)
                                         ).then_inc(stacked[g], 16)

            def rows(b, g, _):
                row_read.wait(sp, b, g)
                for i in range(GH):
                    sp.dma_start(qst[i % 2][96:97, 2 * g + i // 2, :].bitcast(F32),
                                 mT[i:i + 1, g, :].bitcast(F32)).then_inc(row_in[g], 16)

            sp.wait_ge(zeroed, 5)
            run_attention(sp, cross, {"STACK": stack} | ({"LN": context_in} if cross else {"M": rows}))

        @block.gpsimd
        def _(pool):
            pool.memset(vaug[:, :, :, :], 0.0).then_inc(zeroed, 1)
            pool.wait_ge(zeroed, 1)
            pool.memset(vaug[:, :, :, HD:HD + 1], 0.0 if cross else 1.0).then_inc(zeroed, 1)
            for e in range(2):
                pool.memset(qst[e][:, :, :].bitcast(F32), 0.0).then_inc(zeroed, 1)
            pool.wait_ge(zeroed, 4)
            pool.memset(kst[96:97, :, :].bitcast(F32), 1.0).then_inc(zeroed, 1)
            pool.wait_ge(zeroed, 5)
            ln_rstd.begin(pool)
            if not cross:
                vaug_done.begin(pool)

            def ln(b, *_):
                ln_stats.wait(pool, b, 2 * NT - 1)
                xn_done.wait(pool, b - 1, NT - 1)
                pool.tensor_tensor(rstd[:, 0, :], mv[:, :, 1], const["eps"][:, :], ALU.add).then_inc(ln_rstd.sem, 1)
                ln_rstd.wait(pool, b, 0)
                pool.tensor_tensor(rstd[:, 1, :], rstd[:, 0, :], const["minus_half"][:, :], ALU.pow
                                   ).then_inc(ln_rstd.sem, 1)

            def v_group(b, g, _):
                m_act.wait(pool, b, 3)
                pv_done.wait(pool, b - 1, NT * g + NT - 1)
                src = v[:, bass.ds(b, 1), :, :]
                pool.tensor_copy(vaug[:, :, GH * g:GH * g + GH, 0:HD],
                                 src[:, :, :, GH * HD * g:GH * HD * (g + 1)].rearrange(
                                     "p o t (h d) -> p (o t) h d", d=HD)).then_inc(vaug_done.sem, 1)

            run_attention(pool, cross, {"LN": ln} | ({} if cross else {"STACK": v_group}))

        @block.vector
        def _(dve):
            for s in (ln_stats, xn_done, m_dve, lo_done, a_max, z_read, o_normed, x_added,
                      kmax_done, kbias_done, rz_done) + ((vaug_done,) if cross else ()):
                s.begin(dve)
            dve.wait_ge(w_in, 5 * 16)
            if cross:
                dve.wait_ge(zeroed, 5)

            def ln(b, *_):
                ln_stats.wait(dve, b - 1, 2 * NT - 1)
                for t in range(NT):
                    dve.bn_stats(stats[:, t, :], x[:, bass.ds(b * NT + t, 1), :]).then_inc(ln_stats.sem, 1)
                ln_stats.wait(dve, b, NT - 1)
                ln_rstd.wait(dve, b - 1, 1)
                xn_done.wait(dve, b - 1, NT - 1)
                dve.memset(nothing[:, :], 0.0)
                for t in range(NT):
                    dve.bn_aggr(mv[:, t, :], stats[:, t, :]).then_inc(ln_stats.sem, 1)
                ln_stats.wait(dve, b, 2 * NT - 1)
                ln_rstd.wait(dve, b, 1)
                m_ready.wait(dve, b - 1, 1)
                for t in range(NT):
                    dve.tensor_scalar(xn[:, t, :], x[:, bass.ds(b * NT + t, 1), :], mv[:, t, 0:1],
                                      rstd[:, 1, t:t + 1], ALU.subtract, ALU.mult).then_inc(xn_done.sem, 1)

            def prep(b, use, _):
                if not 2 <= use < 6:
                    return
                i = use - 2
                m_ready.wait(dve, b, use)
                hi_done.wait(dve, b - 1, i)
                lo_done.wait(dve, b - 1, i)
                if causal:
                    ins = dve.scalar_tensor_tensor(qk[:, i, :], m_ps[:, :], bqk[:, i:i + 1], const["rope"][:, :],
                                                   ALU.add, ALU.mult)
                else:
                    ins = dve.tensor_scalar(qk[:, i, :], m_ps[:, :], bqk[:, i:i + 1], None, ALU.add)
                ins.then_inc(m_dve.sem, 1)
                hi_done.wait(dve, b, i)
                m_dve.wait(dve, b, i)
                if not (isinstance(b, int) and b == 0):
                    for g in (2 * (i % 2), 2 * (i % 2) + 1):
                        dve.wait_ge(stacked[g], b * 18 * 16)
                dve.tensor_tensor(lo[:, i, :], qk[:, i, :], hi[:, i, :].bitcast(F32), ALU.subtract
                                  ).then_inc(lo_done.sem, 1)

            def row_max(b, g, u):
                h, qt = u // NT, u % NT
                a_ready.wait(dve, b, 16 * g + u)
                if u == 0:
                    row_ready.wait(dve, b - 1, g)
                last = (qt + 1) * P if causal else T
                dve.tensor_reduce(mx[:, g, qt, h:h + 1], a_ps[:, u % 2, 0:last], AX.X, ALU.max
                                  ).then_inc(a_max.sem, 1)

            def norm(b, g, _):
                z_ready.wait(dve, b, g)
                o_normed.wait(dve, b, g - 1)
                dve.reciprocal(rz[:, :], o_ps[:, :]).then_inc(z_read.sem, 1)
                z_read.wait(dve, b, g)
                dve.tensor_tensor(o[:, g, :], o[:, g, :], rz[:, :], ALU.mult).then_inc(o_normed.sem, 1)

            def out(b, j, _):
                out_ready.wait(dve, b, j)
                xs = x[:, bass.ds(b * NT + 2 * j, 2), :]
                dve.tensor_tensor(xs, o_ps[:, :].rearrange("p (t n) -> p t n", n=D), xs, ALU.add
                                  ).then_inc(x_added.sem, 1)

            def key_max(b, g, j):
                n = 8 * g + j
                s_ready.wait(dve, b, n)
                kbias_done.wait(dve, b, n - 1)
                exp_done.wait(dve, b, n - 4)
                dve.tensor_reduce(kmax[:, n % 2, :], s_ps[:, n % 2, :, :], AX.X, ALU.max, negate=True
                                  ).then_inc(kmax_done.sem, 1)
                kmax_done.wait(dve, b, n)
                dve.tensor_scalar(kbias[:, n % 4, :], kmax[:, n % 2, :], SCALE, None, ALU.mult
                                  ).then_inc(kbias_done.sem, 1)

            def scale_v(b, g, kt):
                m_act.wait(dve, b, 3)
                for pp in range(2):
                    n, h = 8 * g + 2 * kt + pp, 4 * g + 2 * pp
                    exp_done.wait(dve, b, n)
                    vaug_done.wait(dve, b, n - 1)
                    dve.reciprocal(rzsum[:, n % 2, :], zsum[:, n % 4, :]).then_inc(rz_done.sem, 1)
                    rz_done.wait(dve, b, n)
                    pv_done.wait(dve, b - 1, NT * g + kt)
                    dve.tensor_tensor(vaug[:, kt, h:h + 2, 0:HD],
                                      v[:, bass.ds(b, 1), kt, HD * h:HD * (h + 2)].rearrange(
                                          "p o (h d) -> p (o h) d", d=HD),
                                      rzsum[:, n % 2, :].unsqueeze(2).to_broadcast([P, 2, HD]), ALU.mult
                                      ).then_inc(vaug_done.sem, 1)

            do = {"LN": ln, "PREP": prep, "OUT": out}
            if cross:
                do |= {"S": key_max, "PV": scale_v}
            else:
                do |= {"A": row_max, "N": norm}
            run_attention(dve, cross, do)

        @block.scalar
        def _(act):
            for s in (m_act, row_read, hi_done, exp_done, o_copied):
                s.begin(act)

            def prep(b, use, _):
                m_ready.wait(act, b, use) if not 2 <= use < 6 else None
                if use < 2:
                    act.activation(xnT[:, use, :], m_ps[:, :], ACT.Copy).then_inc(m_act.sem, 1)
                elif use < 6:
                    i = use - 2
                    m_dve.wait(act, b, i)
                    if not (isinstance(b, int) and b == 0):
                        for g in (2 * (i % 2), 2 * (i % 2) + 1):
                            act.wait_ge(stacked[g], b * 18 * 16)
                    lo_done.wait(act, b - 1, i)
                    act.activation(hi[:, i, :], qk[:, i, :], ACT.Copy).then_inc(hi_done.sem, 1)
                else:
                    t = 2 * (use - 6)
                    act.activation(v[:, bass.ds(b, 1), t:t + 2, :].rearrange("p o t n -> p (o t) n"),
                                   m_ps[:, :].rearrange("p (t n) -> p t n", n=D), ACT.Copy
                                   ).then_inc(m_act.sem, 1)

            def negate_rows(b, g, _):
                row_ready.wait(act, b, g)
                act.activation(mT[:, g, :], m_ps[0:GH, :], ACT.Copy, scale=-1.0).then_inc(row_read.sem, 1)

            def exps(b, g, j):
                n, c0 = 8 * g + j, first_col(j // 2)
                pv_done.wait(act, b, n // 2 - 2)
                if cross:
                    kbias_done.wait(act, b, n)
                    rz_done.wait(act, b, n - 4)
                    for e in range(2):
                        ins = act.activation(probs[:, n % 4, e, :], s_ps[:, n % 2, e, :], ACT.Exp,
                                             bias=kbias[:, n % 4, e:e + 1], scale=SCALE,
                                             accum_out=zsum[:, n % 4, e:e + 1])
                    ins.then_inc(exp_done.sem, 1)
                else:
                    s_ready.wait(act, b, n)
                    act.activation(probs[:, n % 4, :, c0:T], s_ps[:, n % 2, :, c0:T], ACT.Exp, scale=SCALE
                                   ).then_inc(exp_done.sem, 1)

            def copy_o(b, g, _):
                pv_done.wait(act, b, NT * g + NT - 1)
                out_ready.wait(act, b - 1, 1)
                act.activation(o[:, g, :], o_ps[:, :], ACT.Copy).then_inc(o_copied.sem, 1)

            run_attention(act, cross, {"PREP": prep, "S": exps, "O": copy_o}
                          | ({} if cross else {"M": negate_rows}))

        @block.tensor
        def _(pe):
            for s in (m_ready, row_ready, a_ready, s_ready, pv_done, z_ready, out_ready):
                s.begin(pe)
            pe.wait_ge(w_in, 5 * 16)
            pe.wait_ge(zeroed, 5)

            def prep_read(b, use):
                reader, step = reads_m(use)
                reader.wait(pe, b, step)

            def m_free(b, use):
                if use:
                    prep_read(b, use - 1)
                if use in (0, 4) and not cross:
                    row_read.wait(pe, b - 1, 1 if use == 0 else 2)

            def prep(b, use, _):
                m_free(b, use) if use else (row_read.wait(pe, b - 1, 1) if not cross else prep_read(b - 1, 7))
                if use < 2:
                    xn_done.wait(pe, b, NT - 1)
                    for t in range(NT):
                        ins = pe.transpose(m_ps[:, t * P:(t + 1) * P], xn[:, t, use * P:(use + 1) * P],
                                           const["ident"][:, :])
                elif use < 6:
                    i = use - 2
                    m_act.wait(pe, b, 1)
                    if cross and i == 2:
                        pe.wait_ge(ctx_in, (b + 1) * 16)
                    src = ctxT if cross and i >= 2 else xnT
                    for c in range(CC):
                        ins = pe.matmul(m_ps[:, :], wqkv[:, c, i * P:(i + 1) * P], src[:, c, :],
                                        start=c == 0, stop=c == CC - 1)
                else:
                    src = ctxT if cross else xnT
                    for t in (2 * (use - 6), 2 * (use - 6) + 1):
                        at = m_ps[:, (t % 2) * D:(t % 2 + 1) * D]
                        pe.matmul(at, const["ones"][0:1, 0:P], bv[:, :], start=True, stop=False)
                        for c in range(CC):
                            ins = pe.matmul(at, src[:, c, t * P:(t + 1) * P], wqkv[:, c, 2 * D:3 * D],
                                            start=False, stop=c == CC - 1)
                ins.then_inc(m_ready.sem, 1)

            def scores_by_query(b, g, u):
                h, qt = GH * g + u // NT, u % NT
                if u == 0:
                    pe.wait_ge(stacked[g], (b + 1) * 18 * 16)
                a_max.wait(pe, b, 16 * g + u - 2)
                last = (qt + 1) * P if causal else T
                at = a_ps[:, u % 2, 0:last]
                ins = pe.matmul(at, qst[h % 2][0:96, h // 2, qt * P:(qt + 1) * P], kst[0:96, h // 2, 0:last],
                                start=True, stop=not causal)
                if causal:
                    ins = pe.matmul(at[:, qt * P:last], const["ident_b"][:, :], const["mask_q"][:, :],
                                    start=False, stop=True)
                ins.then_inc(a_ready.sem, 1)

            def max_rows(b, g, _):
                a_max.wait(pe, b, 16 * g + 15)
                row_read.wait(pe, b, g - 1)
                if g == 0:
                    prep_read(b, 7)
                elif g >= 2 and not (isinstance(b, int) and b == B - 1):
                    prep_read(b + 1, 4 * g - 5)
                for qt in range(NT):
                    ins = pe.transpose(m_ps[0:GH, qt * P:(qt + 1) * P], mx[:, g, qt, :], const["ident"][:, :])
                ins.then_inc(row_ready.sem, 1)

            def scores_by_key(b, g, j):
                n, kt, p = 8 * g + j, j // 2, 2 * g + j % 2
                if j == 0:
                    pe.wait_ge(*((stacked[g], (b + 1) * 18 * 16) if cross else (row_in[g], (b + 1) * 4 * 16)))
                exp_done.wait(pe, b, n - 2)
                c0, rows = first_col(kt), 96 if cross else 97
                for e in range(2):
                    at = s_ps[:, n % 2, e, c0:T]
                    ins = pe.matmul(at, kst[0:rows, p, kt * P:(kt + 1) * P], qst[e][0:rows, p, c0:T],
                                    start=True, stop=not causal)
                    if causal:
                        ins = pe.matmul(at[:, 0:P], const["ident_b"][:, :], const["mask_k"][:, :],
                                        start=False, stop=True)
                ins.then_inc(s_ready.sem, 1)

            def probs_v(b, g, kt):
                exp_done.wait(pe, b, 8 * g + 2 * kt + 1)
                if cross:
                    vaug_done.wait(pe, b, 8 * g + 2 * kt + 1)
                else:
                    vaug_done.wait(pe, b, g)
                if kt == 0:
                    if g == 0:
                        x_added.wait(pe, b - 1, 1)
                    else:
                        (o_copied if cross else z_read).wait(pe, b, g - 1)
                c0 = first_col(kt)
                for i in range(GH):
                    ins = pe.matmul(o_ps[32 * i:32 * i + 32, c0:T], vaug[:, kt, GH * g + i, :],
                                    probs[:, (2 * kt + i // 2) % 4, i % 2, c0:T],
                                    start=kt == 0, stop=kt == NT - 1)
                ins.then_inc(pv_done.sem, 1)

            def sums(b, g, _):
                o_copied.wait(pe, b, g)
                pe.matmul(o_ps[:, :], const["spread"][:, :], o[:, g, :], start=True, stop=True
                          ).then_inc(z_ready.sem, 1)

            def project(b, j, _):
                if j == 0:
                    (o_copied if cross else o_normed).wait(pe, b, NG - 1)
                else:
                    x_added.wait(pe, b, 0)
                for t in (2 * j, 2 * j + 1):
                    at = o_ps[:, (t % 2) * D:(t % 2 + 1) * D]
                    pe.matmul(at, const["ones"][0:1, 0:P], bo[:, :], start=True, stop=False)
                    for g in range(NG):
                        ins = pe.matmul(at, o[:, g, t * P:(t + 1) * P], wout[:, g, :],
                                        start=False, stop=g == NG - 1)
                ins.then_inc(out_ready.sem, 1)

            do = {"PREP": prep, "S": scores_by_key, "PV": probs_v, "OUT": project}
            if not cross:
                do |= {"A": scores_by_query, "M": max_rows, "N": sums}
            run_attention(pe, cross, do)


def load_constants(nc, ctx, x, inputs):
    const = {}

    def sb(name, shape, dt=F32):
        const[name] = ctx.enter_context(nc.sbuf_tensor(f"const_{name}", shape, dt))
        return const[name]

    ident, spread, rope, ones = sb("ident", [P, P]), sb("spread", [P, P]), sb("rope", [P, T]), sb("ones", [P, P])
    minus_half, eps = sb("minus_half", [P, NT]), sb("eps", [P, NT])
    masks = sb("masks", [P, 2, P])
    iota = sb("iota", [P, 8])
    ident_b, mask_q, mask_k = (sb(n, [P, P], BF16) for n in ("ident_b", "mask_q", "mask_k"))
    loaded = ctx.enter_context(nc.semaphore("const_loaded"))
    made = ctx.enter_context(nc.semaphore("const_made"))
    with nc.Block() as block:
        @block.sync
        def _(sp):
            sp.dma_start(x[:, :, :], inputs["x"].rearrange("b (t p) d -> p (b t) d", p=P)).then_inc(loaded, 16)
            sp.dma_start(ident[:, :], inputs["ident"]).then_inc(loaded, 16)
            sp.dma_start(spread[:, :], inputs["spread"]).then_inc(loaded, 16)
            sp.dma_start(rope[:, :], inputs["rope"]).then_inc(loaded, 16)
            sp.dma_start(masks[:, :, :], inputs["masks"]).then_inc(loaded, 16)
            sp.dma_start(iota[:, :], inputs["iota"]).then_inc(loaded, 16)

        @block.vector
        def _(dve):
            dve.memset(ones[:, :], 1.0).then_inc(made, 1)
            dve.memset(minus_half[:, :], -0.5).then_inc(made, 1)
            dve.memset(eps[:, :], EPS).then_inc(made, 1)
            dve.wait_ge(loaded, 6 * 16)
            dve.tensor_copy(ident_b[:, :], ident[:, :]).then_inc(made, 1)
            dve.tensor_copy(mask_q[:, :], masks[:, 0, :]).then_inc(made, 1)
            dve.tensor_copy(mask_k[:, :], masks[:, 1, :]).then_inc(made, 1)
            dve.wait_ge(made, 6)
    return const


def geglu(nc, tag, x, const, w):
    with ExitStack() as ctx:
        def sb(name, shape, dt=F32):
            return ctx.enter_context(nc.sbuf_tensor(f"{tag}_sb_{name}", shape, dt))

        def ps(name, shape, dt=F32):
            return ctx.enter_context(nc.psum_tensor(f"{tag}_{name}", shape, dt))

        def steps(name, per):
            return Steps(ctx.enter_context(nc.semaphore(f"{tag}_{name}")), per)

        FC = T // P
        stats = sb("stats", [P, NT, 6])
        mv = sb("mv", [P, NT, 2])
        rstd = sb("rstd", [P, 2, NT])
        xn = sb("xn", [P, NT, D])
        xnT = sb("xnT", [P, CC, T])
        ctxT = sb("ctxT", [P, CC, T])
        ctxN = sb("ctxN", [P, FC, D])
        gelu = sb("gelu", [P, FC, T])
        h = sb("h", [P, FC, T])
        nothing = sb("nothing", [P, 1])

        t_ps = ps("t_ps", [P, CC, T])
        g_ps = ps("g_ps", [P, FC, T])
        y_ps = ps("y_ps", [P, 2, 2, D])

        ctxT_in = ctx.enter_context(nc.semaphore(f"{tag}_ctxT_in"))
        ctxN_in = ctx.enter_context(nc.semaphore(f"{tag}_ctxN_in"))
        ln_stats = steps("ln_stats", 2 * NT)
        ln_rstd = steps("ln_rstd", 2)
        xn_done = steps("xn_done", NT)
        t_ready = steps("t_ready", CC)
        t_read = steps("t_read", CC)
        g_ready = steps("g_ready", FC)
        g_gelu = steps("g_gelu", FC)
        h_done = steps("h_done", FC)
        y_ready = steps("y_ready", 2)
        x_added = steps("x_added", 2)

        block = ctx.enter_context(nc.Block())

        def run(eng, do):
            do.get("LN", lambda b: None)(0)

            def body(b, nxt):
                for kind in ("IN", "T", "G"):
                    do.get(kind, lambda b: None)(b)
                if nxt is not None:
                    do.get("LN", lambda b: None)(nxt)
                do.get("Y", lambda b: None)(b)
            batch_body(eng, B, body)

        @block.sync
        def _(sp):
            def context_in(b):
                wait_all(sp, (g_ready, b - 1, FC - 1), (y_ready, b - 1, 1))
                sp.dma_start(ctxT[:, :, :], w["ctxT"][bass.ds(b, 1)].rearrange("o (c p) t -> p (o c) t", p=P)
                             ).then_inc(ctxT_in, 16)
                sp.dma_start(ctxN[:, :, :], w["ctx"][bass.ds(b, 1)].rearrange("o (c p) d -> p (o c) d", p=P)
                             ).then_inc(ctxN_in, 16)
            run(sp, {"IN": context_in})

        @block.gpsimd
        def _(pool):
            ln_rstd.begin(pool)
            run(pool, {"LN": lambda b: inverse_deviation(pool, b, mv, rstd, const, ln_stats, ln_rstd, xn_done)})

        @block.vector
        def _(dve):
            for s in (ln_stats, xn_done, h_done, x_added):
                s.begin(dve)

            def gate(b):
                for f in range(FC):
                    g_gelu.wait(dve, b, f)
                    y_ready.wait(dve, b - 1, 1)
                    dve.tensor_tensor(h[:, f, :], g_ps[:, f, :], gelu[:, f, :], ALU.mult).then_inc(h_done.sem, 1)

            def add(b):
                for j in range(2):
                    y_ready.wait(dve, b, j)
                    xs = x[:, bass.ds(b * NT + 2 * j, 2), :]
                    dve.tensor_tensor(xs, y_ps[:, j, :, :], xs, ALU.add).then_inc(x_added.sem, 1)

            run(dve, {"LN": lambda b: normalise(dve, b, x, stats, mv, rstd, xn, nothing, ln_stats, ln_rstd,
                                                xn_done, t_ready, CC - 1),
                      "G": gate, "Y": add})

        @block.scalar
        def _(act):
            for s in (t_read, g_gelu):
                s.begin(act)

            def transposed(b):
                for c in range(CC):
                    t_ready.wait(act, b, c)
                    g_ready.wait(act, b - 1, FC - 1)
                    act.activation(xnT[:, c, :], t_ps[:, c, :], ACT.Copy).then_inc(t_read.sem, 1)

            def gate(b):
                for f in range(FC):
                    g_ready.wait(act, b, f)
                    h_done.wait(act, b - 1, f)
                    act.activation(gelu[:, f, :], g_ps[:, f, :], ACT.Gelu_apprx_tanh).then_inc(g_gelu.sem, 1)

            run(act, {"T": transposed, "G": gate})

        @block.tensor
        def _(pe):
            for s in (t_ready, g_ready, y_ready):
                s.begin(pe)

            def transpose(b):
                xn_done.wait(pe, b, NT - 1)
                for c in range(CC):
                    t_read.wait(pe, b - 1, c)
                    for t in range(NT):
                        ins = pe.transpose(t_ps[:, c, t * P:(t + 1) * P], xn[:, t, c * P:(c + 1) * P],
                                           const["ident"][:, :])
                    ins.then_inc(t_ready.sem, 1)

            def hidden(b):
                pe.wait_ge(ctxT_in, (b + 1) * 16)
                t_read.wait(pe, b, CC - 1)
                for f in range(FC):
                    h_done.wait(pe, b - 1, f)
                    for c in range(CC):
                        ins = pe.matmul(g_ps[:, f, :], ctxT[:, c, f * P:(f + 1) * P], xnT[:, c, :],
                                        start=c == 0, stop=c == CC - 1)
                    ins.then_inc(g_ready.sem, 1)

            def output(b):
                pe.wait_ge(ctxN_in, (b + 1) * 16)
                h_done.wait(pe, b, FC - 1)
                for j in range(2):
                    x_added.wait(pe, b - 1, j)
                    for t in range(2):
                        for f in range(FC):
                            ins = pe.matmul(y_ps[:, j, t, :], h[:, f, (2 * j + t) * P:(2 * j + t + 1) * P],
                                            ctxN[:, f, :], start=f == 0, stop=f == FC - 1)
                    ins.then_inc(y_ready.sem, 1)

            run(pe, {"T": transpose, "G": hidden, "Y": output})


def inverse_deviation(pool, b, mv, rstd, const, ln_stats, ln_rstd, xn_done):
    ln_stats.wait(pool, b, 2 * NT - 1)
    xn_done.wait(pool, b - 1, NT - 1)
    pool.tensor_tensor(rstd[:, 0, :], mv[:, :, 1], const["eps"][:, :], ALU.add).then_inc(ln_rstd.sem, 1)
    ln_rstd.wait(pool, b, 0)
    pool.tensor_tensor(rstd[:, 1, :], rstd[:, 0, :], const["minus_half"][:, :], ALU.pow).then_inc(ln_rstd.sem, 1)


def normalise(dve, b, x, stats, mv, rstd, xn, nothing, ln_stats, ln_rstd, xn_done, xn_read, last_read):
    ln_stats.wait(dve, b - 1, 2 * NT - 1)
    for t in range(NT):
        dve.bn_stats(stats[:, t, :], x[:, bass.ds(b * NT + t, 1), :]).then_inc(ln_stats.sem, 1)
    ln_stats.wait(dve, b, NT - 1)
    ln_rstd.wait(dve, b - 1, 1)
    xn_done.wait(dve, b - 1, NT - 1)
    dve.memset(nothing[:, :], 0.0)
    for t in range(NT):
        dve.bn_aggr(mv[:, t, :], stats[:, t, :]).then_inc(ln_stats.sem, 1)
    ln_stats.wait(dve, b, 2 * NT - 1)
    ln_rstd.wait(dve, b, 1)
    xn_read.wait(dve, b - 1, last_read)
    for t in range(NT):
        dve.tensor_scalar(xn[:, t, :], x[:, bass.ds(b * NT + t, 1), :], mv[:, t, 0:1],
                          rstd[:, 1, t:t + 1], ALU.subtract, ALU.mult).then_inc(xn_done.sem, 1)


def moe(nc, tag, x, const, w, width, phi, shared):
    E, FC = 8, width // P
    NX = E + (1 if shared else 0)
    NTILE = B * NT
    with ExitStack() as ctx:
        def sb(name, shape, dt=F32):
            return ctx.enter_context(nc.sbuf_tensor(f"{tag}_sb_{name}", shape, dt))

        def ps(name, shape, dt=F32):
            return ctx.enter_context(nc.psum_tensor(f"{tag}_{name}", shape, dt))

        def sem(name):
            return ctx.enter_context(nc.semaphore(f"{tag}_{name}"))

        stats = sb("stats", [P, NT, 6])
        mv = sb("mv", [P, NT, 2])
        rstd = sb("rstd", [P, 2, NT])
        xn = sb("xn", [P, NT, D])
        xnT = sb("xnT", [P, CC, B, T])
        nothing = sb("nothing", [P, 1])
        router = sb("router", [P, CC, E])
        rbias = sb("rbias", [1, E])
        weights = sb("weights", [P, NTILE, NX])
        r = {n: sb(n, [P, NTILE, E]) for n in ("lg", "eq", "cand", "oh1", "oh2", "l2", "ab", "df", "keep")}
        c1 = {n: sb(n, [P, NTILE]) for n in ("m1", "m2", "first", "ex", "den", "r1", "r2")}
        w1 = sb("w1", [P, 2, CC, width])
        w3 = sb("w3", [P, 2, CC, width])
        w2 = sb("w2", [P, 2, FC, D])
        silu = sb("silu", [P, 2, T])
        h = sb("h", [P, 2, FC, T])

        ln_stats = Steps(sem("ln_stats"), 2 * NT)
        ln_rstd = Steps(sem("ln_rstd"), 2)
        xn_done = Steps(sem("xn_done"), NT)
        t_ready = Steps(sem("t_ready"), CC)
        t_read = Steps(sem("t_read"), CC)
        router_in = sem("router_in")
        logits_ready = sem("logits_ready")
        routed = sem("routed")
        route_exp = sem("route_exp")

        with ExitStack() as inner:
            t_ps = inner.enter_context(nc.psum_tensor(f"{tag}_t_ps", [P, CC, T], F32))
            l_ps = inner.enter_context(nc.psum_tensor(f"{tag}_l_ps", [P, NTILE, E], F32))
            block = inner.enter_context(nc.Block())

            @block.sync
            def _(sp):
                sp.dma_start(router[:, :, :], w["router"].rearrange("(c p) e -> p c e", p=P)).then_inc(router_in, 16)
                sp.dma_start(rbias[:, :], w["router_bias"]).then_inc(router_in, 16)

            @block.gpsimd
            def _(pool):
                ln_rstd.begin(pool)
                for b in range(B):
                    inverse_deviation(pool, b, mv, rstd, const, ln_stats, ln_rstd, xn_done)

            @block.scalar
            def _(act):
                t_read.begin(act)
                for b in range(B):
                    for c in range(CC):
                        t_ready.wait(act, b, c)
                        act.activation(xnT[:, c, b, :], t_ps[:, c, :], ACT.Copy).then_inc(t_read.sem, 1)
                if phi:
                    for k, name in enumerate(("df", "l2")):
                        act.wait_ge(routed, PHI_EXP[k])
                        act.activation(r[name][:, :, :], r[name][:, :, :], ACT.Exp).then_inc(route_exp, 1)
                else:
                    act.wait_ge(routed, TOP2_EXP)
                    act.activation(c1["ex"][:, :], c1["ex"][:, :], ACT.Exp).then_inc(route_exp, 1)

            @block.tensor
            def _(pe):
                t_ready.begin(pe)
                pe.wait_ge(router_in, 32)
                for b in range(B):
                    xn_done.wait(pe, b, NT - 1)
                    for c in range(CC):
                        t_read.wait(pe, b - 1, c)
                        for t in range(NT):
                            ins = pe.transpose(t_ps[:, c, t * P:(t + 1) * P], xn[:, t, c * P:(c + 1) * P],
                                               const["ident"][:, :])
                        ins.then_inc(t_ready.sem, 1)
                t_read.wait(pe, B - 1, CC - 1)
                for b in range(B):
                    for t in range(NT):
                        at = l_ps[:, b * NT + t, :]
                        pe.matmul(at, const["ones"][0:1, 0:P], rbias[:, :], start=True, stop=False)
                        for c in range(CC):
                            ins = pe.matmul(at, xnT[:, c, b, t * P:(t + 1) * P], router[:, c, :],
                                            start=False, stop=c == CC - 1)
                ins.then_inc(logits_ready, 1)

            @block.vector
            def _(dve):
                for s in (ln_stats, xn_done):
                    s.begin(dve)
                for b in range(B):
                    normalise(dve, b, x, stats, mv, rstd, xn, nothing, ln_stats, ln_rstd, xn_done,
                              t_ready, CC - 1)
                dve.wait_ge(logits_ready, 1)
                route(dve, const, l_ps, r, c1, weights, phi, shared, routed, route_exp)

        with ExitStack() as inner:
            g_ps = inner.enter_context(nc.psum_tensor(f"{tag}_g_ps", [P, 2, 2, T], F32))
            y_ps = inner.enter_context(nc.psum_tensor(f"{tag}_y_ps", [P, 4, T], F32))
            PER = B * FC * 2
            w_in = [sem(f"w_in{k}") for k in range(2)]
            g_ready = Steps(sem("g_ready"), PER)
            g_silu = Steps(sem("g_silu"), PER)
            h_done = Steps(sem("h_done"), PER)
            y_ready = Steps(sem("y_ready"), 2 * B * NT)
            x_added = Steps(sem("x_added"), 2 * B * NT)
            block = inner.enter_context(nc.Block())

            def pair(i, experts, do):
                todo = [(k, tb) for k in range(experts) for tb in range(B)]
                for n, (k, tb) in enumerate(todo):
                    for f in range(FC):
                        do("G", i, k, tb, f)
                        if n and f % (FC // NT) == FC // NT - 1:
                            do("Y", i, *todo[n - 1], f // (FC // NT))
                for t in range(NT):
                    do("Y", i, *todo[-1], t)

            def run(eng, do):
                def step(kind, *args):
                    if kind in do:
                        do[kind](*args)
                with eng.Fori(0, E // 2) as i:
                    pair(i, 2, step)
                if shared:
                    pair(E // 2, 1, step)

            @block.sync
            def _(sp):
                def load(i, k):
                    wait_all(sp, (y_ready, i - 1, 16 * k + 15))
                    e = i * 2 + k
                    sp.dma_start(w1[:, k, :, :], w["w1"][bass.ds(e, 1)].rearrange("o (c p) f -> p (o c) f", p=P)).then_inc(w_in[k], 16)
                    sp.dma_start(w3[:, k, :, :], w["w3"][bass.ds(e, 1)].rearrange("o (c p) f -> p (o c) f", p=P)).then_inc(w_in[k], 16)
                    sp.dma_start(w2[:, k, :, :], w["w2"][bass.ds(e, 1)].rearrange("o (c p) d -> p (o c) d", p=P)).then_inc(w_in[k], 16)
                with sp.Fori(0, E // 2) as i:
                    load(i, 0)
                    load(i, 1)
                if shared:
                    load(E // 2, 0)

            @block.scalar
            def _(act):
                g_silu.begin(act)

                def gate(i, k, tb, f):
                    n = (k * B + tb) * FC + f
                    g_ready.wait(act, i, n)
                    h_done.wait(act, i, n - 2)
                    act.activation(silu[:, n % 2, :], g_ps[:, n % 2, 0, :], ACT.Silu).then_inc(g_silu.sem, 1)
                run(act, {"G": gate})

            @block.vector
            def _(dve):
                for s in (h_done, x_added):
                    s.begin(dve)

                def hidden(i, k, tb, f):
                    n = (k * B + tb) * FC + f
                    g_silu.wait(dve, i, n)
                    y_ready.wait(dve, i, (k * B + tb - 2) * NT + NT - 1)
                    dve.tensor_tensor(h[:, tb % 2, f, :], g_ps[:, n % 2, 1, :], silu[:, n % 2, :], ALU.mult
                                      ).then_inc(h_done.sem, 1)

                def add(i, k, tb, t):
                    m = (k * B + tb) * NT + t
                    tile = tb * NT + t
                    y_ready.wait(dve, i, m)
                    x_added.wait(dve, i, m - 16)
                    dve.scalar_tensor_tensor(x[:, tile, :], y_ps[:, m % 4, 0:D],
                                             weights[:, tile, bass.ds(i * 2 + k, 1)].rearrange("p o -> p o"),
                                             x[:, tile, :], ALU.mult, ALU.add).then_inc(x_added.sem, 1)
                run(dve, {"G": hidden, "Y": add})

            @block.tensor
            def _(pe):
                for s in (g_ready, y_ready):
                    s.begin(pe)

                def hidden(i, k, tb, f):
                    n = (k * B + tb) * FC + f
                    if tb == 0 and f == 0:
                        pe.wait_ge(w_in[k], (i + 1) * 48)
                    h_done.wait(pe, i, n - 2)
                    for half, ws in enumerate((w1, w3)):
                        for c in range(CC):
                            ins = pe.matmul(g_ps[:, n % 2, half, :], ws[:, k, c, f * P:(f + 1) * P],
                                            xnT[:, c, tb, :], start=c == 0, stop=c == CC - 1)
                    ins.then_inc(g_ready.sem, 1)

                def output(i, k, tb, t):
                    m = (k * B + tb) * NT + t
                    h_done.wait(pe, i, (k * B + tb) * FC + FC - 1)
                    x_added.wait(pe, i, m - 4)
                    for f in range(FC):
                        ins = pe.matmul(y_ps[:, m % 4, 0:D], h[:, tb % 2, f, t * P:(t + 1) * P], w2[:, k, f, :],
                                        start=f == 0, stop=f == FC - 1)
                    ins.then_inc(y_ready.sem, 1)
                run(pe, {"G": hidden, "Y": output})


PHI_EXP = (12, 28)
TOP2_EXP = 13


def route(dve, const, l_ps, r, c1, weights, phi, shared, routed, route_exp):
    E, NTILE = 8, B * NT
    step = [0]

    def then(ins):
        step[0] += 1
        ins.then_inc(routed, 1)
        dve.wait_ge(routed, step[0])

    def full(t):
        return t[:, :, :]

    def wide(t):
        return t[:, :].unsqueeze(2).to_broadcast([P, NTILE, E])

    iota = const["iota"][:, :].unsqueeze(1).to_broadcast([P, NTILE, E])
    lg, eq, cand, oh1, oh2, l2 = (r[n] for n in ("lg", "eq", "cand", "oh1", "oh2", "l2"))
    then(dve.tensor_copy(full(lg), l_ps[:, :, :]))

    def top(src, m, oh):
        then(dve.tensor_reduce(c1[m][:, :], full(src), AX.X, ALU.max))
        then(dve.tensor_tensor(full(eq), full(src), wide(c1[m]), ALU.not_equal))
        then(dve.scalar_tensor_tensor(full(cand), full(eq), float(E), iota, ALU.mult, ALU.add))
        then(dve.tensor_reduce(c1["first"][:, :], full(cand), AX.X, ALU.min))
        then(dve.tensor_tensor(full(oh), wide(c1["first"]), iota, ALU.is_equal))

    def unmasked_sum(m, ex, drop, out, nexp):
        ab, keep = r["ab"], r["keep"]
        then(dve.scalar_tensor_tensor(full(ab), full(lg), -1.0, full(lg), ALU.mult, ALU.max))
        then(dve.tensor_tensor(full(ab), full(ab), wide(c1[m]), ALU.max))
        then(dve.tensor_tensor(full(keep), wide(c1[m]), full(lg), ALU.subtract))
        then(dve.scalar_tensor_tensor(full(keep), full(ab), 0.02, full(keep), ALU.mult, ALU.is_ge))
        if drop is not None:
            then(dve.scalar_tensor_tensor(full(keep), full(drop), 0.0, full(keep), ALU.is_equal, ALU.mult))
        then(dve.tensor_tensor(full(ex), full(lg), wide(c1[m]), ALU.subtract))
        then(dve.tensor_scalar(full(ex), full(ex), 0.0, None, ALU.min))
        assert step[0] == PHI_EXP[nexp - 1], step[0]
        dve.wait_ge(route_exp, nexp)
        then(dve.tensor_tensor(full(ex), full(ex), full(keep), ALU.mult))
        then(dve.tensor_reduce(c1["den"][:, :], full(ex), AX.X, ALU.add))
        then(dve.reciprocal(c1[out][:, :], c1["den"][:, :]))

    top(lg, "m1", oh1)
    if phi:
        unmasked_sum("m1", r["df"], None, "r1", 1)
    then(dve.scalar_tensor_tensor(full(l2), full(oh1), -3e38, full(lg), ALU.mult, ALU.add))

    top(l2, "m2", oh2)
    if phi:
        unmasked_sum("m2", l2, oh1, "r2", 2)
    else:
        then(dve.tensor_tensor(c1["ex"][:, :], c1["m2"][:, :], c1["m1"][:, :], ALU.subtract))
        assert step[0] == TOP2_EXP
        dve.wait_ge(route_exp, 1)
        then(dve.tensor_scalar(c1["den"][:, :], c1["ex"][:, :], 1.0, None, ALU.add))
        then(dve.reciprocal(c1["r1"][:, :], c1["den"][:, :]))
        then(dve.tensor_tensor(c1["r2"][:, :], c1["ex"][:, :], c1["r1"][:, :], ALU.mult))
    then(dve.tensor_tensor(full(oh1), full(oh1), wide(c1["r1"]), ALU.mult))
    then(dve.tensor_tensor(full(oh2), full(oh2), wide(c1["r2"]), ALU.mult))
    then(dve.tensor_tensor(weights[:, :, 0:E], full(oh1), full(oh2), ALU.add))
    if shared:
        then(dve.memset(weights[:, :, E:E + 1], 1.0))


def build(nc, inputs, out):
    with ExitStack() as ctx:
        x = ctx.enter_context(nc.sbuf_tensor("x_sb", [P, B * NT, D], F32))
        const = load_constants(nc, ctx, x, inputs)

        def of(tag):
            return {n[len(tag) + 1:]: a for n, a in inputs.items() if n.startswith(tag + "_")}

        context = {"ctx": inputs["ctx"], "ctxT": inputs["ctxT"]}
        attention(nc, "l0a", x, const, of("l0a"), "causal")
        geglu(nc, "l0g", x, const, context)
        moe(nc, "l0m", x, const, of("l0m"), 512, phi=False, shared=True)
        attention(nc, "l1a", x, const, of("l1a"), "full")
        attention(nc, "l1x", x, const, of("l1x") | context, "cross")
        moe(nc, "l1m", x, const, of("l1m"), 1024, phi=True, shared=False)

        stored = ctx.enter_context(nc.semaphore("stored"))
        with nc.Block() as block:
            @block.sync
            def _(sp):
                sp.dma_start(out.rearrange("b (t p) d -> p (b t) d", p=P), x[:, :, :]).then_inc(stored, 16)
                sp.wait_ge(stored, 16)


def rope_factor():
    theta = np.float32(1) / np.float32(10000) ** (np.float32(2) * np.arange(HD // 2, dtype=np.float32) / np.float32(HD))
    ang = np.arange(1, T + 1, dtype=np.float32)[:, None] * theta.astype(np.float32)[None]
    ang = np.concatenate([ang, ang], axis=-1).astype(np.float32)
    return (np.cos(ang) + np.sin(ang)).astype(np.float32)


def layout(i):
    a = {"x": i["x"], "ctx": i["ctx_1024"], "ctxT": i["ctx_1024"].transpose(0, 2, 1)}
    at = np.arange(P)
    a["ident"] = np.eye(P, dtype=np.float32)
    a["spread"] = ((at[:, None] % 32 == HD) & (at[:, None] // 32 == at[None] // 32)).astype(np.float32)
    a["rope"] = np.tile(rope_factor().T, (P // HD, 1))
    a["masks"] = np.stack([np.where(at[None] > at[:, None], NEG, 0), np.where(at[None] < at[:, None], NEG, 0)],
                          axis=1).astype(np.float32)
    a["iota"] = np.tile(np.arange(8, dtype=np.float32), (P, 1))

    def heads_padded(wt):
        padded = np.zeros((GH, 32, NG, D), np.float32)
        padded[:, 0:HD] = wt.reshape(NG, GH, HD, D).transpose(1, 2, 0, 3)
        return padded.reshape(P, NG, D)

    def attn(tag, wt, bias, wout, bout):
        a[tag + "_wqkv"] = wt
        a[tag + "_bqk"] = bias[0:2 * D].reshape(2 * CC, P).T
        a[tag + "_bv"] = bias[None, 2 * D:]
        a[tag + "_wout"] = heads_padded(wout)
        a[tag + "_bo"] = bout[None]

    attn("l0a", i["L0_attn_W_attn"].T, i["L0_attn_b_attn"], i["L0_attn_W_proj"].T, i["L0_attn_b_proj"])
    attn("l1a", i["L1_attn_W_qkv"].reshape(H, 3, HD, D).transpose(1, 0, 2, 3).reshape(3 * D, D).T,
         i["L1_attn_b_qkv"].reshape(H, 3, HD).transpose(1, 0, 2).reshape(3 * D),
         i["L1_attn_W_out"].T, i["L1_attn_b_out"])
    attn("l1x", np.concatenate([i["L1_xattn_Wq"], i["L1_xattn_Wkv"]], axis=1),
         np.concatenate([i["L1_xattn_bq"], i["L1_xattn_bkv"]]), i["L1_xattn_Wo"], i["L1_xattn_bo"])
    a["l0m_router"], a["l0m_router_bias"] = i["L0_ffn_router_w"].T, i["L0_ffn_experts_bias"][None]
    for n in ("w1", "w3", "w2"):
        a["l0m_" + n] = np.concatenate([i["L0_ffn_" + n], i["L0_ffn_s" + n]])
    a["l1m_router"], a["l1m_router_bias"] = i["L1_ffn_gate_w"].T, np.zeros((1, 8), np.float32)
    for n in ("w1", "w3", "w2"):
        a["l1m_" + n] = i["L1_ffn_" + n].transpose(0, 2, 1)
    return a


def kernel(**inputs):
    import concourse.bacc as bacc
    from concourse.bass_utils import run_bass_kernel_spmd

    arrays = {f"in_{n}": np.ascontiguousarray(a) for n, a in layout({n: np.asarray(a) for n, a in inputs.items()}).items()}
    nc = bacc.Bacc("TRN2", target_bir_lowering=False, num_devices=1)
    aps = {n[3:]: nc.dram_tensor(n, a.shape, mybir.dt.from_np(a.dtype), kind="ExternalInput").ap()
           for n, a in arrays.items()}
    out = nc.dram_tensor("out_x", (B, T, D), F32, kind="ExternalOutput").ap()
    build(nc, aps, out)
    r = run_bass_kernel_spmd(nc, [arrays], core_ids=[0])
    return r.results[0]["out_x"]
```

```python
from contextlib import ExitStack

import numpy as np

import concourse.bass as bass
from concourse import mybir

F32 = mybir.dt.float32
F32R = mybir.dt.float32r
BF16 = mybir.dt.bfloat16
I32 = mybir.dt.int32
U32 = mybir.dt.uint32
ALU = mybir.AluOpType
ACT = mybir.ActivationFunctionType
AX = mybir.AxisListType

P = 128
B, T, D = 4, 512, 256
NT = T // P
CC = D // P
H, HD = 16, 16
GH = 4
NG = H // GH
NPAIR = H // 2
EPS = 1e-5
NEG = -1e30
SCALE = 1.0 / 4.0


class Steps:

    def __init__(self, sem, per):
        self.sem, self.per = sem, per

    def begin(self, eng):
        eng.sem_inc(self.sem, self.per)

    def count(self, b, step):
        return (b + 1) * self.per + step + 1

    def wait(self, eng, b, step):
        eng.wait_ge(self.sem, self.count(b, step))


def wait_all(eng, *waits):
    values = [s.count(b, step) for s, b, step in waits]
    for v in values:
        eng.compute_val(v)
    for (s, _, _), v in zip(waits, values):
        eng.wait_ge(s.sem, v)


def batch_body(eng, nb, body):
    with eng.Fori(0, nb - 1) as b:
        body(b, b + 1)
    body(nb - 1, None)


def attention_schedule(b, nxt, cross):
    for g in range(NG):
        target = (b, g + 2) if g < 2 else (nxt, g - 2)
        before = (b, g + 1) if 1 <= g < 3 else (nxt, g - 3)
        for j in range(2 * NT):
            yield "S", b, g, j
            if not cross and target[0] is not None:
                for u in (2 * j, 2 * j + 1):
                    yield "A", *target, u
            if not cross and j == 1 and g >= 1 and before[0] is not None:
                yield "M", *before, 0
            if nxt is not None and g == 0 and j == 0:
                yield "LN", nxt, 0, 0
            if nxt is not None and g < 2 and j % 2:
                yield "PREP", nxt, 4 * g + j // 2, 0
            if j >= 2 and j % 2 == 0:
                yield "PV", b, g, j // 2 - 1
            if j == 0 and g >= 1:
                yield "PV", b, g - 1, NT - 1
                yield "O", b, g - 1, 0
            if j == 1 and g >= 1:
                yield "N", b, g - 1, 0
            if nxt is not None and j == 4 and g >= 1:
                yield "STACK", nxt, g - 1, 0
    yield "PV", b, NG - 1, NT - 1
    yield "O", b, NG - 1, 0
    yield "N", b, NG - 1, 0
    if not cross and nxt is not None:
        yield "M", nxt, 1, 0
    yield "OUT", b, 0, 0
    yield "OUT", b, 1, 0
    if nxt is not None:
        yield "STACK", nxt, NG - 1, 0


def attention_prologue(cross):
    yield "LN", 0, 0, 0
    for use in range(8):
        yield "PREP", 0, use, 0
    for g in range(NG):
        yield "STACK", 0, g, 0
    if not cross:
        for g in range(2):
            for u in range(4 * NT):
                yield "A", 0, g, u
            yield "M", 0, g, 0


def run_attention(eng, cross, do):
    def steps(schedule):
        for kind, b, g, j in schedule:
            if kind in do:
                do[kind](b, g, j)

    steps(attention_prologue(cross))
    batch_body(eng, B, lambda b, nxt: steps(attention_schedule(b, nxt, cross)))


def attention(nc, tag, x, const, w, kind):
    cross, causal = kind == "cross", kind == "causal"
    with ExitStack() as ctx:
        def sb(name, shape, dt=F32):
            return ctx.enter_context(nc.sbuf_tensor(f"{tag}_sb_{name}", shape, dt))

        def ps(name, shape, dt=F32):
            return ctx.enter_context(nc.psum_tensor(f"{tag}_{name}", shape, dt))

        def sem(name):
            sems.append(nc.alloc_semaphore(name=f"{tag}_{name}"))
            return sems[-1]

        def steps(name, per):
            return Steps(sem(name), per)

        sems = []
        ctx.callback(nc.all_engine_barrier)
        ctx.callback(nc.clear_and_free_semaphores, sems)

        wqkv = sb("wqkv", [P, CC, 3 * D])
        wout = sb("wout", [P, NG, D])
        bqk = sb("bqk", [P, 2 * CC])
        bv = sb("bv", [1, D])
        bo = sb("bo", [1, D])
        stats = sb("stats", [P, NT, 6])
        mv = sb("mv", [P, NT, 2])
        rstd = sb("rstd", [P, 2, NT])
        xn = sb("xn", [P, NT, D])
        xnT = sb("xnT", [P, CC, T])
        ctxT = sb("ctxT", [P, CC, T]) if cross else None
        qk = sb("qk", [P, 4, T])
        hi = sb("hi", [P, 4, T], F32R)
        lo = sb("lo", [P, 4, T], F32R)
        kst = sb("kst", [P, NPAIR, T], F32R)
        qst = [sb(f"qst{e}", [P, NPAIR, T], F32R) for e in range(2)]
        v = sb("v", [P, B, NT, D])
        vaug = sb("vaug", [P, NT, H, 32])
        probs = sb("probs", [P, 4, 2, T])
        o = sb("o", [P, NG, T])
        rz = sb("rz", [P, T])
        mx = sb("mx", [P, NG, NT, GH])
        mT = sb("mT", [GH, NG, T], F32R)
        kmax = sb("kmax", [P, 2, 2])
        kbias = sb("kbias", [P, 4, 2])
        zsum = sb("zsum", [P, 4, 2])
        rzsum = sb("rzsum", [P, 2, 2])
        nothing = sb("nothing", [P, 1])

        s_ps = ps("s_ps", [P, 2, 2, T])
        a_ps = None if cross else ps("a_ps", [P, 2, T])
        m_ps = ps("m_ps", [P, T])
        o_ps = ps("o_ps", [P, T])

        w_in = sem("w_in")
        zeroed = sem("zeroed")
        ctx_in = sem("ctx_in")
        stacked = [sem(f"stacked{g}") for g in range(NG)]
        row_in = [sem(f"row_in{g}") for g in range(NG)]
        ln_stats = steps("ln_stats", 2 * NT)
        ln_rstd = steps("ln_rstd", 2)
        xn_done = steps("xn_done", NT)
        m_ready = steps("m_ready", 8)
        m_act = steps("m_act", 4)
        m_dve = steps("m_dve", 4)
        hi_done = steps("hi_done", 4)
        lo_done = steps("lo_done", 4)
        a_ready = steps("a_ready", 16 * NG)
        a_max = steps("a_max", 16 * NG)
        row_ready = steps("row_ready", NG)
        row_read = steps("row_read", NG)
        s_ready = steps("s_ready", 8 * NG)
        exp_done = steps("exp_done", 8 * NG)
        pv_done = steps("pv_done", NT * NG)
        vaug_done = steps("vaug_done", 8 * NG if cross else NG)
        o_copied = steps("o_copied", NG)
        z_ready = steps("z_ready", NG)
        z_read = steps("z_read", NG)
        o_normed = steps("o_normed", NG)
        out_ready = steps("out_ready", 2)
        x_added = steps("x_added", 2)
        if cross:
            kmax_done = steps("kmax_done", 8 * NG)
            kbias_done = steps("kbias_done", 8 * NG)
            rz_done = steps("rz_done", 8 * NG)

        def first_col(kt):
            return kt * P if causal else 0

        def reads_m(use):
            if 2 <= use < 6:
                return m_dve, use - 2
            return m_act, use if use < 2 else use - 4

        block = ctx.enter_context(nc.Block())

        @block.sync
        def _(sp):
            sp.dma_start(wqkv[:, :, :], w["wqkv"].rearrange("(c p) n -> p c n", p=P)).then_inc(w_in, 16)
            sp.dma_start(wout[:, :, :], w["wout"]).then_inc(w_in, 16)
            sp.dma_start(bqk[:, :], w["bqk"]).then_inc(w_in, 16)
            sp.dma_start(bv[:, :], w["bv"]).then_inc(w_in, 16)
            sp.dma_start(bo[:, :], w["bo"]).then_inc(w_in, 16)

            def context_in(b, *_):
                m_ready.wait(sp, b - 1, 7)
                sp.dma_start(ctxT[:, :, :], w["ctxT"][bass.ds(b, 1)].rearrange("o (c p) t -> p (o c) t", p=P)
                             ).then_inc(ctx_in, 16)

            def stack(b, g, _):
                hg = g // 2
                wait_all(sp, (hi_done, b, 2 + hg), (lo_done, b, 2 + hg), (s_ready, b - 1, 8 * g + 7))
                for p in (2 * g, 2 * g + 1):
                    r = 32 * (p % 4)
                    for blk, part in enumerate((hi, hi, lo)):
                        sp.dma_start(kst[32 * blk:32 * blk + 32, p, :].bitcast(F32),
                                     part[r:r + 32, 2 + hg, :].bitcast(F32)
                                     ).then_inc(stacked[g], 16)
                    for e in range(2):
                        for blk, part in enumerate((hi, lo, hi)):
                            at = 32 * blk + 16 * e
                            sp.dma_start(qst[e][at:at + 16, p, :].bitcast(F32),
                                         part[r + 16 * e:r + 16 * e + 16, hg, :].bitcast(F32)
                                         ).then_inc(stacked[g], 16)

            def rows(b, g, _):
                row_read.wait(sp, b, g)
                for i in range(GH):
                    sp.dma_start(qst[i % 2][96:97, 2 * g + i // 2, :].bitcast(F32),
                                 mT[i:i + 1, g, :].bitcast(F32)).then_inc(row_in[g], 16)

            sp.wait_ge(zeroed, 5)
            run_attention(sp, cross, {"STACK": stack} | ({"LN": context_in} if cross else {"M": rows}))

        @block.gpsimd
        def _(pool):
            pool.memset(vaug[:, :, :, :], 0.0).then_inc(zeroed, 1)
            pool.wait_ge(zeroed, 1)
            pool.memset(vaug[:, :, :, HD:HD + 1], 0.0 if cross else 1.0).then_inc(zeroed, 1)
            for e in range(2):
                pool.memset(qst[e][:, :, :].bitcast(F32), 0.0).then_inc(zeroed, 1)
            pool.wait_ge(zeroed, 4)
            pool.memset(kst[96:97, :, :].bitcast(F32), 1.0).then_inc(zeroed, 1)
            pool.wait_ge(zeroed, 5)
            ln_rstd.begin(pool)
            if not cross:
                vaug_done.begin(pool)

            def ln(b, *_):
                ln_stats.wait(pool, b, 2 * NT - 1)
                xn_done.wait(pool, b - 1, NT - 1)
                pool.tensor_tensor(rstd[:, 0, :], mv[:, :, 1], const["eps"][:, :], ALU.add).then_inc(ln_rstd.sem, 1)
                ln_rstd.wait(pool, b, 0)
                pool.tensor_tensor(rstd[:, 1, :], rstd[:, 0, :], const["minus_half"][:, :], ALU.pow
                                   ).then_inc(ln_rstd.sem, 1)

            def v_group(b, g, _):
                m_act.wait(pool, b, 3)
                pv_done.wait(pool, b - 1, NT * g + NT - 1)
                src = v[:, bass.ds(b, 1), :, :]
                pool.tensor_copy(vaug[:, :, GH * g:GH * g + GH, 0:HD],
                                 src[:, :, :, GH * HD * g:GH * HD * (g + 1)].rearrange(
                                     "p o t (h d) -> p (o t) h d", d=HD)).then_inc(vaug_done.sem, 1)

            run_attention(pool, cross, {"LN": ln} | ({} if cross else {"STACK": v_group}))

        @block.vector
        def _(dve):
            for s in (ln_stats, xn_done, m_dve, lo_done, a_max, z_read, o_normed, x_added,
                      ) + ((kmax_done, kbias_done, rz_done, vaug_done) if cross else ()):
                s.begin(dve)
            dve.wait_ge(w_in, 5 * 16)
            if cross:
                dve.wait_ge(zeroed, 5)

            def ln(b, *_):
                ln_stats.wait(dve, b - 1, 2 * NT - 1)
                for t in range(NT):
                    dve.bn_stats(stats[:, t, :], x[:, bass.ds(b * NT + t, 1), :]).then_inc(ln_stats.sem, 1)
                ln_stats.wait(dve, b, NT - 1)
                ln_rstd.wait(dve, b - 1, 1)
                xn_done.wait(dve, b - 1, NT - 1)
                dve.memset(nothing[:, :], 0.0)
                for t in range(NT):
                    dve.bn_aggr(mv[:, t, :], stats[:, t, :]).then_inc(ln_stats.sem, 1)
                ln_stats.wait(dve, b, 2 * NT - 1)
                ln_rstd.wait(dve, b, 1)
                m_ready.wait(dve, b - 1, 1)
                for t in range(NT):
                    dve.tensor_scalar(xn[:, t, :], x[:, bass.ds(b * NT + t, 1), :], mv[:, t, 0:1],
                                      rstd[:, 1, t:t + 1], ALU.subtract, ALU.mult).then_inc(xn_done.sem, 1)

            def prep(b, use, _):
                if not 2 <= use < 6:
                    return
                i = use - 2
                m_ready.wait(dve, b, use)
                hi_done.wait(dve, b - 1, i)
                lo_done.wait(dve, b - 1, i)
                if causal:
                    ins = dve.scalar_tensor_tensor(qk[:, i, :], m_ps[:, :], bqk[:, i:i + 1], const["rope"][:, :],
                                                   ALU.add, ALU.mult)
                else:
                    ins = dve.tensor_scalar(qk[:, i, :], m_ps[:, :], bqk[:, i:i + 1], None, ALU.add)
                ins.then_inc(m_dve.sem, 1)
                hi_done.wait(dve, b, i)
                m_dve.wait(dve, b, i)
                if not (isinstance(b, int) and b == 0):
                    for g in (2 * (i % 2), 2 * (i % 2) + 1):
                        dve.wait_ge(stacked[g], b * 18 * 16)
                dve.tensor_tensor(lo[:, i, :], qk[:, i, :], hi[:, i, :].bitcast(F32), ALU.subtract
                                  ).then_inc(lo_done.sem, 1)

            def row_max(b, g, u):
                h, qt = u // NT, u % NT
                a_ready.wait(dve, b, 16 * g + u)
                if u == 0:
                    row_ready.wait(dve, b - 1, g)
                last = (qt + 1) * P if causal else T
                dve.tensor_reduce(mx[:, g, qt, h:h + 1], a_ps[:, u % 2, 0:last], AX.X, ALU.max
                                  ).then_inc(a_max.sem, 1)

            def norm(b, g, _):
                z_ready.wait(dve, b, g)
                o_normed.wait(dve, b, g - 1)
                dve.reciprocal(rz[:, :], o_ps[:, :]).then_inc(z_read.sem, 1)
                z_read.wait(dve, b, g)
                dve.tensor_tensor(o[:, g, :], o[:, g, :], rz[:, :], ALU.mult).then_inc(o_normed.sem, 1)

            def out(b, j, _):
                out_ready.wait(dve, b, j)
                xs = x[:, bass.ds(b * NT + 2 * j, 2), :]
                dve.tensor_tensor(xs, o_ps[:, :].rearrange("p (t n) -> p t n", n=D), xs, ALU.add
                                  ).then_inc(x_added.sem, 1)

            def key_max(b, g, j):
                n = 8 * g + j
                s_ready.wait(dve, b, n)
                kbias_done.wait(dve, b, n - 1)
                exp_done.wait(dve, b, n - 4)
                dve.tensor_reduce(kmax[:, n % 2, :], s_ps[:, n % 2, :, :], AX.X, ALU.max, negate=True
                                  ).then_inc(kmax_done.sem, 1)
                kmax_done.wait(dve, b, n)
                dve.tensor_scalar(kbias[:, n % 4, :], kmax[:, n % 2, :], SCALE, None, ALU.mult
                                  ).then_inc(kbias_done.sem, 1)

            def scale_v(b, g, kt):
                m_act.wait(dve, b, 3)
                for pp in range(2):
                    n, h = 8 * g + 2 * kt + pp, 4 * g + 2 * pp
                    exp_done.wait(dve, b, n)
                    vaug_done.wait(dve, b, n - 1)
                    dve.reciprocal(rzsum[:, n % 2, :], zsum[:, n % 4, :]).then_inc(rz_done.sem, 1)
                    rz_done.wait(dve, b, n)
                    pv_done.wait(dve, b - 1, NT * g + kt)
                    dve.tensor_tensor(vaug[:, kt, h:h + 2, 0:HD],
                                      v[:, bass.ds(b, 1), kt, HD * h:HD * (h + 2)].rearrange(
                                          "p o (h d) -> p (o h) d", d=HD),
                                      rzsum[:, n % 2, :].unsqueeze(2).to_broadcast([P, 2, HD]), ALU.mult
                                      ).then_inc(vaug_done.sem, 1)

            do = {"LN": ln, "PREP": prep, "OUT": out}
            if cross:
                do |= {"S": key_max, "PV": scale_v}
            else:
                do |= {"A": row_max, "N": norm}
            run_attention(dve, cross, do)

        @block.scalar
        def _(act):
            for s in (m_act, row_read, hi_done, exp_done, o_copied):
                s.begin(act)

            def prep(b, use, _):
                m_ready.wait(act, b, use) if not 2 <= use < 6 else None
                if use < 2:
                    act.activation(xnT[:, use, :], m_ps[:, :], ACT.Copy).then_inc(m_act.sem, 1)
                elif use < 6:
                    i = use - 2
                    m_dve.wait(act, b, i)
                    if not (isinstance(b, int) and b == 0):
                        for g in (2 * (i % 2), 2 * (i % 2) + 1):
                            act.wait_ge(stacked[g], b * 18 * 16)
                    lo_done.wait(act, b - 1, i)
                    act.activation(hi[:, i, :], qk[:, i, :], ACT.Copy).then_inc(hi_done.sem, 1)
                else:
                    t = 2 * (use - 6)
                    act.activation(v[:, bass.ds(b, 1), t:t + 2, :].rearrange("p o t n -> p (o t) n"),
                                   m_ps[:, :].rearrange("p (t n) -> p t n", n=D), ACT.Copy
                                   ).then_inc(m_act.sem, 1)

            def negate_rows(b, g, _):
                row_ready.wait(act, b, g)
                act.activation(mT[:, g, :], m_ps[0:GH, :], ACT.Copy, scale=-1.0).then_inc(row_read.sem, 1)

            def exps(b, g, j):
                n, c0 = 8 * g + j, first_col(j // 2)
                pv_done.wait(act, b, n // 2 - 2)
                if cross:
                    kbias_done.wait(act, b, n)
                    rz_done.wait(act, b, n - 4)
                    for e in range(2):
                        ins = act.activation(probs[:, n % 4, e, :], s_ps[:, n % 2, e, :], ACT.Exp,
                                             bias=kbias[:, n % 4, e:e + 1], scale=SCALE,
                                             accum_out=zsum[:, n % 4, e:e + 1])
                    ins.then_inc(exp_done.sem, 1)
                else:
                    s_ready.wait(act, b, n)
                    act.activation(probs[:, n % 4, :, c0:T], s_ps[:, n % 2, :, c0:T], ACT.Exp, scale=SCALE
                                   ).then_inc(exp_done.sem, 1)

            def copy_o(b, g, _):
                pv_done.wait(act, b, NT * g + NT - 1)
                out_ready.wait(act, b - 1, 1)
                act.activation(o[:, g, :], o_ps[:, :], ACT.Copy).then_inc(o_copied.sem, 1)

            run_attention(act, cross, {"PREP": prep, "S": exps, "O": copy_o}
                          | ({} if cross else {"M": negate_rows}))

        @block.tensor
        def _(pe):
            for s in (m_ready, row_ready, a_ready, s_ready, pv_done, z_ready, out_ready):
                s.begin(pe)
            pe.wait_ge(w_in, 5 * 16)
            pe.wait_ge(zeroed, 5)

            def prep_read(b, use):
                reader, step = reads_m(use)
                reader.wait(pe, b, step)

            def m_free(b, use):
                if use:
                    prep_read(b, use - 1)
                if use in (0, 4) and not cross:
                    row_read.wait(pe, b - 1, 1 if use == 0 else 2)

            def prep(b, use, _):
                m_free(b, use) if use else (row_read.wait(pe, b - 1, 1) if not cross else prep_read(b - 1, 7))
                if use < 2:
                    xn_done.wait(pe, b, NT - 1)
                    for t in range(NT):
                        ins = pe.transpose(m_ps[:, t * P:(t + 1) * P], xn[:, t, use * P:(use + 1) * P],
                                           const["ident"][:, :])
                elif use < 6:
                    i = use - 2
                    m_act.wait(pe, b, 1)
                    if cross and i == 2:
                        pe.wait_ge(ctx_in, (b + 1) * 16)
                    src = ctxT if cross and i >= 2 else xnT
                    for c in range(CC):
                        ins = pe.matmul(m_ps[:, :], wqkv[:, c, i * P:(i + 1) * P], src[:, c, :],
                                        start=c == 0, stop=c == CC - 1)
                else:
                    src = ctxT if cross else xnT
                    for t in (2 * (use - 6), 2 * (use - 6) + 1):
                        at = m_ps[:, (t % 2) * D:(t % 2 + 1) * D]
                        pe.matmul(at, const["ones"][0:1, 0:P], bv[:, :], start=True, stop=False)
                        for c in range(CC):
                            ins = pe.matmul(at, src[:, c, t * P:(t + 1) * P], wqkv[:, c, 2 * D:3 * D],
                                            start=False, stop=c == CC - 1)
                ins.then_inc(m_ready.sem, 1)

            def scores_by_query(b, g, u):
                h, qt = GH * g + u // NT, u % NT
                if u == 0:
                    pe.wait_ge(stacked[g], (b + 1) * 18 * 16)
                a_max.wait(pe, b, 16 * g + u - 2)
                last = (qt + 1) * P if causal else T
                at = a_ps[:, u % 2, 0:last]
                ins = pe.matmul(at, qst[h % 2][0:96, h // 2, qt * P:(qt + 1) * P], kst[0:96, h // 2, 0:last],
                                start=True, stop=not causal)
                if causal:
                    ins = pe.matmul(at[:, qt * P:last], const["ident_b"][:, :], const["mask_q"][:, :],
                                    start=False, stop=True)
                ins.then_inc(a_ready.sem, 1)

            def max_rows(b, g, _):
                a_max.wait(pe, b, 16 * g + 15)
                row_read.wait(pe, b, g - 1)
                if g == 0:
                    prep_read(b, 7)
                elif g >= 2 and not (isinstance(b, int) and b == B - 1):
                    prep_read(b + 1, 4 * g - 5)
                for qt in range(NT):
                    ins = pe.transpose(m_ps[0:GH, qt * P:(qt + 1) * P], mx[:, g, qt, :], const["ident"][:, :])
                ins.then_inc(row_ready.sem, 1)

            def scores_by_key(b, g, j):
                n, kt, p = 8 * g + j, j // 2, 2 * g + j % 2
                if j == 0:
                    pe.wait_ge(*((stacked[g], (b + 1) * 18 * 16) if cross else (row_in[g], (b + 1) * 4 * 16)))
                exp_done.wait(pe, b, n - 2)
                c0, rows = first_col(kt), 96 if cross else 97
                for e in range(2):
                    at = s_ps[:, n % 2, e, c0:T]
                    ins = pe.matmul(at, kst[0:rows, p, kt * P:(kt + 1) * P], qst[e][0:rows, p, c0:T],
                                    start=True, stop=not causal)
                    if causal:
                        ins = pe.matmul(at[:, 0:P], const["ident_b"][:, :], const["mask_k"][:, :],
                                        start=False, stop=True)
                ins.then_inc(s_ready.sem, 1)

            def probs_v(b, g, kt):
                exp_done.wait(pe, b, 8 * g + 2 * kt + 1)
                if cross:
                    vaug_done.wait(pe, b, 8 * g + 2 * kt + 1)
                else:
                    vaug_done.wait(pe, b, g)
                if kt == 0:
                    if g == 0:
                        x_added.wait(pe, b - 1, 1)
                    else:
                        (o_copied if cross else z_read).wait(pe, b, g - 1)
                c0 = first_col(kt)
                for i in range(GH):
                    ins = pe.matmul(o_ps[32 * i:32 * i + 32, c0:T], vaug[:, kt, GH * g + i, :],
                                    probs[:, (2 * kt + i // 2) % 4, i % 2, c0:T],
                                    start=kt == 0, stop=kt == NT - 1)
                ins.then_inc(pv_done.sem, 1)

            def sums(b, g, _):
                o_copied.wait(pe, b, g)
                pe.matmul(o_ps[:, :], const["spread"][:, :], o[:, g, :], start=True, stop=True
                          ).then_inc(z_ready.sem, 1)

            def project(b, j, _):
                if j == 0:
                    (o_copied if cross else o_normed).wait(pe, b, NG - 1)
                else:
                    x_added.wait(pe, b, 0)
                for t in (2 * j, 2 * j + 1):
                    at = o_ps[:, (t % 2) * D:(t % 2 + 1) * D]
                    pe.matmul(at, const["ones"][0:1, 0:P], bo[:, :], start=True, stop=False)
                    for g in range(NG):
                        ins = pe.matmul(at, o[:, g, t * P:(t + 1) * P], wout[:, g, :],
                                        start=False, stop=g == NG - 1)
                ins.then_inc(out_ready.sem, 1)

            do = {"PREP": prep, "S": scores_by_key, "PV": probs_v, "OUT": project}
            if not cross:
                do |= {"A": scores_by_query, "M": max_rows, "N": sums}
            run_attention(pe, cross, do)


def load_constants(nc, ctx, x, inputs):
    const = {}

    def sb(name, shape, dt=F32):
        const[name] = ctx.enter_context(nc.sbuf_tensor(f"const_{name}", shape, dt))
        return const[name]

    ident, spread, rope, ones = sb("ident", [P, P]), sb("spread", [P, P]), sb("rope", [P, T]), sb("ones", [P, P])
    minus_half, eps = sb("minus_half", [P, NT]), sb("eps", [P, NT])
    masks = sb("masks", [P, 2, P])
    iota = sb("iota", [P, 32])
    before = sb("before", [P, P])
    zeros = sb("zeros", [P, D])
    for name in ("rows", "outs"):
        const[name + "_dram"] = nc.dram_tensor(name + "_dram", (NBLK * BLK, D), F32, kind="Internal").ap()
    ident_b, mask_q, mask_k = (sb(n, [P, P], BF16) for n in ("ident_b", "mask_q", "mask_k"))
    const["rows_zeroed"] = ctx.enter_context(nc.semaphore("rows_zeroed"))
    loaded = ctx.enter_context(nc.semaphore("const_loaded"))
    made = ctx.enter_context(nc.semaphore("const_made"))
    with nc.Block() as block:
        @block.sync
        def _(sp):
            sp.dma_start(x[:, :, :], inputs["x"].rearrange("b (t p) d -> p (b t) d", p=P)).then_inc(loaded, 16)
            sp.dma_start(ident[:, :], inputs["ident"]).then_inc(loaded, 16)
            sp.dma_start(spread[:, :], inputs["spread"]).then_inc(loaded, 16)
            sp.dma_start(rope[:, :], inputs["rope"]).then_inc(loaded, 16)
            sp.dma_start(masks[:, :, :], inputs["masks"]).then_inc(loaded, 16)
            sp.dma_start(iota[:, :], inputs["iota"]).then_inc(loaded, 16)
            sp.dma_start(before[:, :], inputs["before"]).then_inc(loaded, 16)
            sp.wait_ge(made, 1)
            sp.dma_start(const["rows_dram"].rearrange("(n p) d -> p n d", p=P),
                         zeros[:, :].unsqueeze(1).to_broadcast([P, NBLK * BLK // P, D])
                         ).then_inc(const["rows_zeroed"], 16)

        @block.vector
        def _(dve):
            dve.memset(zeros[:, :], 0.0).then_inc(made, 1)
            dve.memset(ones[:, :], 1.0).then_inc(made, 1)
            dve.memset(minus_half[:, :], -0.5).then_inc(made, 1)
            dve.memset(eps[:, :], EPS).then_inc(made, 1)
            dve.wait_ge(loaded, 7 * 16)
            dve.tensor_copy(ident_b[:, :], ident[:, :]).then_inc(made, 1)
            dve.tensor_copy(mask_q[:, :], masks[:, 0, :]).then_inc(made, 1)
            dve.tensor_copy(mask_k[:, :], masks[:, 1, :]).then_inc(made, 1)
            dve.wait_ge(made, 7)
    return const


def geglu(nc, tag, x, const, w):
    with ExitStack() as ctx:
        def sb(name, shape, dt=F32):
            return ctx.enter_context(nc.sbuf_tensor(f"{tag}_sb_{name}", shape, dt))

        def ps(name, shape, dt=F32):
            return ctx.enter_context(nc.psum_tensor(f"{tag}_{name}", shape, dt))

        def steps(name, per):
            return Steps(ctx.enter_context(nc.semaphore(f"{tag}_{name}")), per)

        FC = T // P
        stats = sb("stats", [P, NT, 6])
        mv = sb("mv", [P, NT, 2])
        rstd = sb("rstd", [P, 2, NT])
        xn = sb("xn", [P, NT, D])
        xnT = sb("xnT", [P, CC, T])
        ctxT = sb("ctxT", [P, CC, T])
        ctxN = sb("ctxN", [P, FC, D])
        gelu = sb("gelu", [P, FC, T])
        h = sb("h", [P, FC, T])
        nothing = sb("nothing", [P, 1])

        t_ps = ps("t_ps", [P, CC, T])
        g_ps = ps("g_ps", [P, FC, T])
        y_ps = ps("y_ps", [P, 2, 2, D])

        ctxT_in = ctx.enter_context(nc.semaphore(f"{tag}_ctxT_in"))
        ctxN_in = ctx.enter_context(nc.semaphore(f"{tag}_ctxN_in"))
        ln_stats = steps("ln_stats", 2 * NT)
        ln_rstd = steps("ln_rstd", 2)
        xn_done = steps("xn_done", NT)
        t_ready = steps("t_ready", CC)
        t_read = steps("t_read", CC)
        g_ready = steps("g_ready", FC)
        g_gelu = steps("g_gelu", FC)
        h_done = steps("h_done", FC)
        y_ready = steps("y_ready", 2)
        x_added = steps("x_added", 2)

        block = ctx.enter_context(nc.Block())

        def run(eng, do):
            do.get("LN", lambda b: None)(0)

            def body(b, nxt):
                for kind in ("IN", "T", "G"):
                    do.get(kind, lambda b: None)(b)
                if nxt is not None:
                    do.get("LN", lambda b: None)(nxt)
                do.get("Y", lambda b: None)(b)
            batch_body(eng, B, body)

        @block.sync
        def _(sp):
            def context_in(b):
                wait_all(sp, (g_ready, b - 1, FC - 1), (y_ready, b - 1, 1))
                sp.dma_start(ctxT[:, :, :], w["ctxT"][bass.ds(b, 1)].rearrange("o (c p) t -> p (o c) t", p=P)
                             ).then_inc(ctxT_in, 16)
                sp.dma_start(ctxN[:, :, :], w["ctx"][bass.ds(b, 1)].rearrange("o (c p) d -> p (o c) d", p=P)
                             ).then_inc(ctxN_in, 16)
            run(sp, {"IN": context_in})

        @block.gpsimd
        def _(pool):
            ln_rstd.begin(pool)
            run(pool, {"LN": lambda b: inverse_deviation(pool, b, mv, rstd, const, ln_stats, ln_rstd, xn_done)})

        @block.vector
        def _(dve):
            for s in (ln_stats, xn_done, h_done, x_added):
                s.begin(dve)

            def gate(b):
                for f in range(FC):
                    g_gelu.wait(dve, b, f)
                    y_ready.wait(dve, b - 1, 1)
                    dve.tensor_tensor(h[:, f, :], g_ps[:, f, :], gelu[:, f, :], ALU.mult).then_inc(h_done.sem, 1)

            def add(b):
                for j in range(2):
                    y_ready.wait(dve, b, j)
                    xs = x[:, bass.ds(b * NT + 2 * j, 2), :]
                    dve.tensor_tensor(xs, y_ps[:, j, :, :], xs, ALU.add).then_inc(x_added.sem, 1)

            run(dve, {"LN": lambda b: normalise(dve, b, x, stats, mv, rstd, xn, nothing, ln_stats, ln_rstd,
                                                xn_done, t_ready, CC - 1),
                      "G": gate, "Y": add})

        @block.scalar
        def _(act):
            for s in (t_read, g_gelu):
                s.begin(act)

            def transposed(b):
                for c in range(CC):
                    t_ready.wait(act, b, c)
                    g_ready.wait(act, b - 1, FC - 1)
                    act.activation(xnT[:, c, :], t_ps[:, c, :], ACT.Copy).then_inc(t_read.sem, 1)

            def gate(b):
                for f in range(FC):
                    g_ready.wait(act, b, f)
                    h_done.wait(act, b - 1, f)
                    act.activation(gelu[:, f, :], g_ps[:, f, :], ACT.Gelu_apprx_tanh).then_inc(g_gelu.sem, 1)

            run(act, {"T": transposed, "G": gate})

        @block.tensor
        def _(pe):
            for s in (t_ready, g_ready, y_ready):
                s.begin(pe)

            def transpose(b):
                xn_done.wait(pe, b, NT - 1)
                for c in range(CC):
                    t_read.wait(pe, b - 1, c)
                    for t in range(NT):
                        ins = pe.transpose(t_ps[:, c, t * P:(t + 1) * P], xn[:, t, c * P:(c + 1) * P],
                                           const["ident"][:, :])
                    ins.then_inc(t_ready.sem, 1)

            def hidden(b):
                pe.wait_ge(ctxT_in, (b + 1) * 16)
                t_read.wait(pe, b, CC - 1)
                for f in range(FC):
                    h_done.wait(pe, b - 1, f)
                    for c in range(CC):
                        ins = pe.matmul(g_ps[:, f, :], ctxT[:, c, f * P:(f + 1) * P], xnT[:, c, :],
                                        start=c == 0, stop=c == CC - 1)
                    ins.then_inc(g_ready.sem, 1)

            def output(b):
                pe.wait_ge(ctxN_in, (b + 1) * 16)
                h_done.wait(pe, b, FC - 1)
                for j in range(2):
                    x_added.wait(pe, b - 1, j)
                    for t in range(2):
                        for f in range(FC):
                            ins = pe.matmul(y_ps[:, j, t, :], h[:, f, (2 * j + t) * P:(2 * j + t + 1) * P],
                                            ctxN[:, f, :], start=f == 0, stop=f == FC - 1)
                    ins.then_inc(y_ready.sem, 1)

            run(pe, {"T": transpose, "G": hidden, "Y": output})


def inverse_deviation(pool, b, mv, rstd, const, ln_stats, ln_rstd, xn_done):
    ln_stats.wait(pool, b, 2 * NT - 1)
    xn_done.wait(pool, b - 1, NT - 1)
    pool.tensor_tensor(rstd[:, 0, :], mv[:, :, 1], const["eps"][:, :], ALU.add).then_inc(ln_rstd.sem, 1)
    ln_rstd.wait(pool, b, 0)
    pool.tensor_tensor(rstd[:, 1, :], rstd[:, 0, :], const["minus_half"][:, :], ALU.pow).then_inc(ln_rstd.sem, 1)


def normalise(dve, b, x, stats, mv, rstd, xn, nothing, ln_stats, ln_rstd, xn_done, xn_read, last_read):
    ln_stats.wait(dve, b - 1, 2 * NT - 1)
    for t in range(NT):
        dve.bn_stats(stats[:, t, :], x[:, bass.ds(b * NT + t, 1), :]).then_inc(ln_stats.sem, 1)
    ln_stats.wait(dve, b, NT - 1)
    ln_rstd.wait(dve, b - 1, 1)
    xn_done.wait(dve, b - 1, NT - 1)
    dve.memset(nothing[:, :], 0.0)
    for t in range(NT):
        dve.bn_aggr(mv[:, t, :], stats[:, t, :]).then_inc(ln_stats.sem, 1)
    ln_stats.wait(dve, b, 2 * NT - 1)
    ln_rstd.wait(dve, b, 1)
    if xn_read is not None:
        xn_read.wait(dve, b - 1, last_read)
    for t in range(NT):
        dve.tensor_scalar(xn[:, t, :], x[:, bass.ds(b * NT + t, 1), :], mv[:, t, 0:1],
                          rstd[:, 1, t:t + 1], ALU.subtract, ALU.mult).then_inc(xn_done.sem, 1)


E, TOP = 8, 2
BLK = 256
NTILE = B * NT
GATHER = 4
NBLK = (B * T * TOP - E) // BLK + E


def moe(nc, tag, x, const, w, width, phi, shared):
    FC = width // P
    with ExitStack() as ctx:
        def sb(name, shape, dt=F32):
            return ctx.enter_context(nc.sbuf_tensor(f"{tag}_sb_{name}", shape, dt))

        def sem(name):
            return ctx.enter_context(nc.semaphore(f"{tag}_{name}"))

        xn = sb("xn", [P, B, NT, D])
        xnT = sb("xnT", [P, CC, B * T])
        weight = [sb(f"weight{k}", [P, NTILE]) for k in range(TOP)]
        place = [sb(f"place{k}", [P, NTILE], U32) for k in range(TOP)]
        block_expert = sb("block_expert", [P, NBLK], I32)
        w1 = sb("w1", [P, 2, CC, width])
        w3 = sb("w3", [P, 2, CC, width])
        w2 = sb("w2", [P, 2, FC, D])
        w13_in = [sem(f"w13_in{k}") for k in range(2)]
        w2_in = [sem(f"w2_in{k}") for k in range(2)]
        scattered = sem("scattered")

        def load_w13(sp, k, e):
            for to, name in ((w1, "w1"), (w3, "w3")):
                sp.dma_start(to[:, k, :, :], w[name][bass.ds(e, 1)].rearrange("o (c p) f -> p (o c) f", p=P)
                             ).then_inc(w13_in[k], 16)

        def load_w2(sp, k, e):
            sp.dma_start(w2[:, k, :, :], w["w2"][bass.ds(e, 1)].rearrange("o (c p) d -> p (o c) d", p=P)
                         ).then_inc(w2_in[k], 16)

        buffers = (w1, w3, w2, w13_in, w2_in)
        routing(nc, tag, x, const, w, phi, shared, xn, xnT, weight, place, block_expert, load_w13, load_w2)
        if shared:
            experts(nc, tag + "s", x, const, FC, xnT, buffers, scatter=(xn, place, scattered))
        experts(nc, tag, x, const, FC, None, buffers, scatter=(xn, place, scattered),
                routed=(weight, block_expert, load_w13, load_w2, 1 if shared else 0))


def routing(nc, tag, x, const, w, phi, shared, xn, xnT, weight, place, block_expert, load_w13, load_w2):
    with ExitStack() as ctx:
        def sb(name, shape, dt=F32):
            return ctx.enter_context(nc.sbuf_tensor(f"{tag}_sb_{name}", shape, dt))

        def ps(name, shape):
            return ctx.enter_context(nc.psum_tensor(f"{tag}_{name}", shape, F32))

        def sem(name):
            return ctx.enter_context(nc.semaphore(f"{tag}_{name}"))

        stats = sb("stats", [P, NT, 6])
        mv = sb("mv", [P, NT, 2])
        rstd = sb("rstd", [P, 2, NT])
        nothing = sb("nothing", [P, 1])
        router = sb("router", [P, CC, E])
        rbias = sb("rbias", [1, E])
        r = {n: sb(n, [P, NTILE, E]) for n in ("lg", "eq", "cand", "oh0", "oh1", "both", "l2", "ab", "df", "keep",
                                               "row", "mine")}
        c1 = {n: sb(n, [P, NTILE]) for n in ("m1", "m2", "first", "ex", "den", "at")}
        c8 = {n: sb(n, [P, E]) for n in ("count", "used", "start", "end")}
        c88 = {n: sb(n, [P, E, E]) for n in ("fills", "before")}
        ends = sb("ends", [P, NBLK, E])
        expert_f = sb("expert_f", [P, NBLK])

        t_ps = ps("t_ps", [P, CC, T])
        l_ps = ps("l_ps", [P, NTILE, E])
        rank_ps = ps("rank_ps", [P, NTILE, E])
        count_ps = ps("count_ps", [P, E])

        ln_stats = Steps(sem("ln_stats"), 2 * NT)
        ln_rstd = Steps(sem("ln_rstd"), 2)
        xn_done = Steps(sem("xn_done"), NT)
        t_ready = Steps(sem("t_ready"), CC)
        t_read = Steps(sem("t_read"), CC)
        router_in = sem("router_in")
        logits_ready = sem("logits_ready")
        routed = sem("routed")
        route_exp = sem("route_exp")
        chosen = sem("chosen")
        ranked = sem("ranked")
        block = ctx.enter_context(nc.Block())

        @block.sync
        def _(sp):
            sp.dma_start(router[:, :, :], w["router"].rearrange("(c p) e -> p c e", p=P)).then_inc(router_in, 16)
            sp.dma_start(rbias[:, :], w["router_bias"]).then_inc(router_in, 16)
            if shared:
                load_w13(sp, 0, E)
                load_w2(sp, 0, E)

        @block.gpsimd
        def _(pool):
            ln_rstd.begin(pool)
            for b in range(B):
                inverse_deviation(pool, b, mv, rstd, const, ln_stats, ln_rstd, xn_done)

        @block.scalar
        def _(act):
            t_read.begin(act)
            for b in range(B):
                for c in range(CC):
                    t_ready.wait(act, b, c)
                    act.activation(xnT[:, c, b * T:(b + 1) * T], t_ps[:, c, :], ACT.Copy).then_inc(t_read.sem, 1)
            if phi:
                for k, name in enumerate(("df", "l2")):
                    act.wait_ge(routed, PHI_EXP[k])
                    act.activation(r[name][:, :, :], r[name][:, :, :], ACT.Exp).then_inc(route_exp, 1)
            else:
                act.wait_ge(routed, TOP2_EXP)
                act.activation(c1["ex"][:, :], c1["ex"][:, :], ACT.Exp).then_inc(route_exp, 1)

        @block.tensor
        def _(pe):
            t_ready.begin(pe)
            pe.wait_ge(router_in, 32)
            for b in range(B):
                xn_done.wait(pe, b, NT - 1)
                for c in range(CC):
                    t_read.wait(pe, b - 1, c)
                    for t in range(NT):
                        ins = pe.transpose(t_ps[:, c, t * P:(t + 1) * P], xn[:, b, t, c * P:(c + 1) * P],
                                           const["ident"][:, :])
                    ins.then_inc(t_ready.sem, 1)
            t_read.wait(pe, B - 1, CC - 1)
            for tile in range(NTILE):
                at = l_ps[:, tile, :]
                pe.matmul(at, const["ones"][0:1, 0:P], rbias[:, :], start=True, stop=False)
                for c in range(CC):
                    ins = pe.matmul(at, xnT[:, c, tile * P:(tile + 1) * P], router[:, c, :],
                                    start=False, stop=c == CC - 1)
            ins.then_inc(logits_ready, 1)
            pe.wait_ge(chosen, 1)
            both = r["both"]
            pe.matmul(rank_ps[:, :, :], const["before"][:, :], both[:, :, :], start=True, stop=False)
            for back in range(1, NTILE):
                pe.matmul(rank_ps[:, back:NTILE, :], const["ones"][:, :], both[:, 0:NTILE - back, :],
                          start=False, stop=back == NTILE - 1)
            for tile in range(NTILE):
                ins = pe.matmul(count_ps[:, :], const["ones"][:, :], both[:, tile, :],
                                start=tile == 0, stop=tile == NTILE - 1)
            ins.then_inc(ranked, 1)

        @block.vector
        def _(dve):
            for s in (ln_stats, xn_done):
                s.begin(dve)
            for b in range(B):
                normalise(dve, b, x, stats, mv, rstd, xn[:, b, :, :], nothing, ln_stats, ln_rstd, xn_done,
                          None, None)
            dve.wait_ge(logits_ready, 1)
            step = [0]

            def then(ins):
                step[0] += 1
                ins.then_inc(routed, 1)
                dve.wait_ge(routed, step[0])

            top_two(dve, then, step, const, l_ps, r, c1, weight, phi, route_exp, chosen)
            dve.wait_ge(ranked, 1)
            placement(dve, then, const, rank_ps, count_ps, r, c1, c8, c88, ends, expert_f, place, block_expert)


PHI_EXP = (12, 29)
TOP2_EXP = 14


def over_experts(t):
    return t[:, :].unsqueeze(2).to_broadcast([P, NTILE, E])


def top_two(dve, then, step, const, l_ps, r, c1, weight, phi, route_exp, chosen):
    def full(t):
        return t[:, :, :]

    wide = over_experts
    iota = const["iota"][:, 0:E].unsqueeze(1).to_broadcast([P, NTILE, E])
    lg, eq, cand, oh0, oh1, l2 = (r[n] for n in ("lg", "eq", "cand", "oh0", "oh1", "l2"))
    then(dve.tensor_copy(full(lg), l_ps[:, :, :]))

    def top(src, m, oh):
        then(dve.tensor_reduce(c1[m][:, :], full(src), AX.X, ALU.max))
        then(dve.tensor_tensor(full(eq), full(src), wide(c1[m]), ALU.not_equal))
        then(dve.scalar_tensor_tensor(full(cand), full(eq), float(E), iota, ALU.mult, ALU.add))
        then(dve.tensor_reduce(c1["first"][:, :], full(cand), AX.X, ALU.min))
        then(dve.tensor_tensor(full(oh), wide(c1["first"]), iota, ALU.is_equal))

    def unmasked_sum(m, ex, drop, out, nexp):
        ab, keep = r["ab"], r["keep"]
        then(dve.scalar_tensor_tensor(full(ab), full(lg), -1.0, full(lg), ALU.mult, ALU.max))
        then(dve.tensor_tensor(full(ab), full(ab), wide(c1[m]), ALU.max))
        then(dve.tensor_tensor(full(keep), wide(c1[m]), full(lg), ALU.subtract))
        then(dve.scalar_tensor_tensor(full(keep), full(ab), 0.02, full(keep), ALU.mult, ALU.is_ge))
        if drop is not None:
            then(dve.scalar_tensor_tensor(full(keep), full(drop), 0.0, full(keep), ALU.is_equal, ALU.mult))
        then(dve.tensor_tensor(full(ex), full(lg), wide(c1[m]), ALU.subtract))
        then(dve.tensor_scalar(full(ex), full(ex), 0.0, None, ALU.min))
        assert step[0] == PHI_EXP[nexp - 1], step[0]
        dve.wait_ge(route_exp, nexp)
        then(dve.tensor_tensor(full(ex), full(ex), full(keep), ALU.mult))
        then(dve.tensor_reduce(c1["den"][:, :], full(ex), AX.X, ALU.add))
        then(dve.reciprocal(out[:, :], c1["den"][:, :]))

    top(lg, "m1", oh0)
    if phi:
        unmasked_sum("m1", r["df"], None, weight[0], 1)
    then(dve.scalar_tensor_tensor(full(l2), full(oh0), -3e38, full(lg), ALU.mult, ALU.add))
    top(l2, "m2", oh1)
    then(dve.tensor_tensor(full(r["both"]), full(oh0), full(oh1), ALU.add))
    dve.sem_inc(chosen, 1)
    if phi:
        unmasked_sum("m2", l2, oh0, weight[1], 2)
    else:
        then(dve.tensor_tensor(c1["ex"][:, :], c1["m2"][:, :], c1["m1"][:, :], ALU.subtract))
        assert step[0] == TOP2_EXP
        dve.wait_ge(route_exp, 1)
        then(dve.tensor_scalar(c1["den"][:, :], c1["ex"][:, :], 1.0, None, ALU.add))
        then(dve.reciprocal(weight[0][:, :], c1["den"][:, :]))
        then(dve.tensor_tensor(weight[1][:, :], c1["ex"][:, :], weight[0][:, :], ALU.mult))


def placement(dve, then, const, rank_ps, count_ps, r, c1, c8, c88, ends, expert_f, place, block_expert):
    iota = const["iota"]
    fills, before = c88["fills"], c88["before"]
    along = iota[:, 0:E].unsqueeze(1).to_broadcast([P, E, E])
    down = iota[:, 0:E].unsqueeze(2).to_broadcast([P, E, E])
    then(dve.tensor_copy(c8["count"][:, :], count_ps[:, :]))
    then(dve.scalar_tensor_tensor(fills[:, :, :], along, float(BLK),
                                  c8["count"][:, :].unsqueeze(2).to_broadcast([P, E, E]), ALU.mult, ALU.is_lt))
    then(dve.tensor_reduce(c8["used"][:, :], fills[:, :, :], AX.X, ALU.add))
    then(dve.tensor_tensor(before[:, :, :], along, down, ALU.is_lt))
    then(dve.tensor_tensor(before[:, :, :], before[:, :, :],
                           c8["used"][:, :].unsqueeze(1).to_broadcast([P, E, E]), ALU.mult))
    then(dve.tensor_reduce(c8["start"][:, :], before[:, :, :], AX.X, ALU.add))
    then(dve.tensor_tensor(c8["end"][:, :], c8["start"][:, :], c8["used"][:, :], ALU.add))
    then(dve.scalar_tensor_tensor(r["row"][:, :, :], c8["start"][:, :].unsqueeze(1).to_broadcast([P, NTILE, E]),
                                  float(BLK), rank_ps[:, :, :], ALU.mult, ALU.add))
    for k in range(TOP):
        then(dve.tensor_tensor(r["mine"][:, :, :], r["row"][:, :, :], r[f"oh{k}"][:, :, :], ALU.mult))
        then(dve.tensor_reduce(c1["at"][:, :], r["mine"][:, :, :], AX.X, ALU.add))
        then(dve.tensor_copy(place[k][:, :], c1["at"][:, :]))
    then(dve.tensor_tensor(ends[:, :, :], c8["end"][:, :].unsqueeze(1).to_broadcast([P, NBLK, E]),
                           iota[:, 0:NBLK].unsqueeze(2).to_broadcast([P, NBLK, E]), ALU.is_le))
    then(dve.tensor_reduce(expert_f[:, :], ends[:, :, :], AX.X, ALU.add))
    then(dve.tensor_scalar(expert_f[:, :], expert_f[:, :], float(E - 1), None, ALU.min))
    then(dve.tensor_copy(block_expert[:, :], expert_f[:, :]))


def run_blocks(eng, nblk, nf, do):
    def step(kind, i, k, f=0):
        if kind in do:
            do[kind](i, k, f)

    def body(i, k, last):
        for f in range(1, nf):
            if f == nf - 1 and not last:
                step("T", i, k + 1)
            step("G", i, k, f)
        if not last:
            step("G", i, k + 1, 0)
        step("Y", i, k)

    step("T", 0, 0)
    step("G", 0, 0, 0)
    turns = (nblk - 1) // 2
    with eng.Fori(0, turns) as i:
        body(i, 0, False)
        body(i, 1, False)
    for n in range(2 * turns, nblk):
        body(turns, n - 2 * turns, n == nblk - 1)


def experts(nc, tag, x, const, FC, xnT, buffers, scatter, routed=None):
    NF = FC // 2
    nblk = NBLK if routed else B * T // BLK
    w1, w3, w2, w13_in, w2_in = buffers
    xn, place, scattered = scatter
    scatter_here = not routed or not routed[4]
    with ExitStack() as ctx:
        def sb(name, shape, dt=F32):
            return ctx.enter_context(nc.sbuf_tensor(f"{tag}_sb_x{name}", shape, dt))

        def ps(name, shape):
            return ctx.enter_context(nc.psum_tensor(f"{tag}_x{name}", shape, F32))

        def sem(name):
            return ctx.enter_context(nc.semaphore(f"{tag}_x{name}"))

        silu = sb("silu", [P, 2, 2 * BLK])
        h = sb("h", [P, 2, FC, BLK])
        if routed:
            rows = sb("rows", [P, 2, BLK // P, D])
            rowsT = sb("rowsT", [P, 2, CC, BLK])
            y = sb("y", [P, 2, BLK // P, D])
            back = sb("back", [P, TOP, NTILE, D])
            t_ps = ps("t_ps", [P, 2, CC, BLK])
        g_ps = ps("g_ps", [P, 2, 2, 2 * BLK])
        y_ps = ps("y_ps", [P, 2, BLK // P, D])

        if routed:
            rows_in = [sem(f"rows_in{k}") for k in range(2)]
            stored = [sem(f"stored{k}") for k in range(2)]
            gathered = [sem(f"gathered{n}") for n in range(NTILE // GATHER)]
            added = sem("added")
            t_ready = Steps(sem("t_ready"), 2)
            t_read = Steps(sem("t_read"), 2)
        g_ready = Steps(sem("g_ready"), 2 * NF)
        g_silu = Steps(sem("g_silu"), 2 * NF)
        h_done = Steps(sem("h_done"), 2 * NF)
        y_ready = Steps(sem("y_ready"), 2)
        y_read = Steps(sem("y_read"), 2)
        block = ctx.enter_context(nc.Block())

        @block.sync
        def _(sp):
            if not routed:
                return
            _, block_expert, load_w13, load_w2, _ = routed

            def expert(i, k):
                return sp.value_load(block_expert[0:1, bass.ds(i * 2 + k, 1)], min_val=0, max_val=E - 1)

            def load_rows(i, k):
                sp.dma_start(rows[:, k % 2, :, :], const["rows_dram"][bass.ds((i * 2 + k) * BLK, BLK), :].rearrange(
                    "(t p) d -> p t d", p=P)).then_inc(rows_in[k % 2], 16)

            def ahead(i, k, more_rows=True, more_weights=True):
                if more_rows:
                    wait_all(sp, (t_ready, i, k + 1))
                    load_rows(i, k + 3)
                if more_weights:
                    e = expert(i, k + 2)
                    wait_all(sp, (g_ready, i, k * NF + NF - 1))
                    load_w13(sp, k % 2, e)
                    wait_all(sp, (y_ready, i, k))
                    load_w2(sp, k % 2, e)
                wait_all(sp, (y_read, i, k))
                sp.dma_start(const["outs_dram"][bass.ds((i * 2 + k) * BLK, BLK), :].rearrange("(t p) d -> p t d", p=P),
                             y[:, k % 2, :, :]).then_inc(stored[k % 2], 16)

            for k in range(2):
                e = expert(0, k)
                load_w13(sp, k, e)
                load_w2(sp, k, e)
            for k in range(2):
                sp.sem_inc(stored[k], 16)
            sp.wait_ge(scattered, TOP * NTILE * 16)
            load_rows(0, 0)
            load_rows(0, 1)
            t_ready.wait(sp, 0, 0)
            load_rows(0, 2)
            with sp.Fori(0, (nblk - 3) // 2) as i:
                ahead(i, 0)
                ahead(i, 1)
            for n in range(nblk - 3, nblk):
                ahead((nblk - 3) // 2, n - (nblk - 3), False, n == nblk - 3)

        @block.gpsimd
        def _(pool):
            if scatter_here:
                pool.wait_ge(const["rows_zeroed"], 16)
                for tile in range(NTILE):
                    for k in range(TOP):
                        pool.indirect_dma_start(const["rows_dram"], bass.IndirectOffsetOnAxis(
                            ap=place[k][:, tile:tile + 1], axis=0), xn[:, tile // NT, tile % NT, :], None
                            ).then_inc(scattered, 16)
            if routed:
                for k in range(2):
                    pool.wait_ge(stored[k], ((nblk + 1 - k) // 2 + 1) * 16)
                for tile in range(NTILE):
                    for k in range(TOP):
                        pool.indirect_dma_start(back[:, k, tile, :], None, const["outs_dram"],
                                                bass.IndirectOffsetOnAxis(ap=place[k][:, tile:tile + 1], axis=0)
                                                ).then_inc(gathered[tile // GATHER], 16)

        @block.scalar
        def _(act):
            for s in (g_silu,) + ((t_read,) if routed else ()):
                s.begin(act)

            def transposed(i, k, _):
                t_ready.wait(act, i, k)
                g_ready.wait(act, i, (k - 1) * NF - 1)
                act.activation(rowsT[:, k % 2, :, :], t_ps[:, k % 2, :, :], ACT.Copy).then_inc(t_read.sem, 1)

            def gate(i, k, f):
                m = k * NF + f
                g_ready.wait(act, i, m)
                h_done.wait(act, i, m - 2)
                act.activation(silu[:, f % 2, :], g_ps[:, f % 2, 0, :], ACT.Silu).then_inc(g_silu.sem, 1)
            run_blocks(act, nblk, NF, {"G": gate} | ({"T": transposed} if routed else {}))

        @block.vector
        def _(dve):
            for s in (h_done, y_read):
                s.begin(dve)

            def hidden(i, k, f):
                m = k * NF + f
                g_silu.wait(dve, i, m)
                y_ready.wait(dve, i, k - 2)
                dve.tensor_tensor(h[:, k % 2, 2 * f:2 * f + 2, :].rearrange("p c n -> p (c n)"), g_ps[:, f % 2, 1, :],
                                  silu[:, f % 2, :], ALU.mult).then_inc(h_done.sem, 1)

            def output(i, k, _):
                y_ready.wait(dve, i, k)
                if routed:
                    dve.wait_ge(stored[k % 2], (i + k // 2 + 1) * 16)
                    ins = dve.tensor_copy(y[:, k % 2, :, :], y_ps[:, k % 2, :, :])
                else:
                    xs = x[:, bass.ds(i * 4 + 2 * k, 2), :]
                    ins = dve.tensor_tensor(xs, y_ps[:, k % 2, :, :], xs, ALU.add)
                ins.then_inc(y_read.sem, 1)
            run_blocks(dve, nblk, NF, {"G": hidden, "Y": output})
            if routed:
                for tile in range(NTILE):
                    for k in range(TOP):
                        if k == 0 and tile % GATHER == 0:
                            dve.wait_ge(gathered[tile // GATHER], GATHER * TOP * 16)
                        if k:
                            dve.wait_ge(added, tile * TOP + 1)
                        dve.scalar_tensor_tensor(x[:, tile, :], back[:, k, tile, :],
                                                 routed[0][k][:, tile:tile + 1], x[:, tile, :], ALU.mult, ALU.add
                                                 ).then_inc(added, 1)

        @block.tensor
        def _(pe):
            for s in (g_ready, y_ready) + ((t_ready,) if routed else ()):
                s.begin(pe)

            def transpose(i, k, _):
                pe.wait_ge(rows_in[k % 2], (i + k // 2 + 1) * 16)
                t_read.wait(pe, i, k - 2)
                for c in range(CC):
                    for t in range(BLK // P):
                        ins = pe.transpose(t_ps[:, k % 2, c, t * P:(t + 1) * P],
                                           rows[:, k % 2, t, c * P:(c + 1) * P], const["ident"][:, :])
                ins.then_inc(t_ready.sem, 1)

            def hidden(i, k, f):
                m = k * NF + f
                buf = k % 2 if routed else 0
                if f == 0:
                    if routed:
                        pe.wait_ge(w13_in[buf], (i + k // 2 + 1) * 32 + (32 if routed[4] and buf == 0 else 0))
                        t_read.wait(pe, i, k)
                    elif k == 0 and isinstance(i, int) and i == 0:
                        pe.wait_ge(w13_in[0], 32)
                h_done.wait(pe, i, m - 2)
                for half, ws in enumerate((w1, w3)):
                    for j in range(2):
                        for c in range(CC):
                            src = rowsT[:, k % 2, c, :] if routed else xnT[:, c, bass.ds((i * 2 + k) * BLK, BLK)]
                            ins = pe.matmul(g_ps[:, f % 2, half, j * BLK:(j + 1) * BLK],
                                            ws[:, buf, c, (2 * f + j) * P:(2 * f + j + 1) * P], src,
                                            start=c == 0, stop=c == CC - 1)
                ins.then_inc(g_ready.sem, 1)

            def output(i, k, _):
                buf = k % 2 if routed else 0
                h_done.wait(pe, i, k * NF + NF - 1)
                y_read.wait(pe, i, k - 2)
                if routed:
                    pe.wait_ge(w2_in[buf], (i + k // 2 + 1) * 16 + (16 if routed[4] and buf == 0 else 0))
                else:
                    pe.wait_ge(w2_in[0], 16)
                for t in range(BLK // P):
                    for f in range(FC):
                        ins = pe.matmul(y_ps[:, k % 2, t, :], h[:, k % 2, f, t * P:(t + 1) * P], w2[:, buf, f, :],
                                        start=f == 0, stop=f == FC - 1)
                ins.then_inc(y_ready.sem, 1)
            run_blocks(pe, nblk, NF, {"G": hidden, "Y": output} | ({"T": transpose} if routed else {}))


def build(nc, inputs, out):
    with ExitStack() as ctx:
        x = ctx.enter_context(nc.sbuf_tensor("x_sb", [P, B * NT, D], F32))
        const = load_constants(nc, ctx, x, inputs)

        def of(tag):
            return {n[len(tag) + 1:]: a for n, a in inputs.items() if n.startswith(tag + "_")}

        context = {"ctx": inputs["ctx"], "ctxT": inputs["ctxT"]}
        attention(nc, "l0a", x, const, of("l0a"), "causal")
        geglu(nc, "l0g", x, const, context)
        moe(nc, "l0m", x, const, of("l0m"), 512, phi=False, shared=True)
        attention(nc, "l1a", x, const, of("l1a"), "full")
        attention(nc, "l1x", x, const, of("l1x") | context, "cross")
        moe(nc, "l1m", x, const, of("l1m"), 1024, phi=True, shared=False)

        stored = ctx.enter_context(nc.semaphore("stored"))
        with nc.Block() as block:
            @block.sync
            def _(sp):
                sp.dma_start(out.rearrange("b (t p) d -> p (b t) d", p=P), x[:, :, :]).then_inc(stored, 16)
                sp.wait_ge(stored, 16)


def rope_factor():
    theta = np.float32(1) / np.float32(10000) ** (np.float32(2) * np.arange(HD // 2, dtype=np.float32) / np.float32(HD))
    ang = np.arange(1, T + 1, dtype=np.float32)[:, None] * theta.astype(np.float32)[None]
    ang = np.concatenate([ang, ang], axis=-1).astype(np.float32)
    return (np.cos(ang) + np.sin(ang)).astype(np.float32)


def layout(i):
    a = {"x": i["x"], "ctx": i["ctx_1024"], "ctxT": i["ctx_1024"].transpose(0, 2, 1)}
    at = np.arange(P)
    a["ident"] = np.eye(P, dtype=np.float32)
    a["spread"] = ((at[:, None] % 32 == HD) & (at[:, None] // 32 == at[None] // 32)).astype(np.float32)
    a["rope"] = np.tile(rope_factor().T, (P // HD, 1))
    a["masks"] = np.stack([np.where(at[None] > at[:, None], NEG, 0), np.where(at[None] < at[:, None], NEG, 0)],
                          axis=1).astype(np.float32)
    a["iota"] = np.tile(np.arange(32, dtype=np.float32), (P, 1))
    a["before"] = (at[:, None] < at[None]).astype(np.float32)

    def heads_padded(wt):
        padded = np.zeros((GH, 32, NG, D), np.float32)
        padded[:, 0:HD] = wt.reshape(NG, GH, HD, D).transpose(1, 2, 0, 3)
        return padded.reshape(P, NG, D)

    def attn(tag, wt, bias, wout, bout):
        a[tag + "_wqkv"] = wt
        a[tag + "_bqk"] = bias[0:2 * D].reshape(2 * CC, P).T
        a[tag + "_bv"] = bias[None, 2 * D:]
        a[tag + "_wout"] = heads_padded(wout)
        a[tag + "_bo"] = bout[None]

    attn("l0a", i["L0_attn_W_attn"].T, i["L0_attn_b_attn"], i["L0_attn_W_proj"].T, i["L0_attn_b_proj"])
    attn("l1a", i["L1_attn_W_qkv"].reshape(H, 3, HD, D).transpose(1, 0, 2, 3).reshape(3 * D, D).T,
         i["L1_attn_b_qkv"].reshape(H, 3, HD).transpose(1, 0, 2).reshape(3 * D),
         i["L1_attn_W_out"].T, i["L1_attn_b_out"])
    attn("l1x", np.concatenate([i["L1_xattn_Wq"], i["L1_xattn_Wkv"]], axis=1),
         np.concatenate([i["L1_xattn_bq"], i["L1_xattn_bkv"]]), i["L1_xattn_Wo"], i["L1_xattn_bo"])
    a["l0m_router"], a["l0m_router_bias"] = i["L0_ffn_router_w"].T, i["L0_ffn_experts_bias"][None]
    for n in ("w1", "w3", "w2"):
        a["l0m_" + n] = np.concatenate([i["L0_ffn_" + n], i["L0_ffn_s" + n]])
    a["l1m_router"], a["l1m_router_bias"] = i["L1_ffn_gate_w"].T, np.zeros((1, 8), np.float32)
    for n in ("w1", "w3", "w2"):
        a["l1m_" + n] = i["L1_ffn_" + n].transpose(0, 2, 1)
    return a


def kernel(**inputs):
    import concourse.bacc as bacc
    from concourse.bass_utils import run_bass_kernel_spmd

    arrays = {f"in_{n}": np.ascontiguousarray(a) for n, a in layout({n: np.asarray(a) for n, a in inputs.items()}).items()}
    nc = bacc.Bacc("TRN2", target_bir_lowering=False, num_devices=1)
    aps = {n[3:]: nc.dram_tensor(n, a.shape, mybir.dt.from_np(a.dtype), kind="ExternalInput").ap()
           for n, a in arrays.items()}
    out = nc.dram_tensor("out_x", (B, T, D), F32, kind="ExternalOutput").ap()
    build(nc, aps, out)
    r = run_bass_kernel_spmd(nc, [arrays], core_ids=[0])
    return r.results[0]["out_x"]
```

```python
from contextlib import ExitStack

import numpy as np

import concourse.bass as bass
from concourse import mybir

F32 = mybir.dt.float32
F32R = mybir.dt.float32r
BF16 = mybir.dt.bfloat16
I32 = mybir.dt.int32
U32 = mybir.dt.uint32
ALU = mybir.AluOpType
ACT = mybir.ActivationFunctionType
AX = mybir.AxisListType

P = 128
B, T, D = 4, 512, 256
NT = T // P
CC = D // P
H, HD = 16, 16
GH = 4
NG = H // GH
NPAIR = H // 2
EPS = 1e-5
NEG = -1e30
SCALE = 1.0 / 4.0


class Steps:

    def __init__(self, sem, per):
        self.sem, self.per = sem, per

    def begin(self, eng):
        eng.sem_inc(self.sem, self.per)

    def count(self, b, step):
        return (b + 1) * self.per + step + 1

    def wait(self, eng, b, step):
        eng.wait_ge(self.sem, self.count(b, step))


def wait_all(eng, *waits):
    values = [s.count(b, step) for s, b, step in waits]
    for v in values:
        eng.compute_val(v)
    for (s, _, _), v in zip(waits, values):
        eng.wait_ge(s.sem, v)


def batch_body(eng, nb, body):
    with eng.Fori(0, nb - 1) as b:
        body(b, b + 1)
    body(nb - 1, None)


def attention_slot(b, g, nxt, prev, kind):
    cross, causal = kind == "cross", kind == "causal"
    last = (b, g - 1) if g else (prev, NG - 1)
    maxima = (b, g + 2) if g < 2 else (nxt, g - 2)
    rows = (b, g + 1) if g < 3 else (nxt, 0)
    preps = {0: {3: 0, 4: 1, 6: 2, 7: 3}, 1: {1: 4, 3: 5, 4: 6, 6: 7}}.get(g, {})
    rests = {0: {7: 2}, 1: {0: 3, 2: 4, 4: 5}}.get(g, {})
    for j in range(2 * NT):
        yield "S", b, g, j
        if not cross and maxima[0] is not None:
            yield "A", *maxima, 2 * j
            if causal:
                yield "A", *maxima, 2 * j + 1
        if nxt is not None and j in rests:
            yield "LO", nxt, rests[j], 0
        if j == 0:
            if g == 0 and nxt is not None:
                yield "LN1", nxt, 0, 0
            if g >= 2 and nxt is not None:
                yield "STACK", nxt, g - 1, 0
            if g == 0 and prev is not None:
                yield "STACK", b, NG - 1, 0
            elif g == 0 and cross:
                yield "STACK", b, 2, 0
                yield "STACK", b, 3, 0
        if j % 2 and (j > 1 or last[0] is not None):
            yield "W", *((b, g) if j > 1 else last), (j - 3) // 2 % NT
        if j == 0 and last[0] is not None:
            yield "PV", *last, NT - 2
        if j == 2:
            if g == 0 and nxt is not None:
                yield "LN2", nxt, 0, 0
            if not cross and rows[0] is not None:
                yield "M", *rows, 0
            if last[0] is not None:
                yield "PV", *last, NT - 1
                yield "O", *last, 0
        if j == 3 and not cross and last[0] is not None:
            yield "Z", *last, 0
        if j == 4 and not cross and last[0] is not None:
            yield "N", *last, 0
        if j >= 4 and j % 2 == 0:
            yield "PV", b, g, (j - 4) // 2
        if j in (5, 7) and last[0] is not None:
            yield "OUT", *last, (j - 5) // 2
        if nxt is not None and j in preps:
            yield "PREP", nxt, preps[j], 0
        if j == 3 and g == 1 and nxt is not None:
            yield "STACK", nxt, 0, 0
        if j == 4:
            if g >= 2 and nxt is not None:
                yield "V", nxt, g - 2, 0
            if g == 0 and prev is not None:
                yield "V", b, 2, 0
                yield "V", b, 3, 0
        if kind == "full" and maxima[0] is not None:
            yield "A", *maxima, 2 * j + 1


def attention_prologue(kind):
    yield "LN1", 0, 0, 0
    yield "LN2", 0, 0, 0
    for use in range(8):
        yield "PREP", 0, use, 0
        if 3 <= use < 7:
            yield "LO", 0, use - 1, 0
    for g in range(NG // 2 if kind == "cross" else NG):
        yield "STACK", 0, g, 0
        yield "V", 0, g, 0
    if kind != "cross":
        for g in range(2):
            for u in range(4 * NT):
                yield "A", 0, g, u
            if g == 0:
                yield "M", 0, g, 0


def attention_tail(b, kind):
    yield "W", b, NG - 1, NT - 1
    yield "PV", b, NG - 1, NT - 2
    yield "PV", b, NG - 1, NT - 1
    yield "O", b, NG - 1, 0
    if kind != "cross":
        yield "Z", b, NG - 1, 0
        yield "N", b, NG - 1, 0
    for j in range(2):
        yield "OUT", b, NG - 1, j


def run_attention(eng, kind, do, at_turn=None):
    def steps(schedule):
        for kind, b, g, j in schedule:
            if kind in do:
                do[kind](b, g, j)

    def slots(b, nxt, after):
        for g in range(1, NG):
            steps(attention_slot(b, g, nxt, b, kind))
        if nxt is not None:
            steps(attention_slot(nxt, 0, after, b, kind))

    steps(attention_prologue(kind))
    steps(attention_slot(0, 0, 1, None, kind))
    with eng.Fori(0, B - 2) as b:
        if at_turn:
            at_turn(b)
        slots(b, b + 1, b + 2)
    if at_turn:
        at_turn(B - 2)
    slots(B - 2, B - 1, None)
    slots(B - 1, None, None)
    steps(attention_tail(B - 1, kind))


def attention(nc, tag, x, const, w, kind):
    cross, causal = kind == "cross", kind == "causal"
    with ExitStack() as ctx:
        def sb(name, shape, dt=F32):
            return ctx.enter_context(nc.sbuf_tensor(f"{tag}_sb_{name}", shape, dt))

        def ps(name, shape, dt=F32):
            return ctx.enter_context(nc.psum_tensor(f"{tag}_{name}", shape, dt))

        def sem(name):
            sems.append(nc.alloc_semaphore(name=f"{tag}_{name}"))
            return sems[-1]

        def steps(name, per):
            return Steps(sem(name), per)

        sems = []
        ctx.callback(nc.all_engine_barrier)
        ctx.callback(nc.clear_and_free_semaphores, sems)

        wqkv = sb("wqkv", [P, CC, 3 * D])
        wout = sb("wout", [P, NG, D])
        bqk = sb("bqk", [P, 2 * CC])
        bv = sb("bv", [1 if cross else P, D])
        bo = sb("bo", [1, D]) if cross else None
        stats = sb("stats", [P, NT, 6])
        mv = sb("mv", [P, NT, 2])
        rstd = sb("rstd", [P, 2, NT])
        xn = sb("xn", [P, NT, D])
        xnT = sb("xnT", [P, CC, T])
        ctxT = sb("ctxT", [P, CC, T]) if cross else None
        qk = sb("qk", [P, 4, T])
        hi = sb("hi", [P, 4, T], F32R)
        lo = sb("lo", [P, 4, T], F32R)
        kst = sb("kst", [P, NPAIR, T], F32R)
        qst = [sb(f"qst{e}", [P, NPAIR, T], F32R) for e in range(2)]
        v = sb("v", [P, B, NT, D])
        vaug = sb("vaug", [P, NT, H, 32])
        probs = sb("probs", [P, 8, 2, T])
        o = sb("o", [P, T])
        rz = sb("rz", [P, NT * GH])
        rz_rows = sb("rz_rows", [P, NT * GH, 32])
        mx = sb("mx", [P, NG, NT, GH])
        mT = sb("mT", [GH, NG, T], F32R)
        kmax = sb("kmax", [P, 4, 2])
        zsum = sb("zsum", [P, 4, 2])
        rzsum = sb("rzsum", [P, 2, 2])
        nothing = sb("nothing", [P, 1])
        nothing_p = sb("nothing_p", [P, 1])

        NS = 3 if cross else 2
        scores = [ps(f"s_ps{k}", [P, 2, T]) for k in range(NS)]
        a_ps = None if cross else ps("a_ps", [P, 2, T])
        m_ps = ps("m_ps", [P, T])
        o_ps = ps("o_ps", [P, T])

        w_in = sem("w_in")
        NW = 5 if cross else 4
        zeroed = sem("zeroed")
        q_zeroed = sem("q_zeroed")
        ctx_in = sem("ctx_in")
        stacked = [sem(f"stacked{g}") for g in range(NG)]
        kstacked = [sem(f"kstacked{g}") for g in range(NG)]
        row_in = [] if cross else [sem(f"row_in{g}") for g in range(NG)]
        ln_stats = steps("ln_stats", 2 * NT)
        ln_rstd = steps("ln_rstd", 2)
        xn_done = steps("xn_done", NT)
        m_ready = steps("m_ready", 8)
        m_act = steps("m_act", 4)
        m_dve = steps("m_dve", 4)
        hi_done = steps("hi_done", 4)
        lo_done = steps("lo_done", 4)
        a_ready = steps("a_ready", 16 * NG)
        a_max = steps("a_max", 16 * NG)
        row_ready = steps("row_ready", NG)
        row_read = steps("row_read", NG)
        s_ready = steps("s_ready", 8 * NG)
        exp_done = steps("exp_done", 8 * NG)
        pv_done = steps("pv_done", NT * NG)
        vaug_done = steps("vaug_done", NT * NG if cross else NG)
        o_copied = steps("o_copied", NG)
        z_ready = steps("z_ready", NG)
        z_read = steps("z_read", NG)
        rz_wide = steps("rz_wide", NG)
        rz_ready = steps("rz_ready", NG)
        o_normed = steps("o_normed", NG)
        out_ready = steps("out_ready", 2 * NG)
        x_added = steps("x_added", 2 * NG)
        k_free = steps("k_free", NG)
        if cross:
            kmax_done = steps("kmax_done", 8 * NG)
            rz_done = steps("rz_done", NT * NG)

        turns = [n % NS for n in range(8 * NG - 1)] + [NS - 1]

        def buffer_of(n):
            return turns[n % (8 * NG)]

        def step_back(n):
            return next(k for k in range(1, 8 * NG) if buffer_of(n - k) == buffer_of(n))

        def first_col(kt):
            return kt * P if causal else 0

        def stacks_wait(eng, b, i):
            if isinstance(b, int) and b == 0:
                return
            for g in (2 * (i % 2), 2 * (i % 2) + 1):
                eng.wait_ge(*((stacked[g], b * 12 * 16) if i < 2 else (kstacked[g], b * 6 * 16)))

        def reads_m(use):
            if 2 <= use < 6:
                return m_dve, use - 2
            return m_act, use if use < 2 else use - 4

        block = ctx.enter_context(nc.Block())

        @block.sync
        def _(sp):
            sp.dma_start(wqkv[:, :, :], w["wqkv"].rearrange("(c p) n -> p c n", p=P)).then_inc(w_in, 16)
            sp.dma_start(wout[:, :, :], w["wout"]).then_inc(w_in, 16)
            sp.dma_start(bqk[:, :], w["bqk"]).then_inc(w_in, 16)
            sp.dma_start(bv[:, :], w["bv"] if cross else w["bv"].to_broadcast([P, D])).then_inc(w_in, 16)
            if cross:
                sp.dma_start(bo[:, :], w["bo"]).then_inc(w_in, 16)

            def context_in(b, *_):
                m_ready.wait(sp, b - 1, 7)
                sp.dma_start(ctxT[:, :, :], w["ctxT"][bass.ds(b, 1)].rearrange("o (c p) t -> p (o c) t", p=P)
                             ).then_inc(ctx_in, 16)

            def stack(b, g, _):
                hg = g // 2
                wait_all(sp, (hi_done, b, hg), (lo_done, b, hg), (s_ready, b - 1, 8 * g + 7))
                for p in (2 * g, 2 * g + 1):
                    r = 32 * (p % 4)
                    for e in range(2):
                        for blk, part in enumerate((hi, lo, hi)):
                            at = 32 * blk + 16 * e
                            sp.dma_start(qst[e][at:at + 16, p, :].bitcast(F32),
                                         part[r + 16 * e:r + 16 * e + 16, hg, :].bitcast(F32)
                                         ).then_inc(stacked[g], 16)

            def rows(b, g, _):
                row_read.wait(sp, b, g)
                for i in range(GH):
                    sp.dma_start(qst[i % 2][96:97, 2 * g + i // 2, :].bitcast(F32),
                                 mT[i:i + 1, g, :].bitcast(F32)).then_inc(row_in[g], 16)

            sp.wait_ge(zeroed, 2)
            sp.wait_ge(q_zeroed, 1)
            run_attention(sp, kind, {"STACK": stack} | ({"LN1": context_in} if cross else {"M": rows}))

        @block.gpsimd
        def _(pool):
            ln_rstd.begin(pool)
            k_free.begin(pool)
            if not cross:
                vaug_done.begin(pool)

            def ln(b, *_):
                ln_stats.wait(pool, b, 2 * NT - 1)
                xn_done.wait(pool, b - 1, NT - 1)
                pool.tensor_tensor(rstd[:, 0, :], mv[:, :, 1], const["eps"][:, :], ALU.add).then_inc(ln_rstd.sem, 1)
                ln_rstd.wait(pool, b, 0)
                pool.tensor_tensor(rstd[:, 1, :], rstd[:, 0, :], const["minus_half"][:, :], ALU.pow
                                   ).then_inc(ln_rstd.sem, 1)
                if isinstance(b, int) and b == 0:
                    pool.memset(qst[0][:, :, :].bitcast(F32), 0.0).then_inc(zeroed, 1)
                    pool.wait_ge(zeroed, 1)
                    pool.memset(kst[96:97, :, :].bitcast(F32), 1.0).then_inc(zeroed, 1)
                    pool.wait_ge(zeroed, 2)
                    pool.memset(vaug[:, :, :, :], 0.0).then_inc(zeroed, 1)
                    pool.wait_ge(zeroed, 3)
                    pool.memset(vaug[:, :, :, HD:HD + 1], 0.0 if cross else 1.0).then_inc(zeroed, 1)
                    pool.wait_ge(zeroed, 4)

            def stack(b, g, _):
                hg = g // 2
                wait_all(pool, (hi_done, b, 2 + hg), (lo_done, b, 2 + hg), (s_ready, b - 1, 8 * g + 7),
                         (k_free, b, g - 1))
                pool.tensor_tensor(nothing_p[:, :], const["eps"][:, 0:1], const["eps"][:, 0:1], ALU.add
                                   ).then_inc(k_free.sem, 1)
                for p in (2 * g, 2 * g + 1):
                    r = 32 * (p % 4)
                    for blk, part in enumerate((hi, hi, lo)):
                        pool.dma_start(kst[32 * blk:32 * blk + 32, p, :].bitcast(F32),
                                       part[r:r + 32, 2 + hg, :].bitcast(F32)).then_inc(kstacked[g], 16)

            def v_group(b, g, _):
                if isinstance(b, int) and b == 0 and g == 0:
                    pool.wait_ge(w_in, NW * 16)
                m_act.wait(pool, b, 3)
                pv_done.wait(pool, b - 1, NT * g + NT - 1)
                src = v[:, bass.ds(b, 1), :, :]
                pool.tensor_tensor(vaug[:, :, GH * g:GH * g + GH, 0:HD],
                                   src[:, :, :, GH * HD * g:GH * HD * (g + 1)].rearrange(
                                       "p o t (h d) -> p (o t) h d", d=HD),
                                   bv[:, GH * HD * g:GH * HD * (g + 1)].rearrange("p (h d) -> p h d", d=HD)
                                   .unsqueeze(1).to_broadcast([P, NT, GH, HD]), ALU.add
                                   ).then_inc(vaug_done.sem, 1)

            run_attention(pool, kind, {"LN1": ln, "STACK": stack} | ({} if cross else {"V": v_group}))

        @block.vector
        def _(dve):
            for s in (ln_stats, xn_done, m_dve, lo_done, a_max, z_read, rz_wide, o_normed, x_added,
                      ) + ((kmax_done, rz_done, vaug_done) if cross else ()):
                s.begin(dve)

            def ln(b, *_):
                if causal and isinstance(b, int) and b == 1:
                    dve.wait_ge(const["x_in"], 16)
                ln_stats.wait(dve, b - 1, 2 * NT - 1)
                for t in range(NT):
                    dve.bn_stats(stats[:, t, :], x[:, bass.ds(b * NT + t, 1), :]).then_inc(ln_stats.sem, 1)
                ln_stats.wait(dve, b, NT - 1)
                ln_rstd.wait(dve, b - 1, 1)
                xn_done.wait(dve, b - 1, NT - 1)
                dve.memset(nothing[:, :], 0.0)
                for t in range(NT):
                    dve.bn_aggr(mv[:, t, :], stats[:, t, :]).then_inc(ln_stats.sem, 1)

            def normal(b, *_):
                ln_stats.wait(dve, b, 2 * NT - 1)
                ln_rstd.wait(dve, b, 1)
                m_ready.wait(dve, b - 1, 1)
                for t in range(NT):
                    dve.tensor_scalar(xn[:, t, :], x[:, bass.ds(b * NT + t, 1), :], mv[:, t, 0:1],
                                      rstd[:, 1, t:t + 1], ALU.subtract, ALU.mult).then_inc(xn_done.sem, 1)
                if isinstance(b, int) and b == 0:
                    dve.memset(qst[1][:, :, :].bitcast(F32), 0.0).then_inc(q_zeroed, 1)

            def prep(b, use, _):
                if not 2 <= use < 6:
                    return
                if isinstance(b, int) and b == 0 and use == 2:
                    dve.wait_ge(w_in, NW * 16)
                i = use - 2
                m_ready.wait(dve, b, use)
                hi_done.wait(dve, b - 1, i)
                lo_done.wait(dve, b - 1, i)
                if cross and i < 2:
                    ins = dve.tensor_scalar(qk[:, i, :], m_ps[:, :], bqk[:, i:i + 1], SCALE, ALU.add, ALU.mult)
                elif causal:
                    ins = dve.scalar_tensor_tensor(qk[:, i, :], m_ps[:, :], bqk[:, i:i + 1], const["rope"][:, :],
                                                   ALU.add, ALU.mult)
                else:
                    ins = dve.tensor_scalar(qk[:, i, :], m_ps[:, :], bqk[:, i:i + 1], None, ALU.add)
                ins.then_inc(m_dve.sem, 1)

            def rest(b, use, _):
                i = use - 2
                hi_done.wait(dve, b, i)
                m_dve.wait(dve, b, i)
                stacks_wait(dve, b, i)
                dve.tensor_tensor(lo[:, i, :], qk[:, i, :], hi[:, i, :].bitcast(F32), ALU.subtract
                                  ).then_inc(lo_done.sem, 1)

            def row_max(b, g, u):
                h, qt = u // NT, u % NT
                a_ready.wait(dve, b, 16 * g + u)
                if u == 0:
                    row_ready.wait(dve, b - 1, g)
                last = (qt + 1) * P if causal else T
                dve.tensor_reduce(mx[:, g, qt, h:h + 1], a_ps[:, u % 2, 0:last], AX.X, ALU.max
                                  ).then_inc(a_max.sem, 1)

            def invert(b, g, _):
                z_ready.wait(dve, b, g)
                rz_ready.wait(dve, b, g - 1)
                dve.reciprocal(rz[:, :], o_ps[:, 0:NT * GH]).then_inc(z_read.sem, 1)
                z_read.wait(dve, b, g)
                dve.tensor_copy(rz_rows[:, :, :], rz[:, :].unsqueeze(2).to_broadcast([P, NT * GH, 32])
                                ).then_inc(rz_wide.sem, 1)

            def norm(b, g, _):
                rz_ready.wait(dve, b, g)
                dve.tensor_tensor(o[:, :], o[:, :], m_ps[:, :], ALU.mult).then_inc(o_normed.sem, 1)

            def out(b, g, j):
                out_ready.wait(dve, b, 2 * g + j)
                if g:
                    x_added.wait(dve, b, 2 * g + j - 2)
                xs = x[:, bass.ds(b * NT + 2 * j, 2), :]
                dve.tensor_tensor(xs, m_ps[:, :].rearrange("p (t n) -> p t n", n=D), xs, ALU.add
                                  ).then_inc(x_added.sem, 1)

            def key_max(b, g, j):
                n = 8 * g + j
                s_ready.wait(dve, b, n)
                exp_done.wait(dve, b, n - 4)
                dve.tensor_reduce(kmax[:, n % 4, :], scores[buffer_of(n)][:, :, :], AX.X, ALU.max, negate=True
                                  ).then_inc(kmax_done.sem, 1)

            def scale_v(b, g, kt):
                m_act.wait(dve, b, 3)
                if isinstance(b, int) and b == 0 and g == 0 and kt == 0:
                    dve.wait_ge(zeroed, 4)
                w, n = NT * g + kt, 8 * g + 2 * kt
                exp_done.wait(dve, b, n + 1)
                vaug_done.wait(dve, b, w - 1)
                dve.reciprocal(rzsum[:, :, :], zsum[:, n % 4:n % 4 + 2, :]).then_inc(rz_done.sem, 1)
                rz_done.wait(dve, b, w)
                pv_done.wait(dve, b - 1, w)
                dve.tensor_tensor(vaug[:, kt, GH * g:GH * g + GH, 0:HD],
                                  v[:, bass.ds(b, 1), kt, GH * HD * g:GH * HD * (g + 1)].rearrange(
                                      "p o (h d) -> p (o h) d", d=HD),
                                  rzsum[:, :, :].rearrange("p n e -> p (n e)").unsqueeze(2).to_broadcast([P, GH, HD]),
                                  ALU.mult).then_inc(vaug_done.sem, 1)

            do = {"LN1": ln, "LN2": normal, "PREP": prep, "LO": rest, "OUT": out}
            if cross:
                do |= {"S": key_max, "W": scale_v}
            else:
                do |= {"A": row_max, "Z": invert, "N": norm}
            run_attention(dve, kind, do)

        @block.scalar
        def _(act):
            for s in (m_act, row_read, hi_done, exp_done, o_copied):
                s.begin(act)

            def prep(b, use, _):
                m_ready.wait(act, b, use) if not 2 <= use < 6 else None
                if use < 2:
                    act.activation(xnT[:, use, :], m_ps[:, :], ACT.Copy).then_inc(m_act.sem, 1)
                elif use < 6:
                    i = use - 2
                    m_dve.wait(act, b, i)
                    stacks_wait(act, b, i)
                    lo_done.wait(act, b - 1, i)
                    act.activation(hi[:, i, :], qk[:, i, :], ACT.Copy).then_inc(hi_done.sem, 1)
                else:
                    t = 2 * (use - 6)
                    act.activation(v[:, bass.ds(b, 1), t:t + 2, :].rearrange("p o t n -> p (o t) n"),
                                   m_ps[:, :].rearrange("p (t n) -> p t n", n=D), ACT.Copy
                                   ).then_inc(m_act.sem, 1)

            def negate_rows(b, g, _):
                row_ready.wait(act, b, g)
                act.activation(mT[:, g, :], m_ps[0:GH, :], ACT.Copy, scale=-1.0).then_inc(row_read.sem, 1)

            def exps(b, g, j):
                n, c0 = 8 * g + j, first_col(j // 2)
                pv_done.wait(act, b, n // 2 - 4)
                if cross:
                    kmax_done.wait(act, b, n)
                    rz_done.wait(act, b, n // 2 - 2)
                    for e in range(2):
                        ins = act.activation(probs[:, n % 8, e, :], scores[buffer_of(n)][:, e, :], ACT.Exp,
                                             bias=kmax[:, n % 4, e:e + 1],
                                             accum_out=zsum[:, n % 4, e:e + 1])
                    ins.then_inc(exp_done.sem, 1)
                else:
                    s_ready.wait(act, b, n)
                    act.activation(probs[:, n % 8, :, c0:T], scores[buffer_of(n)][:, :, c0:T], ACT.Exp, scale=SCALE
                                   ).then_inc(exp_done.sem, 1)

            def copy_o(b, g, _):
                pv_done.wait(act, b, NT * g + NT - 1)
                out_ready.wait(act, b, 2 * g - 1)
                act.activation(o[:, :], o_ps[:, :], ACT.Copy).then_inc(o_copied.sem, 1)

            run_attention(act, kind, {"PREP": prep, "S": exps, "O": copy_o}
                          | ({} if cross else {"M": negate_rows}))

        @block.tensor
        def _(pe):
            for s in (m_ready, row_ready, a_ready, s_ready, pv_done, z_ready, rz_ready, out_ready):
                s.begin(pe)

            m_reader = [None]

            def take_m(steps, b, step):
                if m_reader[0]:
                    last, lb, lstep = m_reader[0]
                    last.wait(pe, lb, lstep)
                m_reader[0] = (steps, b, step)

            def at_turn(b):
                m_reader[0] = (m_dve, b + 1, 1)

            def prep(b, use, _):
                reader, step = reads_m(use)
                take_m(reader, b, step)
                if use < 2:
                    xn_done.wait(pe, b, NT - 1)
                    for t in range(NT):
                        ins = pe.transpose(m_ps[:, t * P:(t + 1) * P], xn[:, t, use * P:(use + 1) * P],
                                           const["ident"][:, :])
                elif use < 6:
                    i = use - 2
                    if isinstance(b, int) and b == 0 and i == 0:
                        pe.wait_ge(w_in, NW * 16)
                    m_act.wait(pe, b, 1)
                    if cross and i == 2:
                        pe.wait_ge(ctx_in, (b + 1) * 16)
                    src = ctxT if cross and i >= 2 else xnT
                    for c in range(CC):
                        ins = pe.matmul(m_ps[:, :], wqkv[:, c, i * P:(i + 1) * P], src[:, c, :],
                                        start=c == 0, stop=c == CC - 1)
                else:
                    src = ctxT if cross else xnT
                    for t in (2 * (use - 6), 2 * (use - 6) + 1):
                        at = m_ps[:, (t % 2) * D:(t % 2 + 1) * D]
                        if cross:
                            pe.matmul(at, const["ones"][0:1, 0:P], bv[:, :], start=True, stop=False)
                        for c in range(CC):
                            ins = pe.matmul(at, src[:, c, t * P:(t + 1) * P], wqkv[:, c, 2 * D:3 * D],
                                            start=not cross and c == 0, stop=c == CC - 1)
                ins.then_inc(m_ready.sem, 1)

            def scores_by_query(b, g, u):
                h, qt = GH * g + u // NT, u % NT
                if u == 0:
                    pe.wait_ge(stacked[g], (b + 1) * 12 * 16)
                    pe.wait_ge(kstacked[g], (b + 1) * 6 * 16)
                a_max.wait(pe, b, 16 * g + u - 2)
                last = (qt + 1) * P if causal else T
                at = a_ps[:, u % 2, 0:last]
                ins = pe.matmul(at, qst[h % 2][0:96, h // 2, qt * P:(qt + 1) * P], kst[0:96, h // 2, 0:last],
                                start=True, stop=not causal)
                if causal:
                    ins = pe.matmul(at[:, qt * P:last], const["ident_b"][:, :], const["mask_q"][:, :],
                                    start=False, stop=True)
                ins.then_inc(a_ready.sem, 1)

            def max_rows(b, g, _):
                a_max.wait(pe, b, 16 * g + 15)
                take_m(row_read, b, g)
                for qt in range(NT):
                    ins = pe.transpose(m_ps[0:GH, qt * P:(qt + 1) * P], mx[:, g, qt, :], const["ident"][:, :])
                ins.then_inc(row_ready.sem, 1)

            def scores_by_key(b, g, j):
                n, kt, p = 8 * g + j, j // 2, 2 * g + j % 2
                if j == 0 and cross:
                    pe.wait_ge(stacked[g], (b + 1) * 12 * 16)
                    pe.wait_ge(kstacked[g], (b + 1) * 6 * 16)
                elif j == 0:
                    pe.wait_ge(row_in[g], (b + 1) * 4 * 16)
                exp_done.wait(pe, b, n - step_back(n))
                c0, rows = first_col(kt), 96 if cross else 97
                for e in range(2):
                    at = scores[buffer_of(n)][:, e, c0:T]
                    ins = pe.matmul(at, kst[0:rows, p, kt * P:(kt + 1) * P], qst[e][0:rows, p, c0:T],
                                    start=True, stop=not causal)
                    if causal:
                        ins = pe.matmul(at[:, 0:P], const["ident_b"][:, :], const["mask_k"][:, :],
                                        start=False, stop=True)
                ins.then_inc(s_ready.sem, 1)

            def probs_v(b, g, kt):
                exp_done.wait(pe, b, 8 * g + 2 * kt + 1)
                if cross:
                    vaug_done.wait(pe, b, NT * g + kt)
                else:
                    vaug_done.wait(pe, b, g)
                if kt == 0:
                    (o_copied if cross else z_read).wait(pe, b, g - 1)
                c0 = first_col(kt)
                for i in range(GH):
                    ins = pe.matmul(o_ps[32 * i:32 * i + 32, c0:T], vaug[:, kt, GH * g + i, :],
                                    probs[:, (8 * g + 2 * kt + i // 2) % 8, i % 2, c0:T],
                                    start=kt == 0, stop=kt == NT - 1)
                ins.then_inc(pv_done.sem, 1)

            def sums(b, g, _):
                o_copied.wait(pe, b, g)
                for qt in range(NT):
                    ins = pe.matmul(o_ps[:, qt * GH:(qt + 1) * GH], o[:, qt * P:(qt + 1) * P], const["sums_of"][:, :],
                                    start=True, stop=True)
                ins.then_inc(z_ready.sem, 1)

            def spread(b, g, _):
                rz_wide.wait(pe, b, g)
                take_m(o_normed, b, g)
                for qt in range(NT):
                    ins = pe.matmul(m_ps[:, qt * P:(qt + 1) * P],
                                    rz_rows[:, qt * GH:(qt + 1) * GH, :].rearrange("p h d -> p (h d)"),
                                    const["ident"][:, :],
                                    start=True, stop=True)
                ins.then_inc(rz_ready.sem, 1)

            def project(b, g, j):
                (o_copied if cross else o_normed).wait(pe, b, g)
                take_m(x_added, b, 2 * g + j)
                for t in (2 * j, 2 * j + 1):
                    at = m_ps[:, (t % 2) * D:(t % 2 + 1) * D]
                    biased = cross and g == 0
                    if biased:
                        pe.matmul(at, const["ones"][0:1, 0:P], bo[:, :], start=True, stop=False)
                    ins = pe.matmul(at, o[:, t * P:(t + 1) * P], wout[:, g, :], start=not biased, stop=True)
                ins.then_inc(out_ready.sem, 1)

            do = {"PREP": prep, "S": scores_by_key, "PV": probs_v, "OUT": project}
            if not cross:
                do |= {"A": scores_by_query, "M": max_rows, "Z": sums, "N": spread}
            run_attention(pe, kind, do, at_turn)


def load_constants(nc, ctx, x, inputs):
    const = {}

    def sb(name, shape, dt=F32):
        const[name] = ctx.enter_context(nc.sbuf_tensor(f"const_{name}", shape, dt))
        return const[name]

    ident, sums_of, rope, ones = sb("ident", [P, P]), sb("sums_of", [P, GH]), sb("rope", [P, T]), sb("ones", [P, P])
    minus_half, eps = sb("minus_half", [P, NT]), sb("eps", [P, NT])
    masks = sb("masks", [P, 2, P])
    iota = sb("iota", [P, 32])
    before = sb("before", [P, P])
    zeros = sb("zeros", [P, D])
    for name in ("rows", "outs"):
        const[name + "_dram"] = nc.dram_tensor(name + "_dram", (NBLK * BLK, D), F32, kind="Internal").ap()
    ident_b, mask_q, mask_k, before_b, ones_b = (sb(n, [P, P], BF16) for n in (
        "ident_b", "mask_q", "mask_k", "before_b", "ones_b"))
    const["x_in"] = ctx.enter_context(nc.semaphore("x_in"))
    const["rows_zeroed"] = ctx.enter_context(nc.semaphore("rows_zeroed"))
    loaded = ctx.enter_context(nc.semaphore("const_loaded"))
    made = ctx.enter_context(nc.semaphore("const_made"))
    with nc.Block() as block:
        @block.sync
        def _(sp):
            xs = inputs["x"].rearrange("b (t p) d -> p (b t) d", p=P)
            sp.dma_start(x[:, 0:NT, :], xs[:, 0:NT, :]).then_inc(loaded, 16)
            sp.dma_start(ident[:, :], inputs["ident"]).then_inc(loaded, 16)
            sp.dma_start(sums_of[:, :], inputs["sums_of"]).then_inc(loaded, 16)
            sp.dma_start(rope[:, :], inputs["rope"]).then_inc(loaded, 16)
            sp.dma_start(masks[:, :, :], inputs["masks"]).then_inc(loaded, 16)
            sp.dma_start(iota[:, :], inputs["iota"]).then_inc(loaded, 16)
            sp.dma_start(before[:, :], inputs["before"]).then_inc(loaded, 16)
            sp.dma_start(x[:, NT:, :], xs[:, NT:, :]).then_inc(const["x_in"], 16)

        @block.vector
        def _(dve):
            dve.memset(zeros[:, :], 0.0).then_inc(made, 1)
            dve.memset(ones[:, :], 1.0).then_inc(made, 1)
            dve.memset(minus_half[:, :], -0.5).then_inc(made, 1)
            dve.memset(eps[:, :], EPS).then_inc(made, 1)
            dve.wait_ge(loaded, 7 * 16)
            dve.tensor_copy(ident_b[:, :], ident[:, :]).then_inc(made, 1)
            dve.tensor_copy(mask_q[:, :], masks[:, 0, :]).then_inc(made, 1)
            dve.tensor_copy(mask_k[:, :], masks[:, 1, :]).then_inc(made, 1)
            dve.tensor_copy(before_b[:, :], before[:, :]).then_inc(made, 1)
            dve.memset(ones_b[:, :], 1.0).then_inc(made, 1)
            dve.wait_ge(made, 9)
    return const


def geglu(nc, tag, x, const, w):
    with ExitStack() as ctx:
        def sb(name, shape, dt=F32):
            return ctx.enter_context(nc.sbuf_tensor(f"{tag}_sb_{name}", shape, dt))

        def ps(name, shape, dt=F32):
            return ctx.enter_context(nc.psum_tensor(f"{tag}_{name}", shape, dt))

        def steps(name, per):
            return Steps(ctx.enter_context(nc.semaphore(f"{tag}_{name}")), per)

        FC = T // P
        stats = sb("stats", [P, NT, 6])
        mv = sb("mv", [P, NT, 2])
        rstd = sb("rstd", [P, 2, NT])
        xn = sb("xn", [P, NT, D])
        xnT = sb("xnT", [P, CC, T])
        ctxT = sb("ctxT", [P, CC, T])
        ctxN = sb("ctxN", [P, FC, D])
        gelu = sb("gelu", [P, FC, T])
        h = sb("h", [P, FC, T])
        nothing = sb("nothing", [P, 1])

        t_ps = ps("t_ps", [P, CC, T])
        g_ps = ps("g_ps", [P, FC, T])
        y_ps = ps("y_ps", [P, 2, 2, D])

        ctxT_in = ctx.enter_context(nc.semaphore(f"{tag}_ctxT_in"))
        ctxN_in = ctx.enter_context(nc.semaphore(f"{tag}_ctxN_in"))
        ln_stats = steps("ln_stats", 2 * NT)
        ln_rstd = steps("ln_rstd", 2)
        xn_done = steps("xn_done", NT)
        t_ready = steps("t_ready", CC)
        t_read = steps("t_read", CC)
        g_ready = steps("g_ready", FC)
        g_gelu = steps("g_gelu", FC)
        h_done = steps("h_done", FC)
        y_ready = steps("y_ready", 2)
        x_added = steps("x_added", 2)

        block = ctx.enter_context(nc.Block())

        def run(eng, do):
            def step(kind, *at):
                if kind in do:
                    do[kind](*at)

            step("LN", 0)
            step("T", 0)

            def body(b, nxt):
                step("IN", b)
                step("G", b)
                if nxt is not None:
                    step("LN", nxt)
                step("Y", b, 0)
                if nxt is not None:
                    step("T", nxt)
                step("Y", b, 1)
            batch_body(eng, B, body)

        @block.sync
        def _(sp):
            def context_in(b):
                wait_all(sp, (g_ready, b - 1, FC - 1))
                sp.dma_start(ctxT[:, :, :], w["ctxT"][bass.ds(b, 1)].rearrange("o (c p) t -> p (o c) t", p=P)
                             ).then_inc(ctxT_in, 16)
                wait_all(sp, (y_ready, b - 1, 1))
                sp.dma_start(ctxN[:, :, :], w["ctx"][bass.ds(b, 1)].rearrange("o (c p) d -> p (o c) d", p=P)
                             ).then_inc(ctxN_in, 16)
            run(sp, {"IN": context_in})

        @block.gpsimd
        def _(pool):
            ln_rstd.begin(pool)
            run(pool, {"LN": lambda b: inverse_deviation(pool, b, mv, rstd, const, ln_stats, ln_rstd, xn_done)})

        @block.vector
        def _(dve):
            for s in (ln_stats, xn_done, t_read, h_done, x_added):
                s.begin(dve)

            def gate(b):
                for f in range(FC):
                    g_gelu.wait(dve, b, f)
                    y_ready.wait(dve, b - 1, 1)
                    dve.tensor_tensor(h[:, f, :], g_ps[:, f, :], gelu[:, f, :], ALU.mult).then_inc(h_done.sem, 1)

            def add(b, j):
                y_ready.wait(dve, b, j)
                xs = x[:, bass.ds(b * NT + 2 * j, 2), :]
                dve.tensor_tensor(xs, y_ps[:, j, :, :], xs, ALU.add).then_inc(x_added.sem, 1)

            def transposed(b):
                for c in range(CC):
                    t_ready.wait(dve, b, c)
                    g_ready.wait(dve, b - 1, FC - 1)
                    dve.tensor_copy(xnT[:, c, :], t_ps[:, c, :]).then_inc(t_read.sem, 1)

            run(dve, {"LN": lambda b: normalise(dve, b, x, stats, mv, rstd, xn, nothing, ln_stats, ln_rstd,
                                                xn_done, t_ready, CC - 1),
                      "T": transposed, "G": gate, "Y": add})

        @block.scalar
        def _(act):
            g_gelu.begin(act)

            def gate(b):
                for f in range(FC):
                    g_ready.wait(act, b, f)
                    h_done.wait(act, b - 1, f)
                    act.activation(gelu[:, f, :], g_ps[:, f, :], ACT.Gelu_apprx_tanh).then_inc(g_gelu.sem, 1)

            run(act, {"G": gate})

        @block.tensor
        def _(pe):
            for s in (t_ready, g_ready, y_ready):
                s.begin(pe)

            def transpose(b):
                xn_done.wait(pe, b, NT - 1)
                for c in range(CC):
                    t_read.wait(pe, b - 1, c)
                    for t in range(NT):
                        ins = pe.transpose(t_ps[:, c, t * P:(t + 1) * P], xn[:, t, c * P:(c + 1) * P],
                                           const["ident"][:, :])
                    ins.then_inc(t_ready.sem, 1)

            def hidden(b):
                pe.wait_ge(ctxT_in, (b + 1) * 16)
                t_read.wait(pe, b, CC - 1)
                for f in range(FC):
                    h_done.wait(pe, b - 1, f)
                    for c in range(CC):
                        ins = pe.matmul(g_ps[:, f, :], ctxT[:, c, f * P:(f + 1) * P], xnT[:, c, :],
                                        start=c == 0, stop=c == CC - 1)
                    ins.then_inc(g_ready.sem, 1)

            def output(b, j):
                if j == 0:
                    pe.wait_ge(ctxN_in, (b + 1) * 16)
                    h_done.wait(pe, b, FC - 1)
                x_added.wait(pe, b - 1, j)
                for t in range(2):
                    for f in range(FC):
                        ins = pe.matmul(y_ps[:, j, t, :], h[:, f, (2 * j + t) * P:(2 * j + t + 1) * P],
                                        ctxN[:, f, :], start=f == 0, stop=f == FC - 1)
                ins.then_inc(y_ready.sem, 1)

            run(pe, {"T": transpose, "G": hidden, "Y": output})


def inverse_deviation(pool, b, mv, rstd, const, ln_stats, ln_rstd, xn_done):
    ln_stats.wait(pool, b, 2 * NT - 1)
    xn_done.wait(pool, b - 1, NT - 1)
    pool.tensor_tensor(rstd[:, 0, :], mv[:, :, 1], const["eps"][:, :], ALU.add).then_inc(ln_rstd.sem, 1)
    ln_rstd.wait(pool, b, 0)
    pool.tensor_tensor(rstd[:, 1, :], rstd[:, 0, :], const["minus_half"][:, :], ALU.pow).then_inc(ln_rstd.sem, 1)


def normalise(dve, b, x, stats, mv, rstd, xn, nothing, ln_stats, ln_rstd, xn_done, xn_read, last_read):
    ln_stats.wait(dve, b - 1, 2 * NT - 1)
    for t in range(NT):
        dve.bn_stats(stats[:, t, :], x[:, bass.ds(b * NT + t, 1), :]).then_inc(ln_stats.sem, 1)
    ln_stats.wait(dve, b, NT - 1)
    ln_rstd.wait(dve, b - 1, 1)
    xn_done.wait(dve, b - 1, NT - 1)
    dve.memset(nothing[:, :], 0.0)
    for t in range(NT):
        dve.bn_aggr(mv[:, t, :], stats[:, t, :]).then_inc(ln_stats.sem, 1)
    ln_stats.wait(dve, b, 2 * NT - 1)
    ln_rstd.wait(dve, b, 1)
    if xn_read is not None:
        xn_read.wait(dve, b - 1, last_read)
    for t in range(NT):
        dve.tensor_scalar(xn[:, t, :], x[:, bass.ds(b * NT + t, 1), :], mv[:, t, 0:1],
                          rstd[:, 1, t:t + 1], ALU.subtract, ALU.mult).then_inc(xn_done.sem, 1)


E, TOP = 8, 2
BLK = 256
NTILE = B * NT
GATHER = 4
NBLK = (B * T * TOP - E) // BLK + E


def moe(nc, tag, x, const, w, width, phi, shared, out=None):
    FC = width // P
    with ExitStack() as ctx:
        def sb(name, shape, dt=F32):
            return ctx.enter_context(nc.sbuf_tensor(f"{tag}_sb_{name}", shape, dt))

        def sem(name):
            return ctx.enter_context(nc.semaphore(f"{tag}_{name}"))

        xn = sb("xn", [P, B, NT, D])
        weight = [sb(f"weight{k}", [P, NTILE]) for k in range(TOP)]
        place = [sb(f"place{k}", [P, NTILE], U32) for k in range(TOP)]
        block_expert = sb("block_expert", [P, NBLK], I32)
        n2 = 2 if FC == 4 else 1
        raw13, raw2 = sb("raw13", [P, 2, CC, width]), sb("raw2", [P, n2, FC, D])
        hi1, lo1, hi3, lo3 = (sb(n, [P, 2, CC, width], F32R) for n in ("hi1", "lo1", "hi3", "lo3"))
        hi2, lo2 = (sb(n, [P, n2, FC, D], F32R) for n in ("hi2", "lo2"))
        w13_in = [sem(f"w13_in{f}") for f in range(FC // 2)]
        w2_in = [sem(f"w2_in{k}") for k in range(n2)]
        scattered = sem("scattered")

        def load_w13(sp, e, f):
            cols = slice(2 * f * P, (2 * f + 2) * P)
            for n, name in enumerate(("w1", "w3")):
                sp.dma_start(raw13[:, n, :, cols],
                             w[name][bass.ds(e, 1), :, cols].rearrange("o (c p) f -> p (o c) f", p=P)
                             ).then_inc(w13_in[f], 16)

        def load_w2(sp, k, e):
            sp.dma_start(raw2[:, k % n2, :, :], w["w2"][bass.ds(e, 1)].rearrange("o (c p) d -> p (o c) d", p=P)
                         ).then_inc(w2_in[k % n2], 16)

        buffers = (raw13, raw2, (hi1, lo1), (hi3, lo3), (hi2, lo2), w13_in, w2_in)
        with ExitStack() as early:
            xnT = early.enter_context(nc.sbuf_tensor(f"{tag}_sb_xnT", [P, CC, B * T], F32))
            routing(nc, tag, x, const, w, phi, shared, xn, xnT, weight, place, block_expert, load_w13, load_w2)
            if shared:
                experts(nc, tag + "s", x, const, FC, xnT, buffers, scatter=(xn, place, scattered),
                        first=(block_expert, load_w13, load_w2))
        experts(nc, tag, x, const, FC, None, buffers, scatter=(xn, place, scattered),
                routed=(weight, block_expert, load_w13, load_w2, shared), out=out)


def routing(nc, tag, x, const, w, phi, shared, xn, xnT, weight, place, block_expert, load_w13, load_w2):
    with ExitStack() as ctx:
        def sb(name, shape, dt=F32):
            return ctx.enter_context(nc.sbuf_tensor(f"{tag}_sb_{name}", shape, dt))

        def ps(name, shape):
            return ctx.enter_context(nc.psum_tensor(f"{tag}_{name}", shape, F32))

        def sem(name):
            return ctx.enter_context(nc.semaphore(f"{tag}_{name}"))

        stats = sb("stats", [P, NT, 6])
        mv = sb("mv", [P, NT, 2])
        rstd = sb("rstd", [P, 2, NT])
        nothing = sb("nothing", [P, 1])
        router = sb("router", [P, CC, E])
        rbias = sb("rbias", [P, E])
        r = {n: sb(n, [P, NTILE, E]) for n in ("lg", "eq", "cand", "oh0", "oh1", "l2", "ab", "df", "keep",
                                               "row", "mine")}
        both = sb("both", [P, NTILE, E], BF16)
        c1 = {n: sb(n, [P, NTILE]) for n in ("m1", "m2", "first", "ex", "den", "at")}
        c8 = {n: sb(n, [P, E]) for n in ("count", "used", "start", "end")}
        c88 = {n: sb(n, [P, E, E]) for n in ("fills", "before")}
        ends = sb("ends", [P, NBLK, E])
        expert_f = sb("expert_f", [P, NBLK])

        t_ps = ps("t_ps", [P, CC, T])
        l_ps = ps("l_ps", [P, NTILE, E])
        rank_ps = ps("rank_ps", [P, NTILE, E])
        count_ps = ps("count_ps", [P, E])

        ln_stats = Steps(sem("ln_stats"), 2 * NT)
        ln_rstd = Steps(sem("ln_rstd"), 2)
        xn_done = Steps(sem("xn_done"), NT)
        t_ready = Steps(sem("t_ready"), CC)
        t_read = Steps(sem("t_read"), CC)
        router_in = sem("router_in")
        logits_ready = sem("logits_ready")
        routed = sem("routed")
        route_exp = sem("route_exp")
        chosen = sem("chosen")
        ranked = sem("ranked")
        block = ctx.enter_context(nc.Block())

        @block.sync
        def _(sp):
            sp.dma_start(router[:, :, :], w["router"].rearrange("(c p) e -> p c e", p=P)).then_inc(router_in, 16)
            sp.dma_start(rbias[:, :], w["router_bias"].to_broadcast([P, E])).then_inc(router_in, 16)
            if shared:
                for f in range(w["w1"].shape[2] // P // 2):
                    load_w13(sp, E, f)
                load_w2(sp, 0, E)
                sp.dma_start(const["rows_dram"].rearrange("(n p) d -> p n d", p=P),
                             const["zeros"][:, :].unsqueeze(1).to_broadcast([P, NBLK * BLK // P, D])
                             ).then_inc(const["rows_zeroed"], 16)

        @block.gpsimd
        def _(pool):
            ln_rstd.begin(pool)
            for b in range(B):
                inverse_deviation(pool, b, mv, rstd, const, ln_stats, ln_rstd, xn_done)

        @block.scalar
        def _(act):
            t_read.begin(act)
            for b in range(B):
                for c in range(CC):
                    t_ready.wait(act, b, c)
                    act.activation(xnT[:, c, b * T:(b + 1) * T], t_ps[:, c, :], ACT.Copy).then_inc(t_read.sem, 1)
            if phi:
                for k, name in enumerate(("df", "l2")):
                    act.wait_ge(routed, PHI_EXP[k])
                    act.activation(r[name][:, :, :], r[name][:, :, :], ACT.Exp).then_inc(route_exp, 1)
            else:
                act.wait_ge(routed, TOP2_EXP)
                act.activation(c1["ex"][:, :], c1["ex"][:, :], ACT.Exp).then_inc(route_exp, 1)

        @block.tensor
        def _(pe):
            t_ready.begin(pe)

            def logits(b):
                for c in range(CC):
                    t_read.wait(pe, b, c)
                for tile in range(b * NT, (b + 1) * NT):
                    for c in range(CC):
                        ins = pe.matmul(l_ps[:, tile, :], xnT[:, c, tile * P:(tile + 1) * P], router[:, c, :],
                                        start=c == 0, stop=c == CC - 1)
                ins.then_inc(logits_ready, 1)

            for b in range(B):
                xn_done.wait(pe, b, NT - 1)
                for c in range(CC):
                    t_read.wait(pe, b - 1, c)
                    for t in range(NT):
                        ins = pe.transpose(t_ps[:, c, t * P:(t + 1) * P], xn[:, b, t, c * P:(c + 1) * P],
                                           const["ident"][:, :])
                    ins.then_inc(t_ready.sem, 1)
                if b == 1:
                    pe.wait_ge(router_in, 32)
                if b:
                    logits(b - 1)
            logits(B - 1)
            pe.wait_ge(chosen, 1)
            pe.matmul(rank_ps[:, :, :], const["before_b"][:, :], both[:, :, :], start=True, stop=False)
            for back in range(1, NTILE):
                pe.matmul(rank_ps[:, back:NTILE, :], const["ones_b"][:, :], both[:, 0:NTILE - back, :],
                          start=False, stop=back == NTILE - 1)
            for tile in range(NTILE):
                ins = pe.matmul(count_ps[:, :], const["ones_b"][:, :], both[:, tile, :],
                                start=tile == 0, stop=tile == NTILE - 1)
            ins.then_inc(ranked, 1)

        @block.vector
        def _(dve):
            for s in (ln_stats, xn_done):
                s.begin(dve)
            for b in range(B):
                normalise(dve, b, x, stats, mv, rstd, xn[:, b, :, :], nothing, ln_stats, ln_rstd, xn_done,
                          None, None)
            dve.wait_ge(logits_ready, B)
            dve.wait_ge(router_in, 32)
            step = [0]

            def then(ins):
                step[0] += 1
                ins.then_inc(routed, 1)
                dve.wait_ge(routed, step[0])

            top_two(dve, then, step, const, l_ps, rbias, both, r, c1, weight, phi, route_exp, chosen)
            dve.wait_ge(ranked, 1)
            placement(dve, then, const, rank_ps, count_ps, r, c1, c8, c88, ends, expert_f, place, block_expert)


PHI_EXP = (12, 29)
TOP2_EXP = 14


def over_experts(t):
    return t[:, :].unsqueeze(2).to_broadcast([P, NTILE, E])


def top_two(dve, then, step, const, l_ps, rbias, both, r, c1, weight, phi, route_exp, chosen):
    def full(t):
        return t[:, :, :]

    wide = over_experts
    iota = const["iota"][:, 0:E].unsqueeze(1).to_broadcast([P, NTILE, E])
    lg, eq, cand, oh0, oh1, l2 = (r[n] for n in ("lg", "eq", "cand", "oh0", "oh1", "l2"))
    then(dve.tensor_tensor(full(lg), l_ps[:, :, :], rbias[:, :].unsqueeze(1).to_broadcast([P, NTILE, E]), ALU.add))

    def top(src, m, oh):
        then(dve.tensor_reduce(c1[m][:, :], full(src), AX.X, ALU.max))
        then(dve.tensor_tensor(full(eq), full(src), wide(c1[m]), ALU.not_equal))
        then(dve.scalar_tensor_tensor(full(cand), full(eq), float(E), iota, ALU.mult, ALU.add))
        then(dve.tensor_reduce(c1["first"][:, :], full(cand), AX.X, ALU.min))
        then(dve.tensor_tensor(full(oh), wide(c1["first"]), iota, ALU.is_equal))

    def unmasked_sum(m, ex, drop, out, nexp):
        ab, keep = r["ab"], r["keep"]
        then(dve.scalar_tensor_tensor(full(ab), full(lg), -1.0, full(lg), ALU.mult, ALU.max))
        then(dve.tensor_tensor(full(ab), full(ab), wide(c1[m]), ALU.max))
        then(dve.tensor_tensor(full(keep), wide(c1[m]), full(lg), ALU.subtract))
        then(dve.scalar_tensor_tensor(full(keep), full(ab), 0.02, full(keep), ALU.mult, ALU.is_ge))
        if drop is not None:
            then(dve.scalar_tensor_tensor(full(keep), full(drop), 0.0, full(keep), ALU.is_equal, ALU.mult))
        then(dve.tensor_tensor(full(ex), full(lg), wide(c1[m]), ALU.subtract))
        then(dve.tensor_scalar(full(ex), full(ex), 0.0, None, ALU.min))
        assert step[0] == PHI_EXP[nexp - 1], step[0]
        dve.wait_ge(route_exp, nexp)
        then(dve.tensor_tensor(full(ex), full(ex), full(keep), ALU.mult))
        then(dve.tensor_reduce(c1["den"][:, :], full(ex), AX.X, ALU.add))
        then(dve.reciprocal(out[:, :], c1["den"][:, :]))

    top(lg, "m1", oh0)
    if phi:
        unmasked_sum("m1", r["df"], None, weight[0], 1)
    then(dve.scalar_tensor_tensor(full(l2), full(oh0), -3e38, full(lg), ALU.mult, ALU.add))
    top(l2, "m2", oh1)
    then(dve.tensor_tensor(full(both), full(oh0), full(oh1), ALU.add))
    dve.sem_inc(chosen, 1)
    if phi:
        unmasked_sum("m2", l2, oh0, weight[1], 2)
    else:
        then(dve.tensor_tensor(c1["ex"][:, :], c1["m2"][:, :], c1["m1"][:, :], ALU.subtract))
        assert step[0] == TOP2_EXP
        dve.wait_ge(route_exp, 1)
        then(dve.tensor_scalar(c1["den"][:, :], c1["ex"][:, :], 1.0, None, ALU.add))
        then(dve.reciprocal(weight[0][:, :], c1["den"][:, :]))
        then(dve.tensor_tensor(weight[1][:, :], c1["ex"][:, :], weight[0][:, :], ALU.mult))


def placement(dve, then, const, rank_ps, count_ps, r, c1, c8, c88, ends, expert_f, place, block_expert):
    iota = const["iota"]
    fills, before = c88["fills"], c88["before"]
    along = iota[:, 0:E].unsqueeze(1).to_broadcast([P, E, E])
    down = iota[:, 0:E].unsqueeze(2).to_broadcast([P, E, E])
    then(dve.tensor_copy(c8["count"][:, :], count_ps[:, :]))
    then(dve.scalar_tensor_tensor(fills[:, :, :], along, float(BLK),
                                  c8["count"][:, :].unsqueeze(2).to_broadcast([P, E, E]), ALU.mult, ALU.is_lt))
    then(dve.tensor_reduce(c8["used"][:, :], fills[:, :, :], AX.X, ALU.add))
    then(dve.tensor_tensor(before[:, :, :], along, down, ALU.is_lt))
    then(dve.tensor_tensor(before[:, :, :], before[:, :, :],
                           c8["used"][:, :].unsqueeze(1).to_broadcast([P, E, E]), ALU.mult))
    then(dve.tensor_reduce(c8["start"][:, :], before[:, :, :], AX.X, ALU.add))
    then(dve.tensor_tensor(c8["end"][:, :], c8["start"][:, :], c8["used"][:, :], ALU.add))
    then(dve.scalar_tensor_tensor(r["row"][:, :, :], c8["start"][:, :].unsqueeze(1).to_broadcast([P, NTILE, E]),
                                  float(BLK), rank_ps[:, :, :], ALU.mult, ALU.add))
    for k in range(TOP):
        then(dve.tensor_tensor(r["mine"][:, :, :], r["row"][:, :, :], r[f"oh{k}"][:, :, :], ALU.mult))
        then(dve.tensor_reduce(c1["at"][:, :], r["mine"][:, :, :], AX.X, ALU.add))
        then(dve.tensor_copy(place[k][:, :], c1["at"][:, :]))
    then(dve.tensor_tensor(ends[:, :, :], c8["end"][:, :].unsqueeze(1).to_broadcast([P, NBLK, E]),
                           iota[:, 0:NBLK].unsqueeze(2).to_broadcast([P, NBLK, E]), ALU.is_le))
    then(dve.tensor_reduce(expert_f[:, :], ends[:, :, :], AX.X, ALU.add))
    then(dve.tensor_scalar(expert_f[:, :], expert_f[:, :], float(E - 1), None, ALU.min))
    then(dve.tensor_copy(block_expert[:, :], expert_f[:, :]))


def run_blocks(eng, nblk, nf, do):
    def step(kind, i, k, f=0):
        if kind in do:
            do[kind](i, k, f)

    def chunks(i, k, f, ahead):
        step("G", i, k, f)
        h_first = nf > 2 and f == nf - 1
        if h_first:
            step("H", i, k, f)
        if ahead:
            step("W", i, k + 1, f)
        if nf == 2:
            step("V", i, k, f)
        if not h_first:
            step("H", i, k, f)

    def body(i, k, after):
        for f in range(2, nf):
            chunks(i, k, f, after >= 1)
        for t in range(BLK // P):
            if after:
                chunks(i, k + 1, t, after >= 2)
            if t == 0 and after >= 2:
                step("T", i, k + 2)
            step("Y", i, k, t)
        if after and nf > 2:
            for f in range(nf):
                step("V", i, k + 1, f)

    for kind in ("T", "C") if do.get("rows first") else ("C", "T"):
        step(kind, 0, 0)
    for f in range(2):
        chunks(0, 0, f, True)
        if f == 0:
            step("T", 0, 1)
    turns = (nblk - 2) // 2
    with eng.Fori(0, turns) as i:
        body(i, 0, 2)
        body(i, 1, 2)
    for n in range(2 * turns, nblk):
        body(turns, n - 2 * turns, min(2, nblk - 1 - n))


def experts(nc, tag, x, const, FC, xnT, buffers, scatter, routed=None, out=None, first=None):
    NF = FC // 2
    nblk = NBLK if routed else B * T // BLK
    raw13, raw2, (hi1, lo1), (hi3, lo3), (hi2, lo2), w13_in, w2_in = buffers
    n2 = 2 if NF == 2 else 1
    xn, place, scattered = scatter
    scatter_here = not routed or not routed[4]
    with ExitStack() as ctx:
        def sb(name, shape, dt=F32):
            return ctx.enter_context(nc.sbuf_tensor(f"{tag}_sb_x{name}", shape, dt))

        def ps(name, shape):
            return ctx.enter_context(nc.psum_tensor(f"{tag}_x{name}", shape, F32))

        def sem(name):
            return ctx.enter_context(nc.semaphore(f"{tag}_x{name}"))

        silu = sb("silu", [P, 2, 2 * BLK])
        h = sb("h", [P, 2, 2 * BLK])
        h_hi = sb("h_hi", [P, 2, FC, BLK], F32R)
        h_lo = sb("h_lo", [P, 2, FC, BLK], F32R)
        rows_hi = sb("rows_hi", [P, 2, CC, BLK], F32R)
        rows_lo = sb("rows_lo", [P, 2, CC, BLK], F32R)
        if routed:
            rows = sb("rows", [P, 2, BLK // P, D])
            y = sb("y", [P, 2, BLK // P, D])
            back = [xn[:, :, :, :].rearrange("p b t d -> p (b t) d")]
            if 2 * CC * FC * P >= NTILE * D:
                back.append(raw13[:, :, :, :].rearrange("p n c f -> p (n c f)").rearrange("p (t d) -> p t d", d=D))
            else:
                back.append(sb("back", [P, NTILE, D])[:, :, :])
            t_ps = ps("t_ps", [P, 2, CC, BLK])
        g_ps = ps("g_ps", [P, 2, 2, 2 * BLK])
        y_ps = ps("y_ps", [P, 2, BLK // P, D])

        if routed:
            rows_in = [sem(f"rows_in{k}") for k in range(2)]
            stored = [sem(f"stored{k}") for k in range(2)]
            gathered = [sem(f"gathered{n}") for n in range(NTILE // GATHER)]
            added = sem("added")
            w2_free = sem("w2_free")
            out_stored = sem("out_stored")
            t_ready = Steps(sem("t_ready"), 2)
        rows_split = Steps(sem("rows_split"), 2)
        rows_done = Steps(sem("rows_done"), 2)
        w13_split = Steps(sem("w13_split"), 2 * NF)
        w13_done = Steps(sem("w13_done"), 2 * NF)
        w2_split = Steps(sem("w2_split"), 2 * NF)
        w2_done = Steps(sem("w2_done"), 2 * NF)
        g_ready = Steps(sem("g_ready"), 2 * NF)
        g_silu = Steps(sem("g_silu"), 2 * NF)
        h_made = Steps(sem("h_made"), 2 * NF)
        h_split = Steps(sem("h_split"), 2 * NF)
        h_done = Steps(sem("h_done"), 2 * NF)
        y_ready = Steps(sem("y_ready"), 2)
        y_read = Steps(sem("y_read"), 2)
        block = ctx.enter_context(nc.Block())

        def two_chunks(t, k, f):
            return t[:, k, :, 2 * f * P:(2 * f + 2) * P]

        @block.sync
        def _(sp):
            if not routed:
                e = sp.value_load(first[0][0:1, 0:1], min_val=0, max_val=E - 1)
                for f in range(NF):
                    w13_done.wait(sp, 0, f)
                    first[1](sp, e, f)
                w2_done.wait(sp, 0, NF - 1)
                first[2](sp, 0, e)
                return
            _, block_expert, load_w13, load_w2, _ = routed

            def expert(i, k):
                return sp.value_load(block_expert[0:1, bass.ds(i * 2 + k, 1)], min_val=0, max_val=E - 1)

            def load_rows(i, k):
                sp.dma_start(rows[:, k % 2, :, :], const["rows_dram"][bass.ds((i * 2 + k) * BLK, BLK), :].rearrange(
                    "(t p) d -> p t d", p=P)).then_inc(rows_in[k % 2], 16)

            def load_next_w2(i, k, e):
                wait_all(sp, (w2_done, i, (k + 2 - n2) * NF + NF - 1))
                sp.sem_inc(w2_free, 1)
                load_w2(sp, k + 2, e)

            def ahead(i, k, after):
                if after >= 2:
                    e = expert(i, k + 2)
                    if n2 == 2:
                        load_next_w2(i, k, e)
                    for f in range(2, NF):
                        wait_all(sp, (w13_done, i, (k + 1) * NF + f))
                        load_w13(sp, e, f)
                if after >= 3:
                    first = expert(i, k + 3)
                    wait_all(sp, (w13_done, i, (k + 2) * NF))
                    load_w13(sp, first, 0)
                if after >= 4:
                    wait_all(sp, (t_ready, i, k + 2))
                    load_rows(i, k + 4)
                if after >= 3:
                    wait_all(sp, (w13_done, i, (k + 2) * NF + 1))
                    load_w13(sp, first, 1)
                wait_all(sp, (y_read, i, k))
                sp.dma_start(const["outs_dram"][bass.ds((i * 2 + k) * BLK, BLK), :].rearrange("(t p) d -> p t d", p=P),
                             y[:, k % 2, :, :]).then_inc(stored[k % 2], 16)
                if after >= 2 and n2 == 1:
                    load_next_w2(i, k, e)

            e, then = expert(0, 0), expert(0, 1)
            if not routed[4]:
                for f in range(NF):
                    load_w13(sp, e, f)
                load_w2(sp, 0, e)
            if n2 == 2:
                load_w2(sp, 1, then)
            for f in range(NF):
                w13_done.wait(sp, 0, f)
                load_w13(sp, then, f)
            for k in range(2):
                sp.sem_inc(stored[k], 16)
            sp.wait_ge(scattered, TOP * NTILE * 16)
            load_rows(0, 0)
            load_rows(0, 1)
            t_ready.wait(sp, 0, 0)
            load_rows(0, 2)
            e = expert(0, 2)
            w13_done.wait(sp, 0, NF)
            load_w13(sp, e, 0)
            t_ready.wait(sp, 0, 1)
            load_rows(0, 3)
            w13_done.wait(sp, 0, NF + 1)
            load_w13(sp, e, 1)
            if n2 == 1:
                w2_done.wait(sp, 0, NF - 1)
                load_w2(sp, 1, then)
            loops = (nblk - 4) // 2
            with sp.Fori(0, loops) as i:
                ahead(i, 0, 4)
                ahead(i, 1, 4)
            for n in range(2 * loops, nblk):
                ahead(loops, n - 2 * loops, min(4, nblk - 1 - n))
            if out is not None:
                for b in range(B):
                    sp.wait_ge(added, (b + 1) * NT * TOP)
                    sp.dma_start(out[b].rearrange("(t p) d -> p t d", p=P), x[:, b * NT:(b + 1) * NT, :]
                                 ).then_inc(out_stored, 16)
                sp.wait_ge(out_stored, B * 16)

        @block.gpsimd
        def _(pool):
            if scatter_here:
                pool.wait_ge(const["rows_zeroed"], 16)
                for tile in range(NTILE):
                    for k in range(TOP):
                        pool.indirect_dma_start(const["rows_dram"], bass.IndirectOffsetOnAxis(
                            ap=place[k][:, tile:tile + 1], axis=0), xn[:, tile // NT, tile % NT, :], None
                            ).then_inc(scattered, 16)
            if routed:
                for k in range(2):
                    pool.wait_ge(stored[k], ((nblk + 1 - k) // 2 + 1) * 16)
                for tile in range(NTILE):
                    for k in range(TOP):
                        pool.indirect_dma_start(back[k][:, tile, :], None, const["outs_dram"],
                                                bass.IndirectOffsetOnAxis(ap=place[k][:, tile:tile + 1], axis=0)
                                                ).then_inc(gathered[tile // GATHER], 16)

        def loads(i, k):
            return 1 + (i * 2 + k + (1 if routed[4] else 0) if routed else 0)

        def w2_loads(i, k):
            if n2 == 1 or not routed:
                return loads(i, k)
            return 1 + i + k // 2 + (1 if routed[4] and k % 2 == 0 else 0)

        @block.scalar
        def _(act):
            for s in (rows_split, w13_split, w2_split, g_silu, h_split):
                s.begin(act)

            def rows_of(i, k, _):
                if routed:
                    t_ready.wait(act, i, k)
                g_ready.wait(act, i, (k - 1) * NF - 1)
                rows_done.wait(act, i, k - 2)
                src = t_ps[:, k % 2, :, :] if routed else xnT[:, :, bass.ds((i * 2 + k) * BLK, BLK)]
                act.activation(rows_hi[:, k % 2, :, :], src, ACT.Copy).then_inc(rows_split.sem, 1)

            def split_w13(i, k, f):
                act.wait_ge(w13_in[f], loads(i, k) * 32)
                g_ready.wait(act, i, (k - 2) * NF + f)
                for n, hi in enumerate((hi1, hi3)):
                    ins = act.activation(two_chunks(hi, k % 2, f), two_chunks(raw13, n, f), ACT.Copy)
                ins.then_inc(w13_split.sem, 1)

            def split_w2(i, k, f):
                act.wait_ge(w2_in[k % n2], w2_loads(i, k) * 16)
                y_ready.wait(act, i, k - n2)
                act.activation(hi2[:, k % n2, 2 * f:2 * f + 2, :], raw2[:, k % n2, 2 * f:2 * f + 2, :],
                               ACT.Copy).then_inc(w2_split.sem, 1)

            def prepare(i, k, _):
                for f in range(NF):
                    split_w13(0, 0, f)
                if NF > 2 or not routed:
                    for f in range(NF):
                        split_w2(0, 0, f)

            def gate(i, k, f):
                m = k * NF + f
                g_ready.wait(act, i, m)
                h_made.wait(act, i, m - 2)
                act.activation(silu[:, f % 2, :], g_ps[:, f % 2, 0, :], ACT.Silu).then_inc(g_silu.sem, 1)

            def split_h(i, k, f):
                m = k * NF + f
                h_made.wait(act, i, m)
                y_ready.wait(act, i, k - 2)
                act.activation(h_hi[:, k % 2, 2 * f:2 * f + 2, :].rearrange("p c n -> p (c n)"), h[:, f % 2, :],
                               ACT.Copy).then_inc(h_split.sem, 1)
            run_blocks(act, nblk, NF, {"C": prepare, "G": gate, "H": split_h, "T": rows_of}
                       | ({"W": split_w13, "V": split_w2} if routed else {"rows first": True}))

        @block.vector
        def _(dve):
            for s in (rows_done, w13_done, w2_done, h_made, h_done, y_read):
                s.begin(dve)

            def rows_of(i, k, _):
                rows_split.wait(dve, i, k)
                src = t_ps[:, k % 2, :, :] if routed else xnT[:, :, bass.ds((i * 2 + k) * BLK, BLK)]
                dve.tensor_tensor(rows_lo[:, k % 2, :, :], src, rows_hi[:, k % 2, :, :].bitcast(F32), ALU.subtract
                                  ).then_inc(rows_done.sem, 1)

            def rest_w13(i, k, f):
                w13_split.wait(dve, i, k * NF + f)
                for n, (hi, lo) in enumerate(((hi1, lo1), (hi3, lo3))):
                    ins = dve.tensor_tensor(two_chunks(lo, k % 2, f), two_chunks(raw13, n, f),
                                            two_chunks(hi, k % 2, f).bitcast(F32), ALU.subtract)
                ins.then_inc(w13_done.sem, 1)

            def rest_w2(i, k, f):
                w2_split.wait(dve, i, k * NF + f)
                dve.tensor_tensor(lo2[:, k % n2, 2 * f:2 * f + 2, :], raw2[:, k % n2, 2 * f:2 * f + 2, :],
                                  hi2[:, k % n2, 2 * f:2 * f + 2, :].bitcast(F32), ALU.subtract
                                  ).then_inc(w2_done.sem, 1)

            def prepare(i, k, _):
                for f in range(NF):
                    rest_w13(0, 0, f)
                if NF > 2 or not routed:
                    for f in range(NF):
                        rest_w2(0, 0, f)

            def hidden(i, k, f):
                m = k * NF + f
                g_silu.wait(dve, i, m)
                h_done.wait(dve, i, m - 2)
                dve.tensor_tensor(h[:, f % 2, :], g_ps[:, f % 2, 1, :], silu[:, f % 2, :], ALU.mult
                                  ).then_inc(h_made.sem, 1)

            def rest_h(i, k, f):
                m = k * NF + f
                h_split.wait(dve, i, m)
                y_ready.wait(dve, i, k - 2)
                at = (slice(None), k % 2, slice(2 * f, 2 * f + 2), slice(None))
                dve.tensor_tensor(h_lo[at].rearrange("p c n -> p (c n)"), h[:, f % 2, :],
                                  h_hi[at].bitcast(F32).rearrange("p c n -> p (c n)"), ALU.subtract
                                  ).then_inc(h_done.sem, 1)

            def output(i, k, t):
                if t < BLK // P - 1:
                    return
                y_ready.wait(dve, i, k)
                if routed:
                    dve.wait_ge(stored[k % 2], (i + k // 2 + 1) * 16)
                    ins = dve.tensor_copy(y[:, k % 2, :, :], y_ps[:, k % 2, :, :])
                else:
                    xs = x[:, bass.ds(i * 4 + 2 * k, 2), :]
                    ins = dve.tensor_tensor(xs, y_ps[:, k % 2, :, :], xs, ALU.add)
                ins.then_inc(y_read.sem, 1)
            run_blocks(dve, nblk, NF, {"C": prepare, "G": hidden, "H": rest_h, "T": rows_of, "Y": output}
                       | ({"W": rest_w13, "V": rest_w2} if routed else {"rows first": True}))
            if routed:
                for tile in range(NTILE):
                    for k in range(TOP):
                        if k == 0 and tile % GATHER == 0:
                            dve.wait_ge(gathered[tile // GATHER], GATHER * TOP * 16)
                        if k:
                            dve.wait_ge(added, tile * TOP + 1)
                        dve.scalar_tensor_tensor(x[:, tile, :], back[k][:, tile, :],
                                                 routed[0][k][:, tile:tile + 1], x[:, tile, :], ALU.mult, ALU.add
                                                 ).then_inc(added, 1)

        @block.tensor
        def _(pe):
            for s in (g_ready, y_ready) + ((t_ready,) if routed else ()):
                s.begin(pe)

            def transpose(i, k, _):
                pe.wait_ge(rows_in[k % 2], (i + k // 2 + 1) * 16)
                rows_done.wait(pe, i, k - 2)
                for c in range(CC):
                    for t in range(BLK // P):
                        ins = pe.transpose(t_ps[:, k % 2, c, t * P:(t + 1) * P],
                                           rows[:, k % 2, t, c * P:(c + 1) * P], const["ident"][:, :])
                ins.then_inc(t_ready.sem, 1)

            def three_passes(at, chunks):
                passes = [(s[a], m[b]) for s, m in chunks for a, b in ((0, 0), (1, 0), (0, 1))]
                for n, (s, m) in enumerate(passes):
                    ins = pe.matmul(at, s, m, start=n == 0, stop=n == len(passes) - 1)
                return ins

            def hidden(i, k, f):
                m = k * NF + f
                buf = k % 2 if routed else 0
                if f == 0:
                    rows_done.wait(pe, i, k)
                if routed:
                    w13_done.wait(pe, i, m)
                elif isinstance(i, int) and i == 0 and k == 0:
                    w13_done.wait(pe, 0, f)
                h_made.wait(pe, i, m - 2)
                for half, (hi, lo) in enumerate(((hi1, lo1), (hi3, lo3))):
                    for j in range(2):
                        cols = slice((2 * f + j) * P, (2 * f + j + 1) * P)
                        ins = three_passes(g_ps[:, f % 2, half, j * BLK:(j + 1) * BLK],
                                           [((hi[:, buf, c, cols], lo[:, buf, c, cols]),
                                             (rows_hi[:, k % 2, c, :], rows_lo[:, k % 2, c, :])) for c in range(CC)])
                ins.then_inc(g_ready.sem, 1)

            def output(i, k, t):
                buf2 = k % n2 if routed else 0
                if t == 0:
                    if routed:
                        w2_done.wait(pe, i, k * NF + NF - 1)
                    else:
                        w2_done.wait(pe, 0, NF - 1)
                    h_done.wait(pe, i, k * NF + NF - 1)
                    y_read.wait(pe, i, k - 2)
                rows_t = slice(t * P, (t + 1) * P)
                ins = three_passes(y_ps[:, k % 2, t, :],
                                   [((h_hi[:, k % 2, f, rows_t], h_lo[:, k % 2, f, rows_t]),
                                     (hi2[:, buf2, f, :], lo2[:, buf2, f, :])) for f in range(FC)])
                if t == BLK // P - 1:
                    ins.then_inc(y_ready.sem, 1)
            run_blocks(pe, nblk, NF, {"G": hidden, "Y": output} | ({"T": transpose} if routed else {}))


def build(nc, inputs, out):
    with ExitStack() as ctx:
        x = ctx.enter_context(nc.sbuf_tensor("x_sb", [P, B * NT, D], F32))
        const = load_constants(nc, ctx, x, inputs)

        def of(tag):
            return {n[len(tag) + 1:]: a for n, a in inputs.items() if n.startswith(tag + "_")}

        context = {"ctx": inputs["ctx"], "ctxT": inputs["ctxT"]}
        attention(nc, "l0a", x, const, of("l0a"), "causal")
        geglu(nc, "l0g", x, const, context)
        moe(nc, "l0m", x, const, of("l0m"), 512, phi=False, shared=True)
        attention(nc, "l1a", x, const, of("l1a"), "full")
        attention(nc, "l1x", x, const, of("l1x") | context, "cross")
        moe(nc, "l1m", x, const, of("l1m"), 1024, phi=True, shared=False, out=out)


def rope_factor():
    theta = np.float32(1) / np.float32(10000) ** (np.float32(2) * np.arange(HD // 2, dtype=np.float32) / np.float32(HD))
    ang = np.arange(1, T + 1, dtype=np.float32)[:, None] * theta.astype(np.float32)[None]
    ang = np.concatenate([ang, ang], axis=-1).astype(np.float32)
    return (np.cos(ang) + np.sin(ang)).astype(np.float32)


def layout(i):
    a = {"x": i["x"], "ctx": i["ctx_1024"], "ctxT": i["ctx_1024"].transpose(0, 2, 1)}
    at = np.arange(P)
    a["ident"] = np.eye(P, dtype=np.float32)
    a["sums_of"] = (at[:, None] == 32 * np.arange(GH)[None] + HD).astype(np.float32)
    a["rope"] = np.tile(rope_factor().T, (P // HD, 1))
    a["masks"] = np.stack([np.where(at[None] > at[:, None], NEG, 0), np.where(at[None] < at[:, None], NEG, 0)],
                          axis=1).astype(np.float32)
    a["iota"] = np.tile(np.arange(32, dtype=np.float32), (P, 1))
    a["before"] = (at[:, None] < at[None]).astype(np.float32)

    def heads_padded(wt):
        padded = np.zeros((GH, 32, NG, D), np.float32)
        padded[:, 0:HD] = wt.reshape(NG, GH, HD, D).transpose(1, 2, 0, 3)
        return padded.reshape(P, NG, D)

    def attn(tag, wt, bias, wout, bout):
        a[tag + "_wqkv"] = wt
        a[tag + "_bqk"] = bias[0:2 * D].reshape(2 * CC, P).T
        a[tag + "_bv"] = bias[None, 2 * D:]
        a[tag + "_wout"] = heads_padded(wout)
        if tag == "l1x":
            a[tag + "_bo"] = bout[None]
        else:
            a[tag + "_wout"][HD, 0, :] = bout

    attn("l0a", i["L0_attn_W_attn"].T, i["L0_attn_b_attn"], i["L0_attn_W_proj"].T, i["L0_attn_b_proj"])
    attn("l1a", i["L1_attn_W_qkv"].reshape(H, 3, HD, D).transpose(1, 0, 2, 3).reshape(3 * D, D).T,
         i["L1_attn_b_qkv"].reshape(H, 3, HD).transpose(1, 0, 2).reshape(3 * D),
         i["L1_attn_W_out"].T, i["L1_attn_b_out"])
    attn("l1x", np.concatenate([i["L1_xattn_Wq"], i["L1_xattn_Wkv"]], axis=1),
         np.concatenate([i["L1_xattn_bq"], i["L1_xattn_bkv"]]), i["L1_xattn_Wo"], i["L1_xattn_bo"])
    a["l0m_router"], a["l0m_router_bias"] = i["L0_ffn_router_w"].T, i["L0_ffn_experts_bias"][None]
    for n in ("w1", "w3", "w2"):
        a["l0m_" + n] = np.concatenate([i["L0_ffn_" + n], i["L0_ffn_s" + n]])
    a["l1m_router"], a["l1m_router_bias"] = i["L1_ffn_gate_w"].T, np.zeros((1, 8), np.float32)
    for n in ("w1", "w3", "w2"):
        a["l1m_" + n] = i["L1_ffn_" + n].transpose(0, 2, 1)
    return a


def kernel(**inputs):
    import concourse.bacc as bacc
    from concourse.bass_utils import run_bass_kernel_spmd

    arrays = {f"in_{n}": np.ascontiguousarray(a) for n, a in layout({n: np.asarray(a) for n, a in inputs.items()}).items()}
    nc = bacc.Bacc("TRN2", target_bir_lowering=False, num_devices=1)
    aps = {n[3:]: nc.dram_tensor(n, a.shape, mybir.dt.from_np(a.dtype), kind="ExternalInput").ap()
           for n, a in arrays.items()}
    out = nc.dram_tensor("out_x", (B, T, D), F32, kind="ExternalOutput").ap()
    build(nc, aps, out)
    r = run_bass_kernel_spmd(nc, [arrays], core_ids=[0])
    return r.results[0]["out_x"]
```
